# Optimizing a Trainium2 kernel written in Bass

```python
import numpy as np
import jax
import jax.numpy as jnp

def _softmax(x, axis=-1):
    return jax.nn.softmax(x, axis=axis)

def _gelu(x):
    return jax.nn.gelu(x, approximate=True)

def _silu(x):
    return jax.nn.silu(x)

def _sigmoid(x):
    return jax.nn.sigmoid(x)

def _layernorm(x, axis=-1, eps=1e-05):
    m = jnp.mean(x, axis=axis, keepdims=True)
    v = jnp.var(x, axis=axis, keepdims=True)
    return (x - m) / jnp.sqrt(v + eps)

def _scatter_add(tgt, idx, src, axis=0):
    return tgt.at[idx].add(src)

def _segment_sum(src, seg, n):
    return jax.ops.segment_sum(src, seg, n)
kernel_name = 'mk_gps_d1_gnn_r8_b3a167'

def setup_inputs(seed: int=0):
    np.random.seed(seed)
    _w = jnp.asarray

    def _rec_inputs():
        import jax
        import jax.numpy as jnp
        _gk = jax.random.key(seed)
        x = -0.0005207 + 1.001 * jax.random.normal(jax.random.fold_in(_gk, 1), (6250, 256), jnp.float32)
        src = jax.random.randint(jax.random.fold_in(_gk, 2), (100000,), 0, 6250, jnp.int32)
        dst = jnp.minimum((6250 * jax.random.uniform(jax.random.fold_in(_gk, 3), (100000,)) ** 2.0).astype(jnp.int32), 49999)
        _o = jnp.argsort(dst, stable=True)
        src = src[_o]
        dst = dst[_o]
        edge_weight = jax.random.uniform(jax.random.fold_in(_gk, 12), (100000,), jnp.float32, 0.0, 0.999998)
        node_vec = jax.random.uniform(jax.random.fold_in(_gk, 13), (6250,), jnp.float32, 0.0, 0.999833)
        return (x, src, dst, edge_weight, node_vec)
    x, src, dst, edge_weight, node_vec = _rec_inputs()

    def _L0_gnn_setup():
        import jax, jax.numpy as jnp
        import numpy as np
        from jax import lax
        N, E, D = (1024, 32768, 256)
        NH, FOUT = (4, 64)
        D_STATE, D_CONV, DT_RANK = (16, 4, 16)

        def _layer_norm(x, g, b, eps=1e-05):
            mu = jnp.mean(x, -1, keepdims=True)
            var = jnp.var(x, -1, keepdims=True)
            return (x - mu) * lax.rsqrt(var + eps) * g + b

        def _mamba(xs, in_proj_w, conv_w, conv_b, x_proj_w, dt_proj_w, dt_proj_b, A_log, D_param, out_proj_w):
            n = xs.shape[0]
            xz = xs @ in_proj_w.T
            xc, z = jnp.split(xz, 2, axis=-1)
            K = conv_w.shape[1]
            xp = jnp.pad(xc, ((K - 1, 0), (0, 0)))
            xc = sum((xp[k:k + n] * conv_w[:, k] for k in range(K))) + conv_b
            xc = jax.nn.silu(xc)
            dbc = xc @ x_proj_w.T
            dt = jax.nn.softplus(dbc[:, :DT_RANK] @ dt_proj_w.T + dt_proj_b)
            Bm = dbc[:, DT_RANK:DT_RANK + D_STATE]
            Cm = dbc[:, DT_RANK + D_STATE:]
            A = -jnp.exp(A_log)
            dA = jnp.exp(dt[:, :, None] * A)
            dBx = (dt * xc)[:, :, None] * Bm[:, None, :]

            def step(h, t):
                dA_t, dBx_t, C_t = t
                h = dA_t * h + dBx_t
                return (h, h @ C_t)
            _, y = lax.scan(step, jnp.zeros((xc.shape[1], D_STATE), xs.dtype), (dA, dBx, Cm))
            y = y + xc * D_param
            y = y * jax.nn.silu(z)
            return y @ out_proj_w.T

        def _forward(x, edge_index, deg_noise, gat_w, gat_a_src, gat_a_tgt, gat_b, ln_local_g, ln_local_b, ln_global_g, ln_global_b, ln2_g, ln2_b, in_proj_w, conv_w, conv_b, x_proj_w, dt_proj_w, dt_proj_b, A_log, D_param, out_proj_w, wl, wg, ff1_w, ff1_b, ff2_w, ff2_b):
            n = x.shape[0]
            src, tgt = (edge_index[0], edge_index[1])
            proj = (x @ gat_w.T).reshape(n, NH, FOUT)
            s_src = jnp.sum(proj * gat_a_src, -1)
            s_tgt = jnp.sum(proj * gat_a_tgt, -1)
            e = jax.nn.leaky_relu(s_src[src] + s_tgt[tgt], 0.2)
            exp_e = jnp.exp(e - jnp.max(e))
            denom = jax.ops.segment_sum(exp_e, tgt, num_segments=n)
            attn = exp_e / (denom[tgt] + 1e-16)
            agg = jax.ops.segment_sum(proj[src] * attn[:, :, None], tgt, num_segments=n)
            h_local = jax.nn.elu((agg + x.reshape(n, NH, FOUT)).reshape(n, NH * FOUT) + gat_b)
            h_local = _layer_norm(h_local, ln_local_g, ln_local_b)
            deg = jax.ops.segment_sum(jnp.ones((src.shape[0],), x.dtype), src, num_segments=n)
            perm = jnp.argsort(deg + deg_noise, stable=True)
            inv = jnp.argsort(perm)
            y = _mamba(x[perm], in_proj_w, conv_w, conv_b, x_proj_w, dt_proj_w, dt_proj_b, A_log, D_param, out_proj_w)
            h_attn = _layer_norm(x + y[inv], ln_global_g, ln_global_b)
            gate = jax.nn.sigmoid(h_local @ wl.T + h_attn @ wg.T)
            h = gate * h_local + (1.0 - gate) * h_attn
            ff = jax.nn.relu(h @ ff1_w.T + ff1_b) @ ff2_w.T + ff2_b
            return _layer_norm(h + ff, ln2_g, ln2_b)
        key = jax.random.key(seed)
        ks = jax.random.split(key, 24)
        w = lambda i, shape, s=0.05: jax.random.normal(ks[i], shape, dtype=jnp.float32) * s
        return {'x': jax.random.normal(ks[0], (N, D), dtype=jnp.float32), 'edge_index': jax.random.randint(ks[1], (2, E), 0, N, dtype=jnp.int32), 'edge_prob': jax.random.uniform(ks[2], (E,), dtype=jnp.float32), 'deg_noise': jax.random.uniform(ks[3], (N,), dtype=jnp.float32), 'gat_w': w(4, (NH * FOUT, D)), 'gat_a_src': w(5, (NH, FOUT)), 'gat_a_tgt': w(6, (NH, FOUT)), 'gat_b': jnp.zeros((NH * FOUT,), jnp.float32), 'ln_local_g': jnp.ones((D,), jnp.float32), 'ln_local_b': jnp.zeros((D,), jnp.float32), 'ln_global_g': jnp.ones((D,), jnp.float32), 'ln_global_b': jnp.zeros((D,), jnp.float32), 'ln2_g': jnp.ones((D,), jnp.float32), 'ln2_b': jnp.zeros((D,), jnp.float32), 'in_proj_w': w(7, (2 * D, D)), 'conv_w': w(8, (D, D_CONV), 0.2), 'conv_b': jnp.zeros((D,), jnp.float32), 'x_proj_w': w(9, (DT_RANK + 2 * D_STATE, D)), 'dt_proj_w': w(10, (D, DT_RANK)), 'dt_proj_b': w(11, (D,), 0.1) - 4.0, 'A_log': jnp.log(jnp.tile(jnp.arange(1, D_STATE + 1, dtype=jnp.float32), (D, 1))), 'D_param': jnp.ones((D,), jnp.float32), 'out_proj_w': w(12, (D, D)), 'wl': w(13, (D, D)), 'wg': w(14, (D, D)), 'ff1_w': w(15, (2 * D, D)), 'ff1_b': jnp.zeros((2 * D,), jnp.float32), 'ff2_w': w(16, (D, 2 * D)), 'ff2_b': jnp.zeros((D,), jnp.float32)}
    _L0_gnn_all = _L0_gnn_setup()
    _L0_gnn_in = {k: v for k, v in _L0_gnn_all.items() if k in ('gat_w', 'gat_a_src', 'gat_a_tgt', 'gat_b', 'ln_local_g', 'ln_local_b', 'ln_global_g', 'ln_global_b', 'ln2_g', 'ln2_b', 'in_proj_w', 'conv_w', 'conv_b', 'x_proj_w', 'dt_proj_w', 'dt_proj_b', 'A_log', 'D_param', 'out_proj_w', 'wl', 'wg', 'ff1_w', 'ff1_b', 'ff2_w', 'ff2_b')}
    del _L0_gnn_all

    def _L0_mix_setup():
        import jax, jax.numpy as jnp
        import numpy as np
        NHEAD = 8
        ATT_EPS = 1e-06
        LN_EPS = 1e-05

        def _layernorm(x, g, b):
            mu = jnp.mean(x, axis=-1, keepdims=True)
            var = jnp.mean(jnp.square(x - mu), axis=-1, keepdims=True)
            return (x - mu) * jax.lax.rsqrt(var + LN_EPS) * g + b
        key = jax.random.key(seed)
        ks = jax.random.split(key, 7)
        N, L, C = (4, 2048, 256)
        s = 1.0 / np.sqrt(C)
        return {'x': jax.random.normal(ks[0], (N, L, C), jnp.float32), 'Wq': jax.random.normal(ks[1], (C, C), jnp.float32) * s, 'Wk': jax.random.normal(ks[2], (C, C), jnp.float32) * s, 'Wv': jax.random.normal(ks[3], (C, C), jnp.float32) * s, 'Wm': jax.random.normal(ks[4], (C, C), jnp.float32) * s, 'W1': jax.random.normal(ks[5], (2 * C, 2 * C), jnp.float32) * (1.0 / np.sqrt(2 * C)), 'W2': jax.random.normal(ks[6], (2 * C, C), jnp.float32) * (1.0 / np.sqrt(2 * C)), 'g1': jnp.ones((C,), jnp.float32), 'b1': jnp.zeros((C,), jnp.float32), 'g2': jnp.ones((C,), jnp.float32), 'b2': jnp.zeros((C,), jnp.float32)}
    _L0_mix_all = _L0_mix_setup()
    _L0_mix_in = {k: v for k, v in _L0_mix_all.items() if k in ('Wq', 'Wk', 'Wv', 'Wm', 'W1', 'W2', 'g1', 'b1', 'g2', 'b2')}
    del _L0_mix_all

    def _L0_ffn_setup():
        import jax, jax.numpy as jnp
        import numpy as np
        TOP_K = 2
        LN_EPS = 1e-05
        key = jax.random.key(seed)
        ks = jax.random.split(key, 8)
        B, S, D, E, H = (16, 1024, 256, 8, 1024)
        x = jax.random.normal(ks[0], (B, S, D), dtype=jnp.float32)
        Wr = jax.random.normal(ks[1], (D, E), dtype=jnp.float32) * 0.1
        br = jnp.zeros((E,), dtype=jnp.float32)
        ln_g = jnp.ones((E, D), dtype=jnp.float32)
        ln_b = jnp.zeros((E, D), dtype=jnp.float32)
        W1 = jax.random.normal(ks[2], (E, D, H), dtype=jnp.float32) * (1.0 / np.sqrt(D))
        b1 = jnp.zeros((E, H), dtype=jnp.float32)
        W2 = jax.random.normal(ks[3], (E, H, D), dtype=jnp.float32) * (1.0 / np.sqrt(H))
        b2 = jnp.zeros((E, D), dtype=jnp.float32)
        return {'x': x, 'Wr': Wr, 'br': br, 'ln_g': ln_g, 'ln_b': ln_b, 'W1': W1, 'b1': b1, 'W2': W2, 'b2': b2}
    _L0_ffn_all = _L0_ffn_setup()
    _L0_ffn_in = {k: v for k, v in _L0_ffn_all.items() if k in ('Wr', 'br', 'ln_g', 'ln_b', 'W1', 'b1', 'W2', 'b2')}
    del _L0_ffn_all
    return {'x': x, 'src': src, 'dst': dst, 'edge_weight': edge_weight, 'node_vec': node_vec, 'L0_gnn_gat_w': _L0_gnn_in['gat_w'], 'L0_gnn_gat_a_src': _L0_gnn_in['gat_a_src'], 'L0_gnn_gat_a_tgt': _L0_gnn_in['gat_a_tgt'], 'L0_gnn_gat_b': _L0_gnn_in['gat_b'], 'L0_gnn_ln_local_g': _L0_gnn_in['ln_local_g'], 'L0_gnn_ln_local_b': _L0_gnn_in['ln_local_b'], 'L0_gnn_ln_global_g': _L0_gnn_in['ln_global_g'], 'L0_gnn_ln_global_b': _L0_gnn_in['ln_global_b'], 'L0_gnn_ln2_g': _L0_gnn_in['ln2_g'], 'L0_gnn_ln2_b': _L0_gnn_in['ln2_b'], 'L0_gnn_in_proj_w': _L0_gnn_in['in_proj_w'], 'L0_gnn_conv_w': _L0_gnn_in['conv_w'], 'L0_gnn_conv_b': _L0_gnn_in['conv_b'], 'L0_gnn_x_proj_w': _L0_gnn_in['x_proj_w'], 'L0_gnn_dt_proj_w': _L0_gnn_in['dt_proj_w'], 'L0_gnn_dt_proj_b': _L0_gnn_in['dt_proj_b'], 'L0_gnn_A_log': _L0_gnn_in['A_log'], 'L0_gnn_D_param': _L0_gnn_in['D_param'], 'L0_gnn_out_proj_w': _L0_gnn_in['out_proj_w'], 'L0_gnn_wl': _L0_gnn_in['wl'], 'L0_gnn_wg': _L0_gnn_in['wg'], 'L0_gnn_ff1_w': _L0_gnn_in['ff1_w'], 'L0_gnn_ff1_b': _L0_gnn_in['ff1_b'], 'L0_gnn_ff2_w': _L0_gnn_in['ff2_w'], 'L0_gnn_ff2_b': _L0_gnn_in['ff2_b'], 'L0_mix_Wq': _L0_mix_in['Wq'], 'L0_mix_Wk': _L0_mix_in['Wk'], 'L0_mix_Wv': _L0_mix_in['Wv'], 'L0_mix_Wm': _L0_mix_in['Wm'], 'L0_mix_W1': _L0_mix_in['W1'], 'L0_mix_W2': _L0_mix_in['W2'], 'L0_mix_g1': _L0_mix_in['g1'], 'L0_mix_b1': _L0_mix_in['b1'], 'L0_mix_g2': _L0_mix_in['g2'], 'L0_mix_b2': _L0_mix_in['b2'], 'L0_ffn_Wr': _L0_ffn_in['Wr'], 'L0_ffn_br': _L0_ffn_in['br'], 'L0_ffn_ln_g': _L0_ffn_in['ln_g'], 'L0_ffn_ln_b': _L0_ffn_in['ln_b'], 'L0_ffn_W1': _L0_ffn_in['W1'], 'L0_ffn_b1': _L0_ffn_in['b1'], 'L0_ffn_W2': _L0_ffn_in['W2'], 'L0_ffn_b2': _L0_ffn_in['b2']}

def reference(x, src, dst, edge_weight, node_vec, L0_gnn_gat_w, L0_gnn_gat_a_src, L0_gnn_gat_a_tgt, L0_gnn_gat_b, L0_gnn_ln_local_g, L0_gnn_ln_local_b, L0_gnn_ln_global_g, L0_gnn_ln_global_b, L0_gnn_ln2_g, L0_gnn_ln2_b, L0_gnn_in_proj_w, L0_gnn_conv_w, L0_gnn_conv_b, L0_gnn_x_proj_w, L0_gnn_dt_proj_w, L0_gnn_dt_proj_b, L0_gnn_A_log, L0_gnn_D_param, L0_gnn_out_proj_w, L0_gnn_wl, L0_gnn_wg, L0_gnn_ff1_w, L0_gnn_ff1_b, L0_gnn_ff2_w, L0_gnn_ff2_b, L0_mix_Wq, L0_mix_Wk, L0_mix_Wv, L0_mix_Wm, L0_mix_W1, L0_mix_W2, L0_mix_g1, L0_mix_b1, L0_mix_g2, L0_mix_b2, L0_ffn_Wr, L0_ffn_br, L0_ffn_ln_g, L0_ffn_ln_b, L0_ffn_W1, L0_ffn_b1, L0_ffn_W2, L0_ffn_b2):
    import jax
    import jax.numpy as jnp

    def _L0_gnn_ref(x, edge_index, edge_prob, deg_noise, gat_w, gat_a_src, gat_a_tgt, gat_b, ln_local_g, ln_local_b, ln_global_g, ln_global_b, ln2_g, ln2_b, in_proj_w, conv_w, conv_b, x_proj_w, dt_proj_w, dt_proj_b, A_log, D_param, out_proj_w, wl, wg, ff1_w, ff1_b, ff2_w, ff2_b):
        import jax, jax.numpy as jnp
        import numpy as np
        from jax import lax
        N, E, D = (1024, 32768, 256)
        NH, FOUT = (4, 64)
        D_STATE, D_CONV, DT_RANK = (16, 4, 16)

        def _layer_norm(x, g, b, eps=1e-05):
            mu = jnp.mean(x, -1, keepdims=True)
            var = jnp.var(x, -1, keepdims=True)
            return (x - mu) * lax.rsqrt(var + eps) * g + b

        def _mamba(xs, in_proj_w, conv_w, conv_b, x_proj_w, dt_proj_w, dt_proj_b, A_log, D_param, out_proj_w):
            n = xs.shape[0]
            xz = xs @ in_proj_w.T
            xc, z = jnp.split(xz, 2, axis=-1)
            K = conv_w.shape[1]
            xp = jnp.pad(xc, ((K - 1, 0), (0, 0)))
            xc = sum((xp[k:k + n] * conv_w[:, k] for k in range(K))) + conv_b
            xc = jax.nn.silu(xc)
            dbc = xc @ x_proj_w.T
            dt = jax.nn.softplus(dbc[:, :DT_RANK] @ dt_proj_w.T + dt_proj_b)
            Bm = dbc[:, DT_RANK:DT_RANK + D_STATE]
            Cm = dbc[:, DT_RANK + D_STATE:]
            A = -jnp.exp(A_log)
            dA = jnp.exp(dt[:, :, None] * A)
            dBx = (dt * xc)[:, :, None] * Bm[:, None, :]

            def step(h, t):
                dA_t, dBx_t, C_t = t
                h = dA_t * h + dBx_t
                return (h, h @ C_t)
            _, y = lax.scan(step, jnp.zeros((xc.shape[1], D_STATE), xs.dtype), (dA, dBx, Cm))
            y = y + xc * D_param
            y = y * jax.nn.silu(z)
            return y @ out_proj_w.T

        def _forward(x, edge_index, deg_noise, gat_w, gat_a_src, gat_a_tgt, gat_b, ln_local_g, ln_local_b, ln_global_g, ln_global_b, ln2_g, ln2_b, in_proj_w, conv_w, conv_b, x_proj_w, dt_proj_w, dt_proj_b, A_log, D_param, out_proj_w, wl, wg, ff1_w, ff1_b, ff2_w, ff2_b):
            n = x.shape[0]
            src, tgt = (edge_index[0], edge_index[1])
            proj = (x @ gat_w.T).reshape(n, NH, FOUT)
            s_src = jnp.sum(proj * gat_a_src, -1)
            s_tgt = jnp.sum(proj * gat_a_tgt, -1)
            e = jax.nn.leaky_relu(s_src[src] + s_tgt[tgt], 0.2)
            exp_e = jnp.exp(e - jnp.max(e))
            denom = jax.ops.segment_sum(exp_e, tgt, num_segments=n)
            attn = exp_e / (denom[tgt] + 1e-16)
            agg = jax.ops.segment_sum(proj[src] * attn[:, :, None], tgt, num_segments=n)
            h_local = jax.nn.elu((agg + x.reshape(n, NH, FOUT)).reshape(n, NH * FOUT) + gat_b)
            h_local = _layer_norm(h_local, ln_local_g, ln_local_b)
            deg = jax.ops.segment_sum(jnp.ones((src.shape[0],), x.dtype), src, num_segments=n)
            perm = jnp.argsort(deg + deg_noise, stable=True)
            inv = jnp.argsort(perm)
            y = _mamba(x[perm], in_proj_w, conv_w, conv_b, x_proj_w, dt_proj_w, dt_proj_b, A_log, D_param, out_proj_w)
            h_attn = _layer_norm(x + y[inv], ln_global_g, ln_global_b)
            gate = jax.nn.sigmoid(h_local @ wl.T + h_attn @ wg.T)
            h = gate * h_local + (1.0 - gate) * h_attn
            ff = jax.nn.relu(h @ ff1_w.T + ff1_b) @ ff2_w.T + ff2_b
            return _layer_norm(h + ff, ln2_g, ln2_b)
        return _forward(x, edge_index, deg_noise, gat_w, gat_a_src, gat_a_tgt, gat_b, ln_local_g, ln_local_b, ln_global_g, ln_global_b, ln2_g, ln2_b, in_proj_w, conv_w, conv_b, x_proj_w, dt_proj_w, dt_proj_b, A_log, D_param, out_proj_w, wl, wg, ff1_w, ff1_b, ff2_w, ff2_b)

    def _L0_mix_ref(x, Wq, Wk, Wv, Wm, W1, W2, g1, b1, g2, b2):
        import jax, jax.numpy as jnp
        import numpy as np
        NHEAD = 8
        ATT_EPS = 1e-06
        LN_EPS = 1e-05

        def _layernorm(x, g, b):
            mu = jnp.mean(x, axis=-1, keepdims=True)
            var = jnp.mean(jnp.square(x - mu), axis=-1, keepdims=True)
            return (x - mu) * jax.lax.rsqrt(var + LN_EPS) * g + b
        N, L, C = x.shape
        H = NHEAD
        D = C // H
        q = (x @ Wq).reshape(N, L, H, D)
        k = (x @ Wk).reshape(N, L, H, D)
        v = (x @ Wv).reshape(N, L, H, D)
        Q = jax.nn.elu(q) + 1.0
        K = jax.nn.elu(k) + 1.0
        v = v / L
        KV = jnp.einsum('nshd,nshv->nhdv', K, v)
        Z = 1.0 / (jnp.einsum('nlhd,nhd->nlh', Q, K.sum(axis=1)) + ATT_EPS)
        msg = jnp.einsum('nlhd,nhdv,nlh->nlhv', Q, KV, Z) * L
        msg = msg.reshape(N, L, C) @ Wm
        msg = _layernorm(msg, g1, b1)
        h = jnp.concatenate([x, msg], axis=-1) @ W1
        h = jax.nn.relu(h) @ W2
        msg = _layernorm(h, g2, b2)
        return x + msg

    def _L0_ffn_ref(x, Wr, br, ln_g, ln_b, W1, b1, W2, b2):
        import jax, jax.numpy as jnp
        import numpy as np
        TOP_K = 2
        LN_EPS = 1e-05
        B, S, D = x.shape
        N = B * S
        xt = x.reshape(N, D)
        logits = xt @ Wr + br
        probs = jax.nn.softmax(logits, axis=-1)
        top_p, top_idx = jax.lax.top_k(probs, TOP_K)
        weights = top_p / top_p.sum(axis=-1, keepdims=True)
        mu = xt.mean(axis=-1, keepdims=True)
        var = ((xt - mu) ** 2).mean(axis=-1, keepdims=True)
        xn = (xt - mu) * jax.lax.rsqrt(var + LN_EPS)
        xe = xn[None, :, :] * ln_g[:, None, :] + ln_b[:, None, :]
        h = jax.nn.gelu(jnp.einsum('end,edh->enh', xe, W1) + b1[:, None, :], approximate=False)
        y = jnp.einsum('enh,ehd->end', h, W2) + b2[:, None, :]
        y_tok = jnp.transpose(y, (1, 0, 2))
        sel = jnp.take_along_axis(y_tok, top_idx[:, :, None], axis=1)
        out = (weights[:, :, None] * sel).sum(axis=1)
        return out.reshape(B, S, D)
    edge_index = jnp.stack([src, dst])
    xn = _layernorm(x, axis=-1)
    x = x + _L0_gnn_ref(xn, edge_index, edge_weight, node_vec, L0_gnn_gat_w, L0_gnn_gat_a_src, L0_gnn_gat_a_tgt, L0_gnn_gat_b, L0_gnn_ln_local_g, L0_gnn_ln_local_b, L0_gnn_ln_global_g, L0_gnn_ln_global_b, L0_gnn_ln2_g, L0_gnn_ln2_b, L0_gnn_in_proj_w, L0_gnn_conv_w, L0_gnn_conv_b, L0_gnn_x_proj_w, L0_gnn_dt_proj_w, L0_gnn_dt_proj_b, L0_gnn_A_log, L0_gnn_D_param, L0_gnn_out_proj_w, L0_gnn_wl, L0_gnn_wg, L0_gnn_ff1_w, L0_gnn_ff1_b, L0_gnn_ff2_w, L0_gnn_ff2_b) + _L0_mix_ref(xn[None], L0_mix_Wq, L0_mix_Wk, L0_mix_Wv, L0_mix_Wm, L0_mix_W1, L0_mix_W2, L0_mix_g1, L0_mix_b1, L0_mix_g2, L0_mix_b2)[0]
    x = x + _L0_ffn_ref(_layernorm(x, axis=-1)[None], L0_ffn_Wr, L0_ffn_br, L0_ffn_ln_g, L0_ffn_ln_b, L0_ffn_W1, L0_ffn_b1, L0_ffn_W2, L0_ffn_b2)[0]
    return x

_drawn_inputs = setup_inputs


def setup_inputs(seed=0):
    import zlib

    import numpy as np

    out = dict(_drawn_inputs(seed))
    spreads = {'L0_gnn_gat_b': (0.0, 0.303),
     'L0_gnn_ln_local_g': (1.0, 0.2),
     'L0_gnn_ln_local_b': (0.0, 0.308),
     'L0_gnn_ln_global_g': (1.0, 0.2),
     'L0_gnn_ln_global_b': (0.0, 0.327),
     'L0_gnn_ln2_g': (1.0, 0.2),
     'L0_gnn_ln2_b': (0.0, 0.1),
     'L0_gnn_conv_b': (0.0, 0.8),
     'L0_gnn_D_param': (1.0, 0.6),
     'L0_gnn_ff1_b': (0.0, 0.298),
     'L0_gnn_ff2_b': (0.0, 0.1),
     'L0_mix_g1': (1.0, 0.2),
     'L0_mix_b1': (0.0, 0.277),
     'L0_mix_g2': (1.0, 0.2),
     'L0_mix_b2': (0.0, 0.1),
     'L0_ffn_br': (0.0, 0.1),
     'L0_ffn_ln_g': (1.0, 0.2),
     'L0_ffn_ln_b': (0.0, 0.467),
     'L0_ffn_b1': (0.0, 0.456),
     'L0_ffn_b2': (0.0, 0.318)}
    factors = {'node_vec': 3.701,
     'L0_gnn_gat_a_src': 3.327,
     'L0_gnn_gat_a_tgt': 6.397,
     'L0_gnn_in_proj_w': 3.297,
     'L0_gnn_conv_w': 3.661,
     'L0_gnn_x_proj_w': 8.0,
     'L0_gnn_dt_proj_w': 8.0,
     'L0_gnn_dt_proj_b': 8.0,
     'L0_gnn_A_log': 8.0,
     'L0_gnn_out_proj_w': 3.39}
    for name, (base, spread) in spreads.items():
        noise = np.random.default_rng([zlib.crc32(name.encode()), seed]).standard_normal(out[name].shape)
        drawn = base * np.exp(spread * noise) if base else spread * noise
        out[name] = jnp.asarray(drawn.astype(out[name].dtype))
    for name, factor in factors.items():
        out[name] = (out[name] * factor).astype(out[name].dtype)
    return out
```

```python
from contextlib import ExitStack

import concourse.bass as bass
from concourse import mybir

F32 = mybir.dt.float32
BF16 = mybir.dt.bfloat16
I32 = mybir.dt.int32
U32 = mybir.dt.uint32
ALU = mybir.AluOpType
ACT = mybir.ActivationFunctionType
AX = mybir.AxisListType

P = 128
N = 6250
D = 256
H2 = D // P
NT = -(-N // P)
NP = NT * P
TT = 112
TILES = 4
CH = TT * TILES
NCH = NP // CH
NTT = NP // TT
E = 100000
EP, EC = 125, 800
HEADS = 4
FO = D // HEADS
ROW = D + 2 * HEADS
KROW = P + 1
RANKED = 16
LN_EPS = 1e-5
STOP_AFTER = 99
SKIP = ()


def sb(nc, ctx, name, shape, dt=F32):
    return ctx.enter_context(nc.sbuf_tensor(name, shape, dt))


def ps(nc, ctx, name, shape, dt=F32):
    return ctx.enter_context(nc.psum_tensor(name, shape, dt))


def sems(nc, ctx, stage, names):
    return [nc.alloc_semaphore(name=f"{stage}_{n}") for n in names.split()]


def settle(nc, pool, token, settled, times):
    pool.wait_ge(settled, times)
    nc.gpsimd.tensor_tensor(token[:, 1:2], token[:, 0:1], token[:, 0:1], ALU.add).then_inc(settled, 1)


def halves(ap):
    return ap.rearrange("(h p) n -> p h n", p=P)


def over_halves(ap):
    return ap.unsqueeze(1).to_broadcast([P, H2, ap.shape[1]])


def stage_project(nc, a, t):
    with ExitStack() as ctx:
        inv_d = sb(nc, ctx, "p_inv_d", [P, P])
        ident = sb(nc, ctx, "p_ident", [P, P])
        w_gat = sb(nc, ctx, "p_w_gat", [P, H2, ROW])
        w_gat_o = sb(nc, ctx, "p_w_gat_o", [P, H2, D])
        a_blk = sb(nc, ctx, "p_a_blk", [P, H2, 2 * HEADS])
        w_kv = sb(nc, ctx, "p_w_kv", [P, H2, 2 * D])
        valid = sb(nc, ctx, "p_valid", [TT, NTT])
        x_c = sb(nc, ctx, "p_x", [P, H2, CH])
        cent = sb(nc, ctx, "p_cent", [P, H2, CH])
        sq = sb(nc, ctx, "p_sq", [P, H2, CH])
        std = sb(nc, ctx, "p_std", [P, CH])
        rstd = sb(nc, ctx, "p_rstd", [P, CH])
        xn = sb(nc, ctx, "p_xn", [P, H2, CH])
        rows = sb(nc, ctx, "p_rows", [TT, TILES, D])
        tab = sb(nc, ctx, "p_tab", [TT, TILES, ROW])
        kneg = sb(nc, ctx, "p_kneg", [TT, TILES, D])
        kexp = sb(nc, ctx, "p_kexp", [TT, TILES, D])
        k_t = sb(nc, ctx, "p_k", [TT, TILES, D])
        v_t = sb(nc, ctx, "p_v", [TT, TILES, D])
        kv_acc = sb(nc, ctx, "p_kv_acc", [P, H2, KROW])
        eps = sb(nc, ctx, "p_eps", [P, 1])

        mean_ps = ps(nc, ctx, "p_mean_ps", [P, 512])
        var_ps = ps(nc, ctx, "p_var_ps", [P, 512])
        tab_ps = ps(nc, ctx, "p_tab_ps", [P, 2, 512])
        k_ps = ps(nc, ctx, "p_k_ps", [P, 512])
        v_ps = ps(nc, ctx, "p_v_ps", [P, 512])
        rows_ps = ps(nc, ctx, "p_rows_ps", [P, 512])
        kv_ps = ps(nc, ctx, "p_kv_ps", [P, 512])

        (consts, w_in, w_scores, w_scored, x_in, mean_ok, centred, squared, var_ok, std_ok, rstd_ok, xn_ok,
         xn_out, rows_mm, rows_ok, rows_out, tab_out, kexp_ok, k_ok, kneg_ok, kv_mm, kv_ok, kv_out) = sems(
            nc, ctx, "p", "consts w_in w_scores w_scored x_in mean_ok centred squared var_ok std_ok rstd_ok xn_ok "
            "xn_out rows_mm rows_ok rows_out tab_out kexp_ok k_ok kneg_ok kv_mm kv_ok kv_out")
        tab_mm = sems(nc, ctx, "p", "tab_mm0 tab_mm1")
        tab_ok = sems(nc, ctx, "p", "tab_ok0 tab_ok1")
        k_mm, v_mm, v_ok = sems(nc, ctx, "p", "k_mm v_mm v_ok")
        block = ctx.enter_context(nc.Block())

        @block.gpsimd
        def _(pool):
            nc.gpsimd.memset(inv_d[:], 1.0 / D).then_inc(consts, 1)
            nc.gpsimd.memset(eps[:], LN_EPS).then_inc(consts, 1)
            nc.gpsimd.memset(kv_acc[:], 0.0).then_inc(consts, 1)

        @block.sync
        def _(sp):
            sp.dma_start(w_gat_o[:], halves(a["gat_w"])).then_inc(w_in, 16)
            sp.dma_start(w_gat[:, :, 0:D], halves(a["gat_wT"])).then_inc(w_in, 16)
            sp.dma_start(a_blk[:], halves(a["a_blk"])).then_inc(w_in, 16)
            sp.dma_start(w_kv[:, :, 0:D], halves(a["Wk"])).then_inc(w_in, 16)
            sp.dma_start(w_kv[:, :, D:], halves(a["Wv"])).then_inc(w_in, 16)
            sp.dma_start(valid[:], a["valid"]).then_inc(w_in, 16)
            sp.dma_start(ident[:], a["ident"]).then_inc(w_in, 16)
            with sp.Fori(0, NCH) as i:
                sp.wait_ge(centred, i)
                sp.dma_start(x_c[:], halves(a["xT"])[:, :, bass.ds(i * CH, CH)]).then_inc(x_in, 16)
                sp.wait_ge(xn_ok, i + 1)
                sp.dma_start(halves(t["xnT"])[:, :, bass.ds(i * CH, CH)], xn[:]).then_inc(xn_out, 16)
                sp.wait_ge(rows_ok, 4 * i + 4)
                sp.dma_start(t["xn"][bass.ds(i * CH, CH), :].rearrange("(j p) f -> p j f", p=TT), rows[:]).then_inc(rows_out, 16)
                for s in range(2):
                    sp.wait_ge(tab_ok[s], 2 * i + 2)
                sp.dma_start(t["table"][bass.ds(i * CH, CH), :].rearrange("(j p) f -> p j f", p=TT), tab[:]).then_inc(tab_out, 16)
            sp.wait_ge(kv_ok, NCH)
            sp.dma_start(t["kv"], kv_acc[:]).then_inc(kv_out, 16)
            sp.wait_ge(xn_out, 16 * NCH)
            sp.wait_ge(rows_out, 16 * NCH)
            sp.wait_ge(tab_out, 16 * NCH)
            sp.wait_ge(kv_out, 16)

        @block.tensor
        def _(pe):
            pe.wait_ge(consts, 3)
            pe.wait_ge(w_in, 16 * 7)
            for m in range(H2):
                for k in range(H2):
                    last = nc.tensor.matmul(tab_ps[:, 0, 8 * m:8 * m + 8], w_gat_o[:, k, m * P:(m + 1) * P], a_blk[:, k, :],
                                            start=(k == 0), stop=(k == H2 - 1))
            last.then_inc(w_scores, 1)
            pe.wait_ge(w_scored, 1)
            with pe.Fori(0, NCH) as i:
                pe.wait_ge(x_in, 16 * i + 16)
                pe.wait_ge(centred, i)
                for k in range(H2):
                    last = nc.tensor.matmul(mean_ps[:, 0:CH], inv_d[:], x_c[:, k, :], start=(k == 0), stop=(k == 1))
                last.then_inc(mean_ok, 1)
                pe.wait_ge(squared, i + 1)
                pe.wait_ge(std_ok, i)
                for k in range(H2):
                    last = nc.tensor.matmul(var_ps[:, 0:CH], inv_d[:], sq[:, k, :], start=(k == 0), stop=(k == 1))
                last.then_inc(var_ok, 1)
                pe.wait_ge(xn_ok, i + 1)
                for j in range(TILES):
                    s, u = j % 2, j // 2
                    tok = slice(j * TT, (j + 1) * TT)
                    pe.wait_ge(tab_ok[s], 2 * i + u)
                    for k in range(H2):
                        last = nc.tensor.matmul(tab_ps[0:TT, s, 0:ROW], xn[:, k, tok], w_gat[:, k, :],
                                                start=(k == 0), stop=(k == 1))
                    last.then_inc(tab_mm[s], 1)
                    for bank, w, done, read in ((k_ps, 0, k_mm, k_ok), (v_ps, D, v_mm, v_ok)):
                        pe.wait_ge(read, 4 * i + j)
                        for k in range(H2):
                            last = nc.tensor.matmul(bank[0:TT, 0:D], xn[:, k, tok], w_kv[:, k, w:w + D],
                                                    start=(k == 0), stop=(k == 1))
                        last.then_inc(done, 1)
                    pe.wait_ge(rows_ok, 4 * i + j)
                    for k in range(H2):
                        last = nc.tensor.transpose(rows_ps[0:TT, k * P:(k + 1) * P], xn[:, k, tok], ident[:])
                    last.then_inc(rows_mm, 1)
                pe.wait_ge(k_ok, 4 * i + 4)
                pe.wait_ge(v_ok, 4 * i + 4)
                pe.wait_ge(kv_ok, i)
                for b in range(H2):
                    for j in range(TILES):
                        nc.tensor.matmul(kv_ps[:, b * KROW:b * KROW + P], k_t[:, j, b * P:(b + 1) * P],
                                         v_t[:, j, b * P:(b + 1) * P], start=(j == 0), stop=(j == TILES - 1))
                    for j in range(TILES):
                        last = nc.tensor.matmul(kv_ps[:, b * KROW + P:(b + 1) * KROW], k_t[:, j, b * P:(b + 1) * P],
                                                valid[:, bass.ds(i * TILES + j, 1)], start=(j == 0), stop=(j == TILES - 1))
                last.then_inc(kv_mm, 1)

        @block.scalar
        def _(act):
            with act.Fori(0, NCH) as i:
                act.wait_ge(centred, i + 1)
                act.wait_ge(var_ok, i)
                nc.scalar.activation(sq[:], cent[:], ACT.Square).then_inc(squared, 1)
                act.wait_ge(var_ok, i + 1)
                act.wait_ge(rstd_ok, i)
                nc.scalar.activation(std[:], var_ps[:, 0:CH], ACT.Sqrt, bias=eps[:]).then_inc(std_ok, 1)
                act.wait_ge(kv_mm, i)
                act.wait_ge(tab_out, 16 * i)
                for j in range(TILES):
                    s, u = j % 2, j // 2
                    act.wait_ge(tab_mm[s], 2 * i + u + 1)
                    nc.scalar.activation(tab[:, j, :], tab_ps[0:TT, s, 0:ROW], ACT.Copy).then_inc(tab_ok[s], 1)
                    act.wait_ge(v_mm, 4 * i + j + 1)
                    nc.scalar.activation(v_t[:, j, :], v_ps[0:TT, 0:D], ACT.Copy).then_inc(v_ok, 1)
                    act.wait_ge(kneg_ok, 4 * i + j + 1)
                    act.wait_ge(k_ok, 4 * i)
                    nc.scalar.activation(kexp[:, j, :], kneg[:, j, :], ACT.Exp).then_inc(kexp_ok, 1)

        @block.vector
        def _(dve):
            dve.wait_ge(w_scores, 1)
            nc.vector.tensor_copy(w_gat[:, :, D:ROW], tab_ps[:, 0, 0:16].rearrange("p (h c) -> p h c", h=H2)).then_inc(w_scored, 1)
            with dve.Fori(0, NCH) as i:
                dve.wait_ge(mean_ok, i + 1)
                dve.wait_ge(squared, i)
                dve.wait_ge(xn_ok, i)
                nc.vector.tensor_tensor(cent[:], x_c[:], over_halves(mean_ps[:, 0:CH]), ALU.subtract).then_inc(centred, 1)
                dve.wait_ge(std_ok, i + 1)
                nc.vector.reciprocal(rstd[:], std[:]).then_inc(rstd_ok, 1)
                dve.wait_ge(rstd_ok, i + 1)
                dve.wait_ge(centred, i + 1)
                dve.wait_ge(rows_mm, 4 * i)
                dve.wait_ge(xn_out, 16 * i)
                nc.vector.tensor_tensor(xn[:], cent[:], over_halves(rstd[:]), ALU.mult).then_inc(xn_ok, 1)
                dve.wait_ge(rows_out, 16 * i)
                dve.wait_ge(kv_mm, i)
                for j in range(TILES):
                    dve.wait_ge(k_mm, 4 * i + j + 1)
                    dve.wait_ge(kexp_ok, 4 * i)
                    nc.vector.tensor_scalar(kneg[:, j, :], k_ps[0:TT, 0:D], 0.0, None, ALU.min).then_inc(kneg_ok, 1)
                    dve.wait_ge(rows_mm, 4 * i + j + 1)
                    nc.vector.tensor_copy(rows[:, j, :], rows_ps[0:TT, 0:D]).then_inc(rows_ok, 1)
                    dve.wait_ge(kexp_ok, 4 * i + j + 1)
                    nc.vector.scalar_tensor_tensor(k_t[:, j, :], k_ps[0:TT, 0:D], 0.0, kexp[:, j, :],
                                                   ALU.max, ALU.add).then_inc(k_ok, 1)
                dve.wait_ge(kv_mm, i + 1)
                dve.wait_ge(kv_ok, i)
                nc.vector.tensor_tensor(kv_acc[:], kv_acc[:], kv_ps[:, 0:H2 * KROW].rearrange("p (h c) -> p h c", h=H2),
                                        ALU.add).then_inc(kv_ok, 1)


GRP = 20
TINY = 1e-37


def stage_rank(nc, a, t):
    with ExitStack() as ctx:
        src_i = sb(nc, ctx, "r_src_i", [EP, EC], I32)
        part_i = sb(nc, ctx, "r_part_i", [EP, EC], I32)
        lo = sb(nc, ctx, "r_lo", [EP, EC], BF16)
        hi = sb(nc, ctx, "r_hi", [EP, EC], BF16)
        count = sb(nc, ctx, "r_count", [P, P], BF16)
        hot_lo = sb(nc, ctx, "r_hot_lo", [EP, 2, GRP, P], BF16)
        hot_hi = sb(nc, ctx, "r_hot_hi", [EP, 2, GRP, NT], BF16)
        zero = sb(nc, ctx, "r_zero", [P, P], BF16)
        ident = sb(nc, ctx, "r_ident", [P, P])
        noise = sb(nc, ctx, "r_noise", [P, NT])
        v_col = sb(nc, ctx, "r_v_col", [P, NT])
        v_row = sb(nc, ctx, "r_v_row", [NT, P])
        v_all = sb(nc, ctx, "r_v_all", [P, NP])
        before = sb(nc, ctx, "r_before", [P, 2 * NP], BF16)
        hits = sb(nc, ctx, "r_hits", [P, NP], BF16)
        rank_f = sb(nc, ctx, "r_rank_f", [P, NT])
        rank_i = sb(nc, ctx, "r_rank_i", [P, NT], I32)
        rank_row = sb(nc, ctx, "r_rank_row", [NT, P], I32)
        xrows = sb(nc, ctx, "r_xrows", [P, NT, D])
        deg_ps = ps(nc, ctx, "r_deg_ps", [P, 512])
        row_ps = ps(nc, ctx, "r_row_ps", [P, 512])
        (src_in, other_in, xrows_in, consts, before_ok, part_ok, lo_ok, hi_ok, deg_ok, vcol_ok, vrow_mm, vrow_ok,
         vrow_out, vall_in, rankf_ok, ranki_ok, rank_mm, rankrow_ok, rank_out, moved) = sems(
            nc, ctx, "r", "src_in other_in xrows_in consts before_ok part_ok lo_ok hi_ok deg_ok vcol_ok vrow_mm "
            "vrow_ok vrow_out vall_in rankf_ok ranki_ok rank_mm rankrow_ok rank_out moved")
        hotlo_ok = sems(nc, ctx, "r", "hotlo0 hotlo1")
        hothi_ok = sems(nc, ctx, "r", "hothi0 hothi1")
        hot_used = sems(nc, ctx, "r", "hot_used0 hot_used1")
        steps = EC // GRP // 2
        block = ctx.enter_context(nc.Block())

        @block.sync
        def _(sp):
            sp.dma_start(src_i[:], a["src"]).then_inc(src_in, 16)
            sp.dma_start(ident[:], a["ident"]).then_inc(other_in, 16)
            sp.dma_start(noise[:], a["noise"]).then_inc(other_in, 16)
            sp.dma_start(xrows[:], t["xn"].rearrange("(i p) f -> p i f", p=P)).then_inc(xrows_in, 16)
            sp.wait_ge(vrow_ok, 1)
            sp.dma_start(t["v"].rearrange("(i p) -> i p", p=P), v_row[:]).then_inc(vrow_out, 16)
            sp.wait_ge(vrow_out, 16)
            sp.dma_start(v_all[:], t["v"].unsqueeze(0).to_broadcast([P, NP])).then_inc(vall_in, 16)
            sp.wait_ge(rankrow_ok, 1)
            sp.dma_start(t["rank"].rearrange("(i p) -> i p", p=P), rank_row[:]).then_inc(rank_out, 16)
            sp.wait_ge(rank_out, 16)
            sp.wait_ge(moved, 16 * NT)

        @block.gpsimd
        def _(pool):
            nc.gpsimd.iota(count[:], [[1, P]], base=0, channel_multiplier=0,
                           allow_small_or_imprecise_dtypes=True).then_inc(consts, 1)
            nc.gpsimd.memset(zero[:], 0.0).then_inc(consts, 1)
            nc.gpsimd.memset(before[:], TINY).then_inc(before_ok, 1)
            pool.wait_ge(before_ok, 1)
            nc.gpsimd.affine_select(out=before[:], in_=before[:], compare_op=ALU.is_gt, fill=0.0, base=NP,
                                    pattern=[[-1, 2 * NP]], channel_multiplier=1).then_inc(before_ok, 1)
            pool.wait_ge(xrows_in, 16)
            pool.wait_ge(ranki_ok, 1)
            for i in range(NT):
                nc.gpsimd.indirect_dma_start(
                    out=t["xs"], out_offset=bass.IndirectOffsetOnAxis(ap=rank_i[:, i:i + 1], axis=0),
                    in_=xrows[:, i, :], in_offset=None).then_inc(moved, 16)

        @block.vector
        def _(dve):
            dve.wait_ge(src_in, 16)
            nc.vector.tensor_single_scalar(part_i[:], src_i[:], P - 1, op=ALU.bitwise_and).then_inc(part_ok, 1)
            dve.wait_ge(part_ok, 1)
            nc.vector.tensor_copy(lo[:], part_i[:]).then_inc(lo_ok, 1)
            dve.wait_ge(lo_ok, 1)
            nc.vector.tensor_single_scalar(part_i[:], src_i[:], 7, op=ALU.logical_shift_right).then_inc(part_ok, 1)
            dve.wait_ge(part_ok, 2)
            nc.vector.tensor_copy(hi[:], part_i[:]).then_inc(hi_ok, 1)
            dve.wait_ge(consts, 2)
            dve.wait_ge(hi_ok, 1)
            with dve.Fori(0, steps) as i:
                for s in range(2):
                    cols = bass.ds((i * 2 + s) * GRP, GRP)
                    dve.wait_ge(hot_used[s], i)
                    for hot, val, n, done in ((hot_lo, lo, P, hotlo_ok), (hot_hi, hi, NT, hothi_ok)):
                        nc.vector.tensor_tensor(hot[:, s], count[0:EP, 0:n].unsqueeze(1).to_broadcast([EP, GRP, n]),
                                                val[:, cols].unsqueeze(2).to_broadcast([EP, GRP, n]),
                                                ALU.is_equal).then_inc(done[s], 1)
            dve.wait_ge(deg_ok, 1)
            dve.wait_ge(other_in, 32)
            nc.vector.tensor_tensor(v_col[:], deg_ps[:, 0:NT], noise[:], ALU.add).then_inc(vcol_ok, 1)
            dve.wait_ge(vrow_mm, 1)
            nc.vector.tensor_copy(v_row[:], row_ps[0:NT, 0:P]).then_inc(vrow_ok, 1)
            dve.wait_ge(vall_in, 16)
            dve.wait_ge(before_ok, 2)
            dve.wait_ge(vcol_ok, 1)
            with dve.Fori(0, NT) as i:
                dve.wait_ge(rankf_ok, i)
                nc.vector.scalar_tensor_tensor(hits[:], v_all[:], v_col[:, bass.ds(i, 1)], before[:, bass.ds(i * (-P) + NP, NP)],
                                               ALU.subtract, ALU.is_lt, accum_out=rank_f[:, bass.ds(i, 1)]).then_inc(rankf_ok, 1)
            dve.wait_ge(rankf_ok, NT)
            nc.vector.tensor_copy(rank_i[:], rank_f[:]).then_inc(ranki_ok, 1)
            dve.wait_ge(rank_mm, 1)
            nc.vector.tensor_copy(rank_row[:], row_ps[0:NT, 0:P]).then_inc(rankrow_ok, 1)

        @block.tensor
        def _(pe):
            pe.wait_ge(consts, 2)
            nc.tensor.matmul(deg_ps[:, 0:NT], zero[:], zero[:, 0:NT], start=True, stop=False, skip_group_check=True)
            with pe.Fori(0, steps) as i:
                for s in range(2):
                    pe.wait_ge(hotlo_ok[s], i + 1)
                    pe.wait_ge(hothi_ok[s], i + 1)
                    for g in range(GRP):
                        last = nc.tensor.matmul(deg_ps[:, 0:NT], hot_lo[:, s, g, :], hot_hi[:, s, g, :],
                                                start=False, stop=False, skip_group_check=True)
                    last.then_inc(hot_used[s], 1)
            nc.tensor.matmul(deg_ps[:, 0:NT], zero[:], zero[:, 0:NT], start=False, stop=True,
                             skip_group_check=True).then_inc(deg_ok, 1)
            pe.wait_ge(other_in, 32)
            pe.wait_ge(vcol_ok, 1)
            nc.tensor.transpose(row_ps[0:NT, 0:P], v_col[:], ident[:]).then_inc(vrow_mm, 1)
            pe.wait_ge(rankf_ok, NT)
            pe.wait_ge(vrow_ok, 1)
            nc.tensor.transpose(row_ps[0:NT, 0:P], rank_f[:], ident[:]).then_inc(rank_mm, 1)


STATES = 16
TAPS = 4
DBC = 48


def stage_mamba(nc, a, t):
    with ExitStack() as ctx:
        ident = sb(nc, ctx, "m_ident", [P, P])
        w_in = sb(nc, ctx, "m_w_in", [P, H2, 2 * D])
        w_dbc = sb(nc, ctx, "m_w_dbc", [P, H2, DBC])
        w_dt = sb(nc, ctx, "m_w_dt", [DBC, D])
        w_out = sb(nc, ctx, "m_w_out", [P, H2, D])
        pick = sb(nc, ctx, "m_pick", [DBC, 2 * STATES, P])
        vecs = sb(nc, ctx, "m_vecs", [P, H2, TAPS + 3])
        a_log = sb(nc, ctx, "m_a_log", [P, H2, STATES])
        a_exp = sb(nc, ctx, "m_a_exp", [P, H2, STATES])
        a_neg = sb(nc, ctx, "m_a_neg", [P, H2, STATES])
        rows = sb(nc, ctx, "m_rows", [TT, TILES, D])
        xsT = sb(nc, ctx, "m_xsT", [P, H2, CH])
        tail = TAPS - 1
        xpad = sb(nc, ctx, "m_xpad", [P, H2, tail + CH])
        keep = sb(nc, ctx, "m_keep", [P, H2, tail])
        zs = sb(nc, ctx, "m_zs", [P, H2, CH])
        conv = sb(nc, ctx, "m_conv", [P, H2, CH])
        xc = sb(nc, ctx, "m_xc", [P, H2, CH])
        dbc = sb(nc, ctx, "m_dbc", [DBC, CH])
        pre = sb(nc, ctx, "m_pre", [P, H2, CH])
        nabs = sb(nc, ctx, "m_nabs", [P, H2, CH])
        ex = sb(nc, ctx, "m_ex", [P, H2, CH])
        ex1 = sb(nc, ctx, "m_ex1", [P, H2, CH])
        lg = sb(nc, ctx, "m_lg", [P, H2, CH])
        dt = sb(nc, ctx, "m_dt", [P, H2, CH])
        u = sb(nc, ctx, "m_u", [P, H2, CH])
        decay = sb(nc, ctx, "m_decay", [P, 2, H2, CH])
        drive = sb(nc, ctx, "m_drive", [P, 2, H2, CH])
        h_t = sb(nc, ctx, "m_h", [P, 2, H2, CH])
        hc = sb(nc, ctx, "m_hc", [P, 2, H2, CH])
        state = sb(nc, ctx, "m_state", [P, H2, STATES])
        ysum = sb(nc, ctx, "m_ysum", [P, H2, CH])
        yg = sb(nc, ctx, "m_yg", [P, H2, CH])
        yrow = sb(nc, ctx, "m_yrow", [TT, TILES, D])
        row_ps = ps(nc, ctx, "m_row_ps", [P, 512])
        lin_ps = ps(nc, ctx, "m_lin_ps", [P, 512])
        b_ps = ps(nc, ctx, "m_b_ps", [P, 2, 512])
        c_ps = ps(nc, ctx, "m_c_ps", [P, 2, 512])
        y_ps = ps(nc, ctx, "m_y_ps", [P, 2, 512])
        (w_ok, aexp_ok, aneg_ok, state0, rows_in, xs_mm, xs_ok, xz_mm, xz_ok, kept, keep_ok, tap, z_ok, xc_ok, dbc_mm, dbc_ok,
         dt_mm, pre_ok, nabs_ok, ex_ok, ex1_ok, lg_ok, resid, sum_ok, dt_ok, u_ok, ysum_ok, yg_ok, yrow_mm,
         yrow_ok, y_out) = sems(
            nc, ctx, "m", "w_ok aexp_ok aneg_ok state0 rows_in xs_mm xs_ok xz_mm xz_ok kept keep_ok tap z_ok xc_ok dbc_mm "
            "dbc_ok dt_mm pre_ok nabs_ok ex_ok ex1_ok lg_ok resid sum_ok dt_ok u_ok ysum_ok yg_ok yrow_mm yrow_ok y_out")
        b_mm, c_mm, decay_ok, drive_ok, scanned, hc_ok, hc_used, saved = (
            sems(nc, ctx, "m", f"{n}0 {n}1") for n in "b_mm c_mm decay_ok drive_ok scanned hc_ok hc_used saved".split())
        U = STATES // 2
        block = ctx.enter_context(nc.Block())

        @block.sync
        def _(sp):
            loads = [(ident[:], a["ident"]), (w_in[:], halves(a["in_projT"])), (w_dbc[:], halves(a["x_projT"])),
                     (w_dt[:], a["dt_projT"]), (w_out[:], halves(a["out_projT"])), (pick[:], a["pick"]),
                     (vecs[:], halves(a["mamba_vecs"])), (a_log[:], halves(a["A_log"]))]
            for dst, source in loads:
                sp.dma_start(dst, source).then_inc(w_ok, 16)
            with sp.Fori(0, NCH) as i:
                sp.wait_ge(xs_mm, 4 * i)
                sp.dma_start(rows[:], t["xs"][bass.ds(i * CH, CH), :].rearrange("(j p) f -> p j f", p=TT)).then_inc(rows_in, 16)
                sp.wait_ge(yrow_ok, 4 * i + 4)
                sp.dma_start(t["y"][bass.ds(i * CH, CH), :].rearrange("(j p) f -> p j f", p=TT), yrow[:]).then_inc(y_out, 16)
            sp.wait_ge(y_out, 16 * NCH)

        @block.tensor
        def _(pe):
            pe.wait_ge(w_ok, 16 * 8)
            with pe.Fori(0, NCH) as i:
                pe.wait_ge(rows_in, 16 * i + 16)
                for j in range(TILES):
                    pe.wait_ge(xs_ok, 4 * i + j)
                    pe.wait_ge(yrow_ok, 4 * i)
                    for k in range(H2):
                        last = nc.tensor.transpose(row_ps[:, k * TT:(k + 1) * TT], rows[:, j, k * P:(k + 1) * P], ident[0:TT, 0:TT])
                    last.then_inc(xs_mm, 1)
                pe.wait_ge(xs_ok, 4 * i + 4)
                for m in range(4):
                    pe.wait_ge(pre_ok, 2 * i) if m == 0 else pe.wait_ge(xz_ok, 2 * i + m) if m <= 2 else pe.wait_ge(z_ok, 2 * i + 1)
                    for k in range(H2):
                        last = nc.tensor.matmul(lin_ps[:, 0:CH], w_in[:, k, m * P:(m + 1) * P], xsT[:, k, :],
                                                start=(k == 0), stop=(k == 1))
                    last.then_inc(xz_mm, 1)
                pe.wait_ge(z_ok, 2 * i + 2)
                pe.wait_ge(xc_ok, 2 * i + 2)
                for k in range(H2):
                    last = nc.tensor.matmul(lin_ps[0:DBC, 0:CH], w_dbc[:, k, :], xc[:, k, :], start=(k == 0), stop=(k == 1))
                last.then_inc(dbc_mm, 1)
                pe.wait_ge(dbc_ok, i + 1)
                for k in range(H2):
                    pe.wait_ge(pre_ok, 2 * i + k)
                    nc.tensor.matmul(lin_ps[:, 0:CH], w_dt[:, k * P:(k + 1) * P], dbc[:], start=True, stop=True).then_inc(dt_mm, 1)

                def spread(s):
                    q, n = s % 2, s // 2
                    pe.wait_ge(drive_ok[q], U * i + n)
                    nc.tensor.matmul(b_ps[:, q, 0:CH], pick[:, s, :], dbc[:], start=True, stop=True).then_inc(b_mm[q], 1)
                    pe.wait_ge(hc_ok[q], U * i + n)
                    nc.tensor.matmul(c_ps[:, q, 0:CH], pick[:, STATES + s, :], dbc[:], start=True, stop=True).then_inc(c_mm[q], 1)

                spread(0)
                pe.wait_ge(ysum_ok, 2 * i)
                for s in range(STATES):
                    q, n = s % 2, s // 2
                    if s + 1 < STATES:
                        spread(s + 1)
                    pe.wait_ge(hc_ok[q], U * i + n + 1)
                    for k in range(H2):
                        last = nc.tensor.matmul(y_ps[:, k, 0:CH], ident[:], hc[:, q, k, :], start=(s == 0), stop=(s == STATES - 1))
                    last.then_inc(hc_used[q], 1)
                pe.wait_ge(yg_ok, i + 1)
                for j in range(TILES):
                    pe.wait_ge(yrow_ok, 4 * i + j)
                    for k in range(H2):
                        last = nc.tensor.matmul(row_ps[0:TT, 0:D], yg[:, k, j * TT:(j + 1) * TT], w_out[:, k, :],
                                                start=(k == 0), stop=(k == 1))
                    last.then_inc(yrow_mm, 1)

        @block.scalar
        def _(act):
            act.wait_ge(w_ok, 16 * 8)
            nc.scalar.activation(a_exp[:], a_log[:], ACT.Exp).then_inc(aexp_ok, 1)
            act.wait_ge(aneg_ok, 1)
            act.wait_ge(state0, 2)
            with act.Fori(0, NCH) as i:
                act.wait_ge(tap, 8 * i)
                act.wait_ge(kept, i)
                nc.scalar.activation(xpad[:, :, 0:tail], keep[:], ACT.Copy).then_inc(keep_ok, 1)
                for m in range(2):
                    act.wait_ge(xz_mm, 4 * i + m + 1)
                    act.wait_ge(keep_ok, i + 1)
                    nc.scalar.activation(xpad[:, m, tail:], lin_ps[:, 0:CH], ACT.Copy).then_inc(xz_ok, 1)
                act.wait_ge(xz_ok, 2 * i + 2)
                nc.scalar.activation(keep[:], xpad[:, :, CH:], ACT.Copy).then_inc(kept, 1)
                for m in range(2):
                    act.wait_ge(xz_mm, 4 * i + m + 3)
                    act.wait_ge(yg_ok, i)
                    nc.scalar.activation(zs[:, m, :], lin_ps[:, 0:CH], ACT.Silu).then_inc(z_ok, 1)
                for k in range(H2):
                    act.wait_ge(tap, 8 * i + 4 * k + 4)
                    act.wait_ge(ysum_ok, 2 * i)
                    nc.scalar.activation(xc[:, k, :], conv[:, k, :], ACT.Silu, bias=vecs[:, k, TAPS:TAPS + 1]).then_inc(xc_ok, 1)
                act.wait_ge(dbc_mm, i + 1)
                nc.scalar.activation(dbc[:], lin_ps[0:DBC, 0:CH], ACT.Copy).then_inc(dbc_ok, 1)
                act.wait_ge(nabs_ok, i + 1)
                nc.scalar.activation(ex[:], nabs[:], ACT.Exp).then_inc(ex_ok, 1)
                act.wait_ge(ex1_ok, i + 1)
                nc.scalar.activation(lg[:], ex1[:], ACT.Ln).then_inc(lg_ok, 1)
                act.wait_ge(dt_ok, i + 1)

                def save(s):
                    q, n = s % 2, s // 2
                    act.wait_ge(scanned[q], 2 * (U * i + n) + 2)
                    nc.scalar.activation(state[:, :, s:s + 1], h_t[:, q, :, CH - 1:CH], ACT.Copy).then_inc(saved[q], 1)

                for s in range(STATES + 2):
                    if s >= 2:
                        save(s - 2)
                    if s >= STATES:
                        continue
                    q, n = s % 2, s // 2
                    act.wait_ge(scanned[q], 2 * U * i + 2 * n)
                    for k in range(H2):
                        nc.scalar.activation(decay[:, q, k, :], dt[:, k, :], ACT.Exp, scale=a_neg[:, k, s:s + 1]).then_inc(decay_ok[q], 1)

        @block.gpsimd
        def _(pool):
            nc.gpsimd.memset(state[:], 0.0).then_inc(state0, 1)
            nc.gpsimd.memset(keep[:], 0.0).then_inc(state0, 1)

        @block.vector
        def _(dve):
            dve.wait_ge(aexp_ok, 1)
            nc.vector.tensor_scalar(a_neg[:], a_exp[:], -1.0, None, ALU.mult).then_inc(aneg_ok, 1)
            dve.wait_ge(state0, 2)
            with dve.Fori(0, NCH) as i:
                for j in range(TILES):
                    dve.wait_ge(xs_mm, 4 * i + j + 1)
                    dve.wait_ge(xz_mm, 4 * i)
                    nc.vector.tensor_copy(xsT[:, :, j * TT:(j + 1) * TT],
                                          row_ps[:, 0:H2 * TT].rearrange("p (k n) -> p k n", k=H2)).then_inc(xs_ok, 1)
                dve.wait_ge(keep_ok, i + 1)
                dve.wait_ge(xc_ok, 2 * i)
                for k in range(H2):
                    dve.wait_ge(xz_ok, 2 * i + k + 1)
                    nc.vector.tensor_scalar(conv[:, k, :], xpad[:, k, 0:CH], vecs[:, k, 0:1], None, ALU.mult).then_inc(tap, 1)
                    for c in range(1, TAPS):
                        dve.wait_ge(tap, 8 * i + 4 * k + c)
                        nc.vector.scalar_tensor_tensor(conv[:, k, :], xpad[:, k, c:c + CH], vecs[:, k, c:c + 1], conv[:, k, :],
                                                       ALU.mult, ALU.add).then_inc(tap, 1)
                for k in range(H2):
                    dve.wait_ge(dt_mm, 2 * i + k + 1)
                    nc.vector.tensor_scalar(pre[:, k, :], lin_ps[:, 0:CH], vecs[:, k, TAPS + 1:TAPS + 2], None, ALU.add).then_inc(pre_ok, 1)
                dve.wait_ge(pre_ok, 2 * i + 2)
                dve.wait_ge(ex_ok, i)
                nc.vector.scalar_tensor_tensor(nabs[:], pre[:], -1.0, pre[:], ALU.mult, ALU.min).then_inc(nabs_ok, 1)
                dve.wait_ge(ex_ok, i + 1)
                nc.vector.tensor_scalar(ex1[:], ex[:], 1.0, None, ALU.add).then_inc(ex1_ok, 1)
                dve.wait_ge(ex1_ok, i + 1)
                dve.wait_ge(lg_ok, i + 1)
                nc.vector.scalar_tensor_tensor(nabs[:], ex1[:], -1.0, ex[:], ALU.add, ALU.subtract).then_inc(resid, 1)
                dve.wait_ge(resid, i + 1)
                nc.vector.tensor_tensor(nabs[:], lg[:], nabs[:], ALU.subtract).then_inc(sum_ok, 1)
                dve.wait_ge(sum_ok, i + 1)
                dve.wait_ge(decay_ok[1], 2 * U * i)
                nc.vector.scalar_tensor_tensor(dt[:], pre[:], 0.0, nabs[:], ALU.max, ALU.add).then_inc(dt_ok, 1)
                dve.wait_ge(dt_ok, i + 1)
                dve.wait_ge(xc_ok, 2 * i + 2)
                dve.wait_ge(drive_ok[1], U * i)
                nc.vector.tensor_tensor(u[:], dt[:], xc[:], ALU.mult).then_inc(u_ok, 1)
                dve.wait_ge(u_ok, i + 1)

                def drive_of(s):
                    q, n = s % 2, s // 2
                    dve.wait_ge(b_mm[q], U * i + n + 1)
                    dve.wait_ge(scanned[q], 2 * (U * i + n))
                    nc.vector.tensor_tensor(drive[:, q], u[:], over_halves(b_ps[:, q, 0:CH]), ALU.mult).then_inc(drive_ok[q], 1)

                drive_of(0)
                for s in range(STATES):
                    q, n = s % 2, s // 2
                    if s + 1 < STATES:
                        drive_of(s + 1)
                    dve.wait_ge(drive_ok[q], U * i + n + 1)
                    dve.wait_ge(saved[q], U * i + n)
                    dve.wait_ge(hc_ok[q], U * i + n)
                    for k in range(H2):
                        dve.wait_ge(decay_ok[q], 2 * (U * i + n) + k + 1)
                        nc.vector.tensor_tensor_scan(h_t[:, q, k, :], decay[:, q, k, :], drive[:, q, k, :],
                                                     state[:, k, s:s + 1], ALU.mult, ALU.add).then_inc(scanned[q], 1)
                    dve.wait_ge(c_mm[q], U * i + n + 1)
                    dve.wait_ge(scanned[q], 2 * (U * i + n) + 2)
                    dve.wait_ge(hc_used[q], U * i + n)
                    nc.vector.tensor_tensor(hc[:, q], h_t[:, q], over_halves(c_ps[:, q, 0:CH]), ALU.mult).then_inc(hc_ok[q], 1)
                dve.wait_ge(hc_used[1], U * i + U)
                dve.wait_ge(yg_ok, i)
                for k in range(H2):
                    nc.vector.scalar_tensor_tensor(ysum[:, k, :], xc[:, k, :], vecs[:, k, TAPS + 2:TAPS + 3], y_ps[:, k, 0:CH],
                                                   ALU.mult, ALU.add).then_inc(ysum_ok, 1)
                dve.wait_ge(ysum_ok, 2 * i + 2)
                dve.wait_ge(z_ok, 2 * i + 2)
                dve.wait_ge(yrow_mm, 4 * i)
                nc.vector.tensor_tensor(yg[:], ysum[:], zs[:], ALU.mult).then_inc(yg_ok, 1)
                dve.wait_ge(y_out, 16 * i)
                for j in range(TILES):
                    dve.wait_ge(yrow_mm, 4 * i + j + 1)
                    nc.vector.tensor_copy(yrow[:, j, :], row_ps[0:TT, 0:D]).then_inc(yrow_ok, 1)


QUAD = 4
SLOTS = -(-(-(-E // P) + NT) // (2 * QUAD)) * 2 * QUAD
CODE = HEADS + 1
BIG = 1e30


def stage_attend(nc, a, t):
    with ExitStack() as ctx:
        ident = sb(nc, ctx, "g_ident", [P, P])
        token = sb(nc, ctx, "g_token", [P, 2])
        count = sb(nc, ctx, "g_count", [P, P])
        ones = sb(nc, ctx, "g_ones", [P, P])
        below = sb(nc, ctx, "g_below", [P, P])
        dst_i = sb(nc, ctx, "g_dst_i", [EP, EC], I32)
        dst_f = sb(nc, ctx, "g_dst_f", [EP, EC])
        ones_e = sb(nc, ctx, "g_ones_e", [EP, EC])
        less = sb(nc, ctx, "g_less", [EP, EC])
        bound = sb(nc, ctx, "g_bound", [P, NT + 1])
        part = sb(nc, ctx, "g_part", [EP, NT + 1])
        first = sb(nc, ctx, "g_first", [NT, 4])
        slots_i = sb(nc, ctx, "g_slots_i", [NT, 1], I32)
        tile_no = sb(nc, ctx, "g_tile_no", [NT, P])
        kk = sb(nc, ctx, "g_kk", [NT, SLOTS])
        hot = sb(nc, ctx, "g_hot", [NT, SLOTS])
        hot2 = sb(nc, ctx, "g_hot2", [NT, SLOTS])
        at = sb(nc, ctx, "g_at", [NT, SLOTS])
        slot_at = sb(nc, ctx, "g_slot_at", [1, SLOTS], I32)
        slot_tile = sb(nc, ctx, "g_slot_tile", [1, SLOTS], I32)
        slot_base = sb(nc, ctx, "g_slot_base", [P, SLOTS])
        score = sb(nc, ctx, "g_score", [P, NT, 2 * HEADS])
        code = sb(nc, ctx, "g_code", [P, NT, CODE])
        top = sb(nc, ctx, "g_top", [P, 8])
        top8 = sb(nc, ctx, "g_top8", [8, 1])
        lift = sb(nc, ctx, "g_lift", [1, 8])
        shift = sb(nc, ctx, "g_shift", [P, 1])
        guard = sb(nc, ctx, "g_guard", [P, 1])
        emax = sb(nc, ctx, "g_emax", [P, QUAD * HEADS])
        agg = sb(nc, ctx, "g_agg", [P, NT, D + HEADS])
        den = sb(nc, ctx, "g_den", [P, NT, HEADS])
        idx = sb(nc, ctx, "g_idx", [P, 2, QUAD, 2], I32)
        rel = sb(nc, ctx, "g_rel", [P, 2, QUAD])
        got = sb(nc, ctx, "g_got", [P, 2, QUAD, ROW])
        sel = sb(nc, ctx, "g_sel", [P, 2, QUAD, P])
        selT = sb(nc, ctx, "g_selT", [P, 2, QUAD, P])
        z = sb(nc, ctx, "g_z", [P, 2, QUAD, HEADS])
        pen = sb(nc, ctx, "g_pen", [P, 2, QUAD])
        lr = sb(nc, ctx, "g_lr", [P, 2, QUAD, HEADS])
        logit = sb(nc, ctx, "g_logit", [P, 2, QUAD, HEADS])
        wrow = sb(nc, ctx, "g_wrow", [P, 2, QUAD, D + HEADS])
        selT_ps = ps(nc, ctx, "g_selT_ps", [P, 2, 512])
        st_ps = ps(nc, ctx, "g_st_ps", [P, 2, 512])
        acc_ps = ps(nc, ctx, "g_acc_ps", [P, 2, 512])
        set_ps = ps(nc, ctx, "g_set_ps", [P, 2, 512])
        (settled, w_ok, score_in, consts, zeroed, dve_set, pe_set, act_set, emax_ok, fin, stored) = sems(
            nc, ctx, "g", "settled w_ok score_in consts zeroed dve_set pe_set act_set emax_ok fin stored")
        (idx_in, rel_ok, got_in, sel_ok, selT_mm, selT_ok, st_mm, z_ok, pen_ok, lr_ok, logit_ok, exp_ok, w_row_ok) = (
            sems(nc, ctx, "g", f"{n}0 {n}1") for n in
            "idx_in rel_ok got_in sel_ok selT_mm selT_ok st_mm z_ok pen_ok lr_ok logit_ok exp_ok w_row_ok".split())
        acc_mm = sems(nc, ctx, "g", "acc_mm0 acc_mm1")
        acc_ok = sems(nc, ctx, "g", "acc_ok0 acc_ok1")
        HS = SLOTS // 2
        block = ctx.enter_context(nc.Block())
        rounds = SLOTS // QUAD // 2

        @block.sync
        def _(sp):
            for dst, source in ((ident[:], a["ident"]), (below[:], a["below"]), (dst_i[:], a["dst"])):
                sp.dma_start(dst, source).then_inc(w_ok, 16)
            sp.dma_start(score[:], t["table"].rearrange("(i p) f -> p i f", p=P)[:, :, D:ROW]).then_inc(score_in, 16)
            sp.wait_ge(dve_set, 13)
            with sp.Fori(0, rounds) as i:
                for q in range(2):
                    sp.wait_ge(w_row_ok[q], i)
                    sp.wait_ge(rel_ok[q], i)
                    for j in range(QUAD):
                        e0 = sp.value_load(slot_at[0:1, bass.ds((i * 2 + q) * QUAD + j, 1)], min_val=0, max_val=E)
                        sp.dma_start(idx[:, q, j, :], a["edges"][bass.ds(e0, P), :]).then_inc(idx_in[q], 16)
            sp.wait_ge(fin, 3)
            sp.dma_start(t["agg"].rearrange("(i p) f -> p i f", p=P), agg[:, :, 0:D]).then_inc(stored, 16)
            sp.wait_ge(stored, 16)

        @block.gpsimd
        def _(pool):
            nc.gpsimd.iota(count[:], [[1, P]], base=0, channel_multiplier=0, allow_small_or_imprecise_dtypes=True).then_inc(consts, 1)
            nc.gpsimd.iota(bound[:], [[P, NT + 1]], base=0, channel_multiplier=0, allow_small_or_imprecise_dtypes=True).then_inc(consts, 1)
            nc.gpsimd.iota(tile_no[:], [[0, P]], base=0, channel_multiplier=1, allow_small_or_imprecise_dtypes=True).then_inc(consts, 1)
            nc.gpsimd.iota(kk[:], [[1, SLOTS]], base=0, channel_multiplier=0, allow_small_or_imprecise_dtypes=True).then_inc(consts, 1)
            nc.gpsimd.memset(ones[:], 1.0).then_inc(consts, 1)
            nc.gpsimd.memset(ones_e[:], 1.0).then_inc(consts, 1)
            nc.gpsimd.memset(code[:], 1.0).then_inc(consts, 1)
            nc.gpsimd.memset(emax[:], -BIG).then_inc(zeroed, 1)
            nc.gpsimd.memset(agg[:], 0.0).then_inc(zeroed, 1)
            nc.gpsimd.memset(token[:], 0.0).then_inc(zeroed, 1)
            pool.wait_ge(zeroed, 3)
            with pool.Fori(0, rounds) as i:
                for q in range(2):
                    pool.wait_ge(w_row_ok[q], i)
                    pool.wait_ge(idx_in[q], (i + 1) * 16 * QUAD)
                    settle(nc, pool, token, settled, 2 * i + q)
                    for j in range(QUAD):
                        nc.gpsimd.indirect_dma_start(
                            out=got[:, q, j, :], out_offset=None, in_=t["table"],
                            in_offset=bass.IndirectOffsetOnAxis(ap=idx[:, q, j, 0:1], axis=0)).then_inc(got_in[q], 16)

        @block.tensor
        def _(pe):
            pe.wait_ge(w_ok, 48)
            pe.wait_ge(consts, 7)
            pe.wait_ge(dve_set, 2)
            nc.tensor.matmul(set_ps[0:NT, 0, 0:1], part[:, 0:NT], ones[0:EP, 0:1], start=True, stop=True)
            nc.tensor.matmul(set_ps[0:NT, 0, 1:2], part[:, 1:NT + 1], ones[0:EP, 0:1], start=True, stop=True).then_inc(pe_set, 1)
            pe.wait_ge(dve_set, 7)
            nc.tensor.matmul(set_ps[0:NT, 0, 2:3], below[0:NT, 0:NT], first[:, 2:3], start=True, stop=True).then_inc(pe_set, 1)
            pe.wait_ge(dve_set, 12)
            for c in range(2):
                cols = slice(c * HS, (c + 1) * HS)
                pe.wait_ge(dve_set, 12 if c == 0 else 13)
                nc.tensor.matmul(set_ps[0:1, 0, 0:HS], ones[0:NT, 0:1], at[:, cols], start=True, stop=True).then_inc(pe_set, 1)
                nc.tensor.matmul(set_ps[:, 1, 0:HS], tile_no[:], hot2[:, cols], start=True, stop=True).then_inc(pe_set, 1)
                pe.wait_ge(dve_set, 13 + 3 * c + 2)
            pe.wait_ge(dve_set, 20)
            nc.tensor.transpose(set_ps[0:8, 0, 0:P], top[:], ident[:]).then_inc(pe_set, 1)
            pe.wait_ge(dve_set, 21)
            nc.tensor.matmul(set_ps[0:1, 1, 0:8], top8[:], ident[0:8, 0:8], start=True, stop=True).then_inc(pe_set, 1)
            pe.wait_ge(dve_set, 26)
            nc.tensor.matmul(set_ps[:, 0, 0:1], ones[0:1, :], lift[:, 7:8], start=True, stop=True).then_inc(pe_set, 1)

            with pe.Fori(0, rounds) as i:
                for q in range(2):
                    tiles = [pe.value_load(slot_tile[0:1, bass.ds((i * 2 + q) * QUAD + j, 1)], min_val=0, max_val=NT - 1)
                             for j in range(QUAD)]
                    pe.wait_ge(sel_ok[q], i + 1)
                    pe.wait_ge(selT_ok[q], i)
                    for j in range(QUAD):
                        last = nc.tensor.transpose(selT_ps[:, q, j * P:(j + 1) * P], sel[:, q, j, :], ident[:])
                    last.then_inc(selT_mm[q], 1)
                    pe.wait_ge(selT_ok[q], i + 1)
                    pe.wait_ge(pen_ok[q], i)
                    for j in range(QUAD):
                        last = nc.tensor.matmul(st_ps[:, q, j * CODE:(j + 1) * CODE], selT[:, q, j, :],
                                                code[:, bass.ds(tiles[j], 1), :], start=True, stop=True)
                    last.then_inc(st_mm[q], 1)
                    pe.wait_ge(w_row_ok[q], i + 1)
                    for j in range(QUAD):
                        b, n = j % 2, 2 * q + j // 2
                        pe.wait_ge(acc_ok[b], 4 * i + n)
                        nc.tensor.matmul(acc_ps[:, b, 0:D + HEADS], sel[:, q, j, :], wrow[:, q, j, :],
                                         start=True, stop=True).then_inc(acc_mm[b], 1)
            pe.wait_ge(fin, 1)
            nc.tensor.transpose(set_ps[0:1, 0, 0:P], top[:, 0:1], ident[:]).then_inc(pe_set, 1)
            pe.wait_ge(act_set, 1)
            nc.tensor.matmul(set_ps[:, 1, 0:1], ones[0:1, :], lift[:, 6:7], start=True, stop=True).then_inc(pe_set, 1)

        @block.scalar
        def _(act):
            with act.Fori(0, rounds) as i:
                for q in range(2):
                    act.wait_ge(selT_mm[q], i + 1)
                    act.wait_ge(st_mm[q], i)
                    nc.scalar.activation(selT[:, q].rearrange("p j n -> p (j n)"), selT_ps[:, q, :], ACT.Copy).then_inc(selT_ok[q], 1)
                    act.wait_ge(logit_ok[q], i + 1)
                    act.wait_ge(acc_mm[1], 4 * i)
                    act.wait_ge(dve_set, 27)
                    nc.scalar.activation(wrow[:, q, :, D:], logit[:, q], ACT.Exp, bias=shift[:]).then_inc(exp_ok[q], 1)
            act.wait_ge(fin, 2)
            nc.scalar.activation(lift[:, 6:7], lift[:, 5:6], ACT.Exp, bias=shift[0:1, :]).then_inc(act_set, 1)

        @block.vector
        def _(dve):
            step = [0]

            def set_up(ins):
                step[0] += 1
                ins.then_inc(dve_set, 1)
                dve.wait_ge(dve_set, step[0])

            dve.wait_ge(w_ok, 48)
            dve.wait_ge(consts, 7)
            set_up(nc.vector.tensor_copy(dst_f[:], dst_i[:]))
            for b in range(NT + 1):
                last = nc.vector.scalar_tensor_tensor(less[:], dst_f[:], bound[0:EP, b:b + 1], ones_e[:], ALU.is_lt, ALU.mult,
                                                      accum_out=part[:, b:b + 1])
                if b < NT:
                    last.then_inc(emax_ok, 1)
                    dve.wait_ge(emax_ok, b + 1)
            set_up(last)
            dve.wait_ge(pe_set, 1)
            set_up(nc.vector.tensor_copy(first[:, 0:2], set_ps[0:NT, 0, 0:2]))
            set_up(nc.vector.scalar_tensor_tensor(first[:, 1:2], first[:, 0:1], -1.0, first[:, 1:2], ALU.mult, ALU.add))
            set_up(nc.vector.tensor_scalar(slots_i[:], first[:, 1:2], float(P - 1), None, ALU.add))
            set_up(nc.vector.tensor_single_scalar(slots_i[:], slots_i[:], 7, op=ALU.logical_shift_right))
            set_up(nc.vector.tensor_copy(first[:, 2:3], slots_i[:]))
            dve.wait_ge(pe_set, 2)
            set_up(nc.vector.tensor_copy(first[:, 3:4], set_ps[0:NT, 0, 2:3]))
            set_up(nc.vector.tensor_scalar(hot[:], kk[:], first[:, 3:4], None, ALU.is_ge))
            set_up(nc.vector.tensor_scalar(at[:], kk[:], first[:, 3:4], first[:, 2:3], ALU.subtract, ALU.subtract))
            set_up(nc.vector.scalar_tensor_tensor(hot2[:], at[:], 0.0, hot[:], ALU.is_lt, ALU.mult))
            nc.vector.tensor_scalar(hot[:], kk[:], first[:, 3:4], float(P), ALU.subtract, ALU.mult).then_inc(emax_ok, 1)
            dve.wait_ge(emax_ok, NT + 1)
            nc.vector.tensor_scalar(at[:], hot[:], first[:, 0:1], float(-E), ALU.add, ALU.add).then_inc(emax_ok, 1)
            dve.wait_ge(emax_ok, NT + 2)
            set_up(nc.vector.tensor_tensor(at[:], at[:], hot2[:], ALU.mult))
            for c in range(2):
                cols = slice(c * HS, (c + 1) * HS)
                dve.wait_ge(pe_set, 4 + 2 * c)
                set_up(nc.vector.tensor_scalar(slot_at[:, cols], set_ps[0:1, 0, 0:HS], float(E), None, ALU.add))
                set_up(nc.vector.tensor_scalar(slot_base[:, cols], set_ps[:, 1, 0:HS], float(P), None, ALU.mult))
                set_up(nc.vector.tensor_copy(slot_tile[:, cols], set_ps[0:1, 1, 0:HS]))
            dve.wait_ge(score_in, 16)
            set_up(nc.vector.tensor_copy(code[:, :, 0:HEADS], score[:, :, HEADS:]))
            set_up(nc.vector.tensor_reduce(top[:], score[:].rearrange("p i h -> p h i"), AX.X, ALU.max))
            dve.wait_ge(pe_set, 7)
            set_up(nc.vector.tensor_reduce(top8[:], set_ps[0:8, 0, 0:P], AX.X, ALU.max))
            dve.wait_ge(pe_set, 8)
            set_up(nc.vector.tensor_copy(lift[:], set_ps[0:1, 1, 0:8]))
            set_up(nc.vector.tensor_tensor(lift[:, 0:4], lift[:, 0:4], lift[:, 4:8], ALU.add))
            set_up(nc.vector.scalar_tensor_tensor(lift[:, 0:4], lift[:, 0:4], 0.2, lift[:, 0:4], ALU.mult, ALU.max))
            set_up(nc.vector.tensor_reduce(lift[:, 4:5], lift[:, 0:4], AX.X, ALU.max))
            set_up(nc.vector.tensor_scalar(lift[:, 7:8], lift[:, 4:5], -1.0, None, ALU.mult))
            dve.wait_ge(pe_set, 9)
            set_up(nc.vector.tensor_copy(shift[:], set_ps[:, 0, 0:1]))
            dve.wait_ge(zeroed, 2)

            with dve.Fori(0, rounds) as i:
                for q in range(2):
                    dve.wait_ge(idx_in[q], (i + 1) * 16 * QUAD)
                    nc.vector.tensor_tensor(rel[:, q], idx[:, q, :, 1], slot_base[:, bass.ds((i * 2 + q) * QUAD, QUAD)],
                                            ALU.subtract).then_inc(rel_ok[q], 1)
                    dve.wait_ge(rel_ok[q], i + 1)
                    dve.wait_ge(acc_mm[1], 4 * i)
                    nc.vector.tensor_tensor(sel[:, q], count[:].unsqueeze(1).to_broadcast([P, QUAD, P]),
                                            rel[:, q].unsqueeze(2).to_broadcast([P, QUAD, P]), ALU.is_equal).then_inc(sel_ok[q], 1)
                    dve.wait_ge(st_mm[q], i + 1)
                    dve.wait_ge(got_in[q], (i + 1) * 16 * QUAD)
                    st = st_ps[:, q, 0:QUAD * CODE].rearrange("p (j c) -> p j c", c=CODE)
                    nc.vector.tensor_tensor(z[:, q], got[:, q, :, D:D + HEADS], st[:, :, 0:HEADS], ALU.add).then_inc(z_ok[q], 1)
                    nc.vector.tensor_scalar(pen[:, q], st[:, :, HEADS], BIG, -BIG, ALU.mult, ALU.add).then_inc(pen_ok[q], 1)
                    dve.wait_ge(z_ok[q], i + 1)
                    nc.vector.scalar_tensor_tensor(lr[:, q], z[:, q], 0.2, z[:, q], ALU.mult, ALU.max).then_inc(lr_ok[q], 1)
                    dve.wait_ge(lr_ok[q], i + 1)
                    dve.wait_ge(pen_ok[q], i + 1)
                    dve.wait_ge(exp_ok[q], i)
                    nc.vector.tensor_tensor(logit[:, q], lr[:, q], pen[:, q].unsqueeze(2).to_broadcast([P, QUAD, HEADS]),
                                            ALU.add).then_inc(logit_ok[q], 1)
                    dve.wait_ge(logit_ok[q], i + 1)
                    dve.wait_ge(emax_ok, 2 * i + q + NT + 2)
                    nc.vector.tensor_tensor(emax[:], emax[:], logit[:, q].rearrange("p j h -> p (j h)"), ALU.max).then_inc(emax_ok, 1)
                    dve.wait_ge(exp_ok[q], i + 1)
                    for j in range(QUAD):
                        last = nc.vector.tensor_tensor(wrow[:, q, j, 0:D].rearrange("p (h f) -> p h f", h=HEADS),
                                                       got[:, q, j, 0:D].rearrange("p (h f) -> p h f", h=HEADS),
                                                       wrow[:, q, j, D:].unsqueeze(2).to_broadcast([P, HEADS, FO]), ALU.mult)
                    last.then_inc(w_row_ok[q], 1)
                    for j in range(QUAD):
                        b, n = j % 2, 2 * q + j // 2
                        tile = dve.value_load(slot_tile[0:1, bass.ds((i * 2 + q) * QUAD + j, 1)], min_val=0, max_val=NT - 1)
                        dve.wait_ge(acc_mm[b], 4 * i + n + 1)
                        dve.wait_ge(acc_ok[1 - b], 4 * i + n + b)
                        here = agg[:, bass.ds(tile, 1), :].rearrange("p i f -> p (i f)")
                        nc.vector.tensor_tensor(here, here, acc_ps[:, b, 0:D + HEADS], ALU.add).then_inc(acc_ok[b], 1)
            dve.wait_ge(emax_ok, 2 * rounds + NT + 2)
            nc.vector.tensor_reduce(top[:, 0:1], emax[:], AX.X, ALU.max).then_inc(fin, 1)
            dve.wait_ge(pe_set, 10)
            nc.vector.tensor_reduce(lift[:, 5:6], set_ps[0:1, 0, 0:P], AX.X, ALU.max).then_inc(fin, 1)
            dve.wait_ge(pe_set, 11)
            nc.vector.tensor_scalar(guard[:], set_ps[:, 1, 0:1], 1e-16, None, ALU.mult).then_inc(dve_set, 1)
            dve.wait_ge(dve_set, 28)
            for b in range(2):
                dve.wait_ge(acc_ok[b], 4 * rounds)
            nc.vector.tensor_scalar(den[:], agg[:, :, D:], guard[:], None, ALU.add).then_inc(dve_set, 1)
            dve.wait_ge(dve_set, 29)
            nc.vector.reciprocal(den[:], den[:]).then_inc(dve_set, 1)
            dve.wait_ge(dve_set, 30)
            for i in range(NT):
                mean = agg[:, i, 0:D].rearrange("p (h f) -> p h f", h=HEADS)
                last = nc.vector.tensor_tensor(mean, mean, den[:, i, :].unsqueeze(2).to_broadcast([P, HEADS, FO]), ALU.mult)
            last.then_inc(fin, 1)


EXPERTS = 8
ATT_EPS = 1e-6
LNS = 7
(LN_LOCAL, LN_GLOBAL, LN_MSG, LN_GNN, LN_MIX, LN_ROUTER, LN_EXPERT) = range(LNS)
LIN_USES = 22


def stage_mix(nc, a, t):
    with ExitStack() as ctx:
        ident = sb(nc, ctx, "x_ident", [P, P])
        inv_d = sb(nc, ctx, "x_inv_d", [P, P])
        w2 = {n: sb(nc, ctx, f"x_{n}", [P, H2, D]) for n in ("wlT", "wgT", "Wq", "Wm")}
        w_ff1 = sb(nc, ctx, "x_ff1", [P, H2, 2 * D])
        w_ff2 = sb(nc, ctx, "x_ff2", [P, 4, D])
        w_m1 = sb(nc, ctx, "x_m1", [P, 4, 2 * D])
        w_m2 = sb(nc, ctx, "x_m2", [P, 4, D])
        w_r = sb(nc, ctx, "x_wr", [P, H2, EXPERTS])
        b_r = sb(nc, ctx, "x_br", [TT, EXPERTS])
        vecs = sb(nc, ctx, "x_vecs", [P, H2, 12])
        b_ff1 = sb(nc, ctx, "x_bff1", [P, 4])
        eps = sb(nc, ctx, "x_eps", [P, 1])
        same = sb(nc, ctx, "x_same", [P, P])
        kv = sb(nc, ctx, "x_kv", [P, H2, KROW])
        kv_blk = sb(nc, ctx, "x_kv_blk", [P, H2, P])
        ks_blk = sb(nc, ctx, "x_ks_blk", [P, H2, P])
        rank = sb(nc, ctx, "x_rank", [TT, NTT], I32)

        def two(name, shape):
            return [sb(nc, ctx, f"x_{name}{q}", shape) for q in range(2)]

        x, xn, low, up, hl, ha, cent, sq, qp, msg, gate, h, res, mix = (
            two(n, [P, H2, CH]) for n in "x xn low up hl ha cent sq qp msg gate h res mix".split())
        std, den = two("std", [P, CH]), two("den", [P, CH])
        y_at = [sb(nc, ctx, f"x_y_at{q}", [TT, TILES], I32) for q in range(2)]
        arow, yrow = two("arow", [TT, TILES, D]), two("yrow", [TT, TILES, D])
        wide = two("wide", [P, 4, CH])
        logit = two("logit", [TT, TILES, EXPERTS])
        mean_ps = [ps(nc, ctx, f"x_mean_ps{q}", [P, 512]) for q in range(2)]
        var_ps = [ps(nc, ctx, f"x_var_ps{q}", [P, 512]) for q in range(2)]
        lin_ps = [[ps(nc, ctx, f"x_lin_ps{q}{b}", [P, 512]) for b in range(2)] for q in range(2)]
        token = sb(nc, ctx, "x_token", [P, 2])
        settled, w_ok, consts, token_ok, blk_ok = sems(nc, ctx, "x", "settled w_ok consts token_ok blk_ok")
        (rows_in, y_at_ok, y_in, low_ok, up_ok, exp_ok, elu_ok, qlow_ok, qexp_ok, q_ok, den_ok, msg_ok, diff_ok, gated_ok, h_ok,
         sum1_ok, sum2_ok, x2_ok, sq_ok, log_ok, norm_ok, gain_ok, stored) = (
            sems(nc, ctx, "x", f"{n}0 {n}1") for n in
            "rows_in y_at_ok y_in low_ok up_ok exp_ok elu_ok qlow_ok qexp_ok q_ok den_ok msg_ok diff_ok gated_ok h_ok "
            "sum1_ok sum2_ok x2_ok sq_ok log_ok norm_ok gain_ok stored".split())
        mean_full, mean_read, var_full, var_read = (
            sems(nc, ctx, "x", f"{n}0 {n}1") for n in "mean_full mean_read var_full var_read".split())
        lin_full = [sems(nc, ctx, "x", f"lin_full{q}0 lin_full{q}1") for q in range(2)]
        lin_read = [sems(nc, ctx, "x", f"lin_read{q}0 lin_read{q}1") for q in range(2)]
        MEAN_USES = 1 + LNS + 1
        VAR_USES = 1 + LNS
        BANK_USES = 1 + LIN_USES // 2 + TILES
        pairs = NCH // 2
        Q_, NUM, GATE, WM, FF1, FF2, M1, M2 = 0, 2, 6, 8, 10, 14, 16, 20
        block = ctx.enter_context(nc.Block())

        def v(n, k):
            return vecs[:, k, n:n + 1]

        def chunk(i, q):
            return bass.ds((i * 2 + q) * CH, CH)

        @block.sync
        def _(sp):
            loads = [(ident[:], a["ident"]), (w_ff1[:], halves(a["ff1T"])), (w_ff2[:], a["ff2T"].rearrange("(h p) n -> p h n", p=P)),
                     (w_m1[:], a["W1"].rearrange("(h p) n -> p h n", p=P)), (w_m2[:], a["W2"].rearrange("(h p) n -> p h n", p=P)),
                     (w_r[:], halves(a["Wr"])), (b_r[:], a["br"].unsqueeze(0).to_broadcast([TT, EXPERTS])),
                     (vecs[:], halves(a["mix_vecs"])), (b_ff1[:], a["ff1_b"]),
                     (same[:], a["same"]), (kv[:], t["kv"])]
            loads += [(w2[n][:], halves(a[n])) for n in w2]
            assert len(loads) == 15
            for dst, source in loads:
                sp.dma_start(dst, source).then_inc(w_ok, 16)
            with nc.allow_non_contiguous_dma(reason="one rank per partition and token tile"):
                sp.dma_start(rank[:], t["rank"].rearrange("(i p) -> p i", p=TT)).then_inc(w_ok, 16)
            with sp.Fori(0, pairs) as i:
                for q in range(2):
                    sp.wait_ge(stored[q], 48 * i)
                    sp.dma_start(x[q][:], halves(a["xT"])[:, :, chunk(i, q)]).then_inc(rows_in[q], 16)
                    sp.dma_start(xn[q][:], halves(t["xnT"])[:, :, chunk(i, q)]).then_inc(rows_in[q], 16)
                    sp.dma_start(arow[q][:], t["agg"][chunk(i, q), :].rearrange("(j p) f -> p j f", p=TT)).then_inc(rows_in[q], 16)
                for q in range(2):
                    sp.wait_ge(mean_read[q], MEAN_USES * (i + 1))
                    sp.dma_start(t["logit"][chunk(i, q), :].rearrange("(j p) f -> p j f", p=TT), logit[q][:]).then_inc(stored[q], 16)
                    sp.wait_ge(lin_read[q][0], BANK_USES * (i + 1))
                    sp.dma_start(t["x2"][chunk(i, q), :].rearrange("(j p) f -> p j f", p=TT), arow[q][:]).then_inc(stored[q], 16)
                    sp.wait_ge(lin_read[q][1], BANK_USES * (i + 1))
                    sp.dma_start(t["xe"][chunk(i, q), :].rearrange("(j p) f -> p j f", p=TT), yrow[q][:]).then_inc(stored[q], 16)
            for q in range(2):
                sp.wait_ge(stored[q], 48 * pairs)

        @block.gpsimd
        def _(pool):
            nc.gpsimd.memset(inv_d[:], 1.0 / D).then_inc(consts, 1)
            nc.gpsimd.memset(eps[:], LN_EPS).then_inc(consts, 1)
            nc.gpsimd.memset(token[:], 0.0).then_inc(token_ok, 1)
            pool.wait_ge(token_ok, 1)
            with pool.Fori(0, pairs) as i:
                for q in range(2):
                    pool.wait_ge(stored[q], 48 * i)
                    pool.wait_ge(y_at_ok[q], i + 1)
                    settle(nc, pool, token, settled, 2 * i + q)
                    for j in range(TILES):
                        nc.gpsimd.indirect_dma_start(
                            out=yrow[q][:, j, :], out_offset=None, in_=t["y"],
                            in_offset=bass.IndirectOffsetOnAxis(ap=y_at[q][:, j:j + 1], axis=0)).then_inc(y_in[q], 16)

        @block.tensor
        def _(pe):
            pe.wait_ge(w_ok, 256)
            pe.wait_ge(consts, 2)
            pe.wait_ge(blk_ok, 4)
            with pe.Fori(0, pairs) as i:
                def lin(q, u, products):
                    b, n = u % 2, u // 2 + 1
                    pe.wait_ge(lin_read[q][b], BANK_USES * i + n)
                    for m, (w, r) in enumerate(products):
                        last = nc.tensor.matmul(lin_ps[q][b][:, 0:CH], w, r, start=(m == 0), stop=(m == len(products) - 1))
                    last.then_inc(lin_full[q][b], 1)

                def dense(q, u, weights, inputs, outs):
                    for m in range(outs):
                        lin(q, u + m, [(w[:, k, m * P:(m + 1) * P], r) for (w, k), r in zip(weights, inputs)])

                def written(q, u):
                    pe.wait_ge(lin_read[q][u % 2], BANK_USES * i + u // 2 + 2)

                def mean_of(q, n, src):
                    pe.wait_ge(mean_read[q], MEAN_USES * i + 1 + n)
                    for k in range(H2):
                        last = nc.tensor.matmul(mean_ps[q][:, 0:CH], inv_d[:], src[q][:, k, :], start=(k == 0), stop=(k == 1))
                    last.then_inc(mean_full[q], 1)

                def var_of(n):
                    for q in TWO:
                        pe.wait_ge(sq_ok[q], LNS * i + n + 1)
                        pe.wait_ge(var_read[q], VAR_USES * i + 1 + n)
                        for k in range(H2):
                            last = nc.tensor.matmul(var_ps[q][:, 0:CH], inv_d[:], sq[q][:, k, :], start=(k == 0), stop=(k == 1))
                        last.then_inc(var_full[q], 1)

                def xh(buf, q):
                    return [buf[q][:, k, :] for k in range(buf[q].shape[1])]

                TWO = range(2)
                for q in TWO:
                    pe.wait_ge(rows_in[q], 48 * (i + 1))
                    for k, (bank, read, uses, full) in enumerate(((mean_ps, mean_read, MEAN_USES, mean_full),
                                                                  (var_ps, var_read, VAR_USES, var_full))):
                        pe.wait_ge(read[q], uses * i)
                        for j in range(TILES):
                            last = nc.tensor.transpose(bank[q][:, j * TT:(j + 1) * TT], arow[q][:, j, k * P:(k + 1) * P], ident[0:TT, 0:TT])
                        last.then_inc(full[q], 1)
                for q in TWO:
                    pe.wait_ge(y_in[q], 64 * (i + 1))
                    for k in range(H2):
                        pe.wait_ge(lin_read[q][k], BANK_USES * i)
                        for j in range(TILES):
                            last = nc.tensor.transpose(lin_ps[q][k][:, j * TT:(j + 1) * TT], yrow[q][:, j, k * P:(k + 1) * P], ident[0:TT, 0:TT])
                        last.then_inc(lin_full[q][k], 1)
                for q in TWO:
                    dense(q, Q_, [(w2["Wq"], 0), (w2["Wq"], 1)], xh(xn, q), 2)
                for q in TWO:
                    pe.wait_ge(elu_ok[q], i + 1)
                    mean_of(q, LN_LOCAL, hl)
                var_of(LN_LOCAL)
                for q in TWO:
                    mean_of(q, LN_GLOBAL, ha)
                for q in TWO:
                    pe.wait_ge(q_ok[q], 2 * i + 2)
                    for k in range(H2):
                        lin(q, NUM + 2 * k, [(kv_blk[:, k, :], qp[q][:, k, :])])
                        lin(q, NUM + 2 * k + 1, [(ks_blk[:, k, :], qp[q][:, k, :])])
                var_of(LN_GLOBAL)
                for q in TWO:
                    pe.wait_ge(gain_ok[q], 5 * i + 2)
                    dense(q, GATE, [(w2["wlT"], 0), (w2["wlT"], 1), (w2["wgT"], 0), (w2["wgT"], 1)], xh(hl, q) + xh(ha, q), 2)
                for q in TWO:
                    pe.wait_ge(msg_ok[q], 2 * i + 2)
                    dense(q, WM, [(w2["Wm"], 0), (w2["Wm"], 1)], xh(msg, q), 2)
                for q in TWO:
                    pe.wait_ge(h_ok[q], i + 1)
                    dense(q, FF1, [(w_ff1, 0), (w_ff1, 1)], xh(h, q), 4)
                for q in TWO:
                    written(q, WM)
                    written(q, WM + 1)
                    mean_of(q, LN_MSG, qp)
                for q in TWO:
                    for u in (FF1 + 2, FF1 + 3):
                        written(q, u)
                    dense(q, FF2, [(w_ff2, k) for k in range(4)], xh(wide, q), 2)
                var_of(LN_MSG)
                for q in TWO:
                    for u in (FF2, FF2 + 1):
                        written(q, u)
                    mean_of(q, LN_GNN, res)
                for q in TWO:
                    pe.wait_ge(gain_ok[q], 5 * i + 3)
                    dense(q, M1, [(w_m1, k) for k in range(4)], xh(xn, q) + xh(msg, q), 4)
                var_of(LN_GNN)
                for q in TWO:
                    for u in (M1 + 2, M1 + 3):
                        written(q, u)
                    dense(q, M2, [(w_m2, k) for k in range(4)], xh(wide, q), 2)
                for q in TWO:
                    for u in (M2, M2 + 1):
                        written(q, u)
                    mean_of(q, LN_MIX, mix)
                var_of(LN_MIX)
                for q in TWO:
                    pe.wait_ge(x2_ok[q], i + 1)
                    mean_of(q, LN_ROUTER, x)
                var_of(LN_ROUTER)
                for q in TWO:
                    pe.wait_ge(norm_ok[q], LNS * i + LN_ROUTER + 1)
                    mean_of(q, LN_EXPERT, ha)
                var_of(LN_EXPERT)
                for q in TWO:
                    pe.wait_ge(mean_read[q], MEAN_USES * i + 1 + LNS)
                    for j in range(TILES):
                        for k in range(H2):
                            last = nc.tensor.matmul(mean_ps[q][0:TT, j * EXPERTS:(j + 1) * EXPERTS], ha[q][:, k, j * TT:(j + 1) * TT],
                                                    w_r[:, k, :], start=(k == 0), stop=(k == 1))
                    last.then_inc(mean_full[q], 1)
                for q in TWO:
                    pe.wait_ge(norm_ok[q], LNS * i + LNS)
                    for j in range(TILES):
                        for n, src in enumerate((x, hl)):
                            pe.wait_ge(lin_read[q][n], BANK_USES * i + 1 + LIN_USES // 2 + j)
                            for k in range(H2):
                                last = nc.tensor.transpose(lin_ps[q][n][0:TT, k * P:(k + 1) * P], src[q][:, k, j * TT:(j + 1) * TT], ident[:])
                            last.then_inc(lin_full[q][n], 1)

        def full(eng, q, u, i):
            eng.wait_ge(lin_full[q][u % 2], BANK_USES * i + u // 2 + 2)

        @block.scalar
        def _(act):
            act.wait_ge(consts, 2)
            act.wait_ge(w_ok, 256)
            with act.Fori(0, pairs) as i:
                TWO = range(2)

                def square(n):
                    for q in TWO:
                        act.wait_ge(mean_read[q], MEAN_USES * i + n + 2)
                        act.wait_ge(var_full[q], VAR_USES * i + 1 + n)
                        nc.scalar.activation(sq[q][:], cent[q][:], ACT.Square).then_inc(sq_ok[q], 1)

                def root(n):
                    for q in TWO:
                        act.wait_ge(var_full[q], VAR_USES * i + n + 2)
                        act.wait_ge(norm_ok[q], LNS * i + n)
                        nc.scalar.activation(std[q][:], var_ps[q][:, 0:CH], ACT.Ln, bias=eps[:]).then_inc(log_ok[q], 1)
                        act.wait_ge(log_ok[q], LNS * i + n + 1)
                        nc.scalar.activation(std[q][:], std[q][:], ACT.Exp, scale=-0.5).then_inc(var_read[q], 1)

                def affine(n, buf, gained):
                    for q in TWO:
                        act.wait_ge(norm_ok[q], LNS * i + n + 1)
                        for k in range(H2):
                            last = nc.scalar.activation(buf[q][:, k, :], buf[q][:, k, :], ACT.Identity,
                                                        scale=v(2 + 2 * gained, k), bias=v(3 + 2 * gained, k))
                        last.then_inc(gain_ok[q], 1)

                def drain(u, outs, dst, func, bias=None):
                    for q in TWO:
                        for m in range(outs):
                            full(act, q, u + m, i)
                            kw = {} if bias is None else {"bias": bias[:, m:m + 1]}
                            nc.scalar.activation(dst[q][:, m, :], lin_ps[q][(u + m) % 2][:, 0:CH], func, **kw).then_inc(
                                lin_read[q][(u + m) % 2], 1)

                for q in TWO:
                    act.wait_ge(low_ok[q], i + 1)
                    nc.scalar.activation(low[q][:], low[q][:], ACT.Exp).then_inc(exp_ok[q], 1)
                for q in TWO:
                    act.wait_ge(qlow_ok[q], 2 * i + 2)
                    nc.scalar.activation(msg[q][:], msg[q][:], ACT.Exp).then_inc(qexp_ok[q], 1)
                square(LN_LOCAL)
                root(LN_LOCAL)
                affine(LN_LOCAL, hl, 0)
                square(LN_GLOBAL)
                root(LN_GLOBAL)
                affine(LN_GLOBAL, ha, 1)
                drain(GATE, 2, gate, ACT.Sigmoid)
                drain(WM, 2, qp, ACT.Copy)
                drain(FF1, 4, wide, ACT.Relu, b_ff1)
                square(LN_MSG)
                root(LN_MSG)
                affine(LN_MSG, msg, 2)
                square(LN_GNN)
                for q in TWO:
                    full(act, q, FF2 + 1, i)
                drain(M1, 4, wide, ACT.Relu)
                root(LN_GNN)
                affine(LN_GNN, res, 3)
                drain(M2, 2, mix, ACT.Copy)
                square(LN_MIX)
                root(LN_MIX)
                affine(LN_MIX, mix, 4)
                square(LN_ROUTER)
                root(LN_ROUTER)
                square(LN_EXPERT)
                root(LN_EXPERT)
                for q in TWO:
                    for j in range(TILES):
                        act.wait_ge(lin_full[q][1], BANK_USES * i + 1 + LIN_USES // 2 + j + 1)
                        nc.scalar.activation(yrow[q][:, j, :], lin_ps[q][1][0:TT, 0:D], ACT.Copy).then_inc(lin_read[q][1], 1)

        @block.vector
        def _(dve):
            dve.wait_ge(w_ok, 256)
            for k in range(H2):
                nc.vector.tensor_tensor(kv_blk[:, k, :], kv[:, k, 0:P], same[:], ALU.mult).then_inc(blk_ok, 1)
                nc.vector.tensor_scalar(ks_blk[:, k, :], same[:], kv[:, k, P:KROW], None, ALU.mult).then_inc(blk_ok, 1)
            with dve.Fori(0, pairs) as i:
                TWO = range(2)

                def centre(n, src):
                    for q in TWO:
                        dve.wait_ge(mean_full[q], MEAN_USES * i + n + 2)
                        dve.wait_ge(norm_ok[q], LNS * i + n)
                        nc.vector.tensor_tensor(cent[q][:], src[q][:], over_halves(mean_ps[q][:, 0:CH]), ALU.subtract).then_inc(mean_read[q], 1)

                def norm(n, dst):
                    for q in TWO:
                        dve.wait_ge(var_read[q], VAR_USES * i + n + 2)
                        nc.vector.tensor_tensor(dst[q][:], cent[q][:], over_halves(std[q][:]), ALU.mult).then_inc(norm_ok[q], 1)

                for q in TWO:
                    dve.wait_ge(y_in[q], 64 * i)
                    nc.vector.tensor_copy(y_at[q][:], rank[:, bass.ds((i * 2 + q) * TILES, TILES)]).then_inc(y_at_ok[q], 1)
                for q in TWO:
                    dve.wait_ge(rows_in[q], 48 * (i + 1))
                    for k, (bank, ready, uses, read) in enumerate(((mean_ps, mean_full, MEAN_USES, mean_read),
                                                                   (var_ps, var_full, VAR_USES, var_read))):
                        dve.wait_ge(ready[q], uses * i + 1)
                        nc.vector.scalar_tensor_tensor(up[q][:, k, :], bank[q][:, 0:CH], v(0, k), xn[q][:, k, :],
                                                       ALU.add, ALU.add).then_inc(read[q], 1)
                for q in TWO:
                    dve.wait_ge(mean_read[q], MEAN_USES * i + 1)
                    dve.wait_ge(var_read[q], VAR_USES * i + 1)
                    nc.vector.tensor_scalar(low[q][:], up[q][:], 0.0, None, ALU.min).then_inc(low_ok[q], 1)
                    dve.wait_ge(low_ok[q], i + 1)
                    nc.vector.tensor_scalar(up[q][:], up[q][:], 0.0, -1.0, ALU.max, ALU.add).then_inc(up_ok[q], 1)
                for q in TWO:
                    for k in range(H2):
                        dve.wait_ge(lin_full[q][k], BANK_USES * i + 1)
                        nc.vector.tensor_tensor(ha[q][:, k, :], lin_ps[q][k][:, 0:CH], xn[q][:, k, :], ALU.add).then_inc(lin_read[q][k], 1)
                for q in TWO:
                    for k in range(H2):
                        full(dve, q, Q_ + k, i)
                        nc.vector.tensor_scalar(msg[q][:, k, :], lin_ps[q][k][:, 0:CH], 0.0, None, ALU.min).then_inc(qlow_ok[q], 1)
                for q in TWO:
                    dve.wait_ge(up_ok[q], i + 1)
                    dve.wait_ge(exp_ok[q], i + 1)
                    nc.vector.tensor_tensor(hl[q][:], up[q][:], low[q][:], ALU.add).then_inc(elu_ok[q], 1)
                for q in TWO:
                    dve.wait_ge(qexp_ok[q], i + 1)
                    for k in range(H2):
                        nc.vector.scalar_tensor_tensor(qp[q][:, k, :], lin_ps[q][k][:, 0:CH], 0.0, msg[q][:, k, :],
                                                       ALU.max, ALU.add).then_inc(lin_read[q][k], 1)
                    for k in range(H2):
                        dve.wait_ge(lin_read[q][k], BANK_USES * i + 2)
                    nc.vector.sem_inc(q_ok[q], 2)
                centre(LN_LOCAL, hl)
                norm(LN_LOCAL, hl)
                centre(LN_GLOBAL, ha)
                for q in TWO:
                    for k in range(H2):
                        full(dve, q, NUM + 2 * k + 1, i)
                        nc.vector.tensor_scalar(den[q][:], lin_ps[q][1][:, 0:CH], ATT_EPS, None, ALU.add).then_inc(lin_read[q][1], 1)
                        dve.wait_ge(lin_read[q][1], BANK_USES * i + 3 + k)
                        nc.vector.reciprocal(den[q][:], den[q][:]).then_inc(den_ok[q], 1)
                        dve.wait_ge(den_ok[q], 2 * i + k + 1)
                        full(dve, q, NUM + 2 * k, i)
                        nc.vector.tensor_tensor(msg[q][:, k, :], lin_ps[q][0][:, 0:CH], den[q][:], ALU.mult).then_inc(lin_read[q][0], 1)
                        dve.wait_ge(lin_read[q][0], BANK_USES * i + 3 + k)
                    nc.vector.sem_inc(msg_ok[q], 2)
                norm(LN_GLOBAL, ha)
                for q in TWO:
                    dve.wait_ge(gain_ok[q], 5 * i + 2)
                    nc.vector.tensor_tensor(low[q][:], hl[q][:], ha[q][:], ALU.subtract).then_inc(diff_ok[q], 1)
                    for k in range(H2):
                        dve.wait_ge(lin_read[q][k], BANK_USES * i + GATE // 2 + 2)
                    dve.wait_ge(diff_ok[q], i + 1)
                    nc.vector.tensor_tensor(gate[q][:], gate[q][:], low[q][:], ALU.mult).then_inc(gated_ok[q], 1)
                    dve.wait_ge(gated_ok[q], i + 1)
                    nc.vector.tensor_tensor(h[q][:], gate[q][:], ha[q][:], ALU.add).then_inc(h_ok[q], 1)
                centre(LN_MSG, qp)
                for q in TWO:
                    for k in range(H2):
                        full(dve, q, FF2 + k, i)
                        nc.vector.scalar_tensor_tensor(res[q][:, k, :], lin_ps[q][k][:, 0:CH], v(1, k), h[q][:, k, :],
                                                       ALU.add, ALU.add).then_inc(lin_read[q][k], 1)
                norm(LN_MSG, msg)
                centre(LN_GNN, res)
                norm(LN_GNN, res)
                for q in TWO:
                    dve.wait_ge(rows_in[q], 48 * (i + 1))
                    nc.vector.tensor_tensor(x[q][:], x[q][:], xn[q][:], ALU.add).then_inc(sum1_ok[q], 1)
                    dve.wait_ge(gain_ok[q], 5 * i + 4)
                    dve.wait_ge(sum1_ok[q], i + 1)
                    nc.vector.tensor_tensor(x[q][:], x[q][:], res[q][:], ALU.add).then_inc(sum2_ok[q], 1)
                centre(LN_MIX, mix)
                norm(LN_MIX, mix)
                for q in TWO:
                    dve.wait_ge(gain_ok[q], 5 * i + 5)
                    dve.wait_ge(sum2_ok[q], i + 1)
                    nc.vector.tensor_tensor(x[q][:], x[q][:], mix[q][:], ALU.add).then_inc(x2_ok[q], 1)
                centre(LN_ROUTER, x)
                norm(LN_ROUTER, ha)
                centre(LN_EXPERT, ha)
                norm(LN_EXPERT, hl)
                for q in TWO:
                    dve.wait_ge(mean_full[q], MEAN_USES * (i + 1))
                    nc.vector.tensor_tensor(logit[q][:], mean_ps[q][0:TT, 0:TILES * EXPERTS].rearrange("p (j e) -> p j e", j=TILES),
                                            b_r[:].unsqueeze(1).to_broadcast([TT, TILES, EXPERTS]), ALU.add).then_inc(mean_read[q], 1)
                for q in TWO:
                    for j in range(TILES):
                        dve.wait_ge(lin_full[q][0], BANK_USES * i + 1 + LIN_USES // 2 + j + 1)
                        nc.vector.tensor_copy(arow[q][:, j, :], lin_ps[q][0][0:TT, 0:D]).then_inc(lin_read[q][0], 1)


TOP = 2
XSLOTS = -(-((N * TOP + EXPERTS * (P - 1)) // P) // 2) * 2
FAR = 1e6


def stage_route(nc, a, t):
    with ExitStack() as ctx:
        shape = [TT, NTT, EXPERTS]
        logit, rest, mark, hot1, hot2, both, inner, upto, pos = (
            sb(nc, ctx, f"o_{n}", shape) for n in "logit rest mark hot1 hot2 both inner upto pos".split())
        valid, first, second, m1, m2, diff, w1, w2, invalid, p1, p2 = (
            sb(nc, ctx, f"o_{n}", [TT, NTT]) for n in "valid first second m1 m2 diff w1 w2 invalid p1 p2".split())
        below = sb(nc, ctx, "o_below", [P, P])
        ones = sb(nc, ctx, "o_ones", [TT, NTT * EXPERTS])
        order = sb(nc, ctx, "o_order", [TT, EXPERTS])
        tiles_i = sb(nc, ctx, "o_tiles_i", [TT, EXPERTS], I32)
        tiles, ends, base = (sb(nc, ctx, f"o_{n}", [TT, EXPERTS]) for n in ("tiles", "ends", "base"))
        slot = sb(nc, ctx, "o_slot", [1, XSLOTS])
        slot_e = sb(nc, ctx, "o_slot_e", [1, XSLOTS])
        slot_i = sb(nc, ctx, "o_slot_i", [1, XSLOTS], I32)
        send = [sb(nc, ctx, f"o_send{c}", [TT, NTT], I32) for c in range(TOP)]
        fetch = [sb(nc, ctx, f"o_fetch{c}", [TT, NTT], I32) for c in range(TOP)]
        to = [sb(nc, ctx, f"o_to{q}", [TT, TOP, TILES], I32) for q in range(2)]
        rows = [sb(nc, ctx, f"o_rows{q}", [TT, TILES, D]) for q in range(2)]
        zeros = sb(nc, ctx, "o_zeros", [P, D])
        inner_ps = ps(nc, ctx, "o_inner_ps", [P, 512])
        total_ps = ps(nc, ctx, "o_total_ps", [P, 512])
        token = sb(nc, ctx, "o_token", [P, 2])
        settled, loaded, consts, token_ok, step_ok, counted, emptied, exp_ok, saved = sems(
            nc, ctx, "o", "settled loaded consts token_ok step_ok counted emptied exp_ok saved")
        rows_in, to_ok, sent = (sems(nc, ctx, "o", f"{n}0 {n}1") for n in "rows_in to_ok sent".split())
        pairs = NCH // 2
        XSTEPS = 17
        block = ctx.enter_context(nc.Block())

        def each(ap):
            return ap.unsqueeze(2).to_broadcast(shape)

        @block.sync
        def _(sp):
            for dst, source in ((logit[:], t["logit"].rearrange("(i p) e -> p i e", p=TT)), (valid[:], a["valid"]), (below[:], a["below"])):
                sp.dma_start(dst, source).then_inc(loaded, 16)
            sp.wait_ge(consts, 4)
            sp.dma_start(t["xd"].rearrange("(s p) f -> p s f", p=P), zeros[:].unsqueeze(1).to_broadcast([P, XSLOTS, D])).then_inc(emptied, 16)
            with sp.Fori(0, pairs) as i:
                for q in range(2):
                    sp.wait_ge(sent[q], 16 * TOP * TILES * i)
                    sp.dma_start(rows[q][:], t["xe"][bass.ds((i * 2 + q) * CH, CH), :].rearrange("(j p) f -> p j f", p=TT)).then_inc(rows_in[q], 16)
            sp.wait_ge(counted, 2)
            for dst, source in ((t["fetch0"], fetch[0]), (t["fetch1"], fetch[1]), (t["w1"], w1), (t["w2"], w2), (t["slot_e"], slot_i)):
                sp.dma_start(dst, source[:]).then_inc(saved, 16)
            sp.wait_ge(saved, 80)
            for q in range(2):
                sp.wait_ge(sent[q], 16 * TOP * TILES * pairs)

        @block.gpsimd
        def _(pool):
            nc.gpsimd.iota(order[:], [[-1, EXPERTS]], base=EXPERTS, channel_multiplier=0, allow_small_or_imprecise_dtypes=True).then_inc(consts, 1)
            nc.gpsimd.iota(slot[:], [[1, XSLOTS]], base=0, channel_multiplier=0, allow_small_or_imprecise_dtypes=True).then_inc(consts, 1)
            nc.gpsimd.memset(ones[:], 1.0).then_inc(consts, 1)
            nc.gpsimd.memset(zeros[:], 0.0).then_inc(consts, 1)
            nc.gpsimd.memset(token[:], 0.0).then_inc(token_ok, 1)
            pool.wait_ge(token_ok, 1)
            pool.wait_ge(emptied, 16)
            with pool.Fori(0, pairs) as i:
                for q in range(2):
                    pool.wait_ge(rows_in[q], 16 * (i + 1))
                    pool.wait_ge(to_ok[q], TOP * (i + 1))
                    settle(nc, pool, token, settled, 2 * i + q)
                    for c in range(TOP):
                        for j in range(TILES):
                            nc.gpsimd.indirect_dma_start(
                                out=t["xd"], out_offset=bass.IndirectOffsetOnAxis(ap=to[q][:, c, j:j + 1], axis=0),
                                in_=rows[q][:, j, :], in_offset=None, bounds_check=XSLOTS * P - 1, oob_is_err=False).then_inc(sent[q], 16)

        @block.tensor
        def _(pe):
            pe.wait_ge(loaded, 48)
            pe.wait_ge(counted, 1)
            flat = both[:].rearrange("p i e -> p (i e)")
            nc.tensor.matmul(inner_ps[0:TT, 0:NTT * EXPERTS], below[0:TT, 0:TT], flat, start=True, stop=True)
            nc.tensor.matmul(total_ps[0:TT, 0:NTT * EXPERTS], ones[:, 0:TT], flat, start=True, stop=True).then_inc(exp_ok, 1)

        @block.scalar
        def _(act):
            act.wait_ge(step_ok, XSTEPS)
            nc.scalar.activation(w2[:], diff[:], ACT.Exp).then_inc(exp_ok, 1)

        @block.vector
        def _(dve):
            n = [0]

            def go(ins):
                n[0] += 1
                ins.then_inc(step_ok, 1)
                dve.wait_ge(step_ok, n[0])

            V = nc.vector
            dve.wait_ge(loaded, 48)
            dve.wait_ge(consts, 4)
            rank_of = order[:].unsqueeze(1).to_broadcast(shape)
            for l, m, f, hot in ((logit, m1, first, hot1), (rest, m2, second, hot2)):
                go(V.tensor_reduce(m[:], l[:], AX.X, ALU.max))
                go(V.tensor_tensor(mark[:], l[:], each(m[:]), ALU.is_equal))
                go(V.tensor_tensor(mark[:], mark[:], rank_of, ALU.mult))
                go(V.tensor_reduce(f[:], mark[:], AX.X, ALU.max))
                go(V.tensor_tensor(hot[:], each(f[:]), rank_of, ALU.is_equal))
                if hot is hot1:
                    go(V.scalar_tensor_tensor(rest[:].rearrange("p i e -> p (i e)"), hot1[:].rearrange("p i e -> p (i e)"), -BIG,
                                              logit[:].rearrange("p i e -> p (i e)"), ALU.mult, ALU.add))
            go(V.tensor_tensor(both[:], hot1[:], hot2[:], ALU.add))
            both_done = V.tensor_tensor(both[:], both[:], each(valid[:]), ALU.mult)
            both_done.then_inc(counted, 1)
            go(V.tensor_tensor(diff[:], m2[:], m1[:], ALU.subtract))
            go(V.tensor_scalar(invalid[:], valid[:], -FAR, FAR, ALU.mult, ALU.add))
            for _ in range(3):
                go(V.tensor_copy(tiles_i[:], order[:]))
            dve.wait_ge(exp_ok, 2)
            go(V.tensor_scalar(diff[:], w2[:], 1.0, None, ALU.add))
            go(V.reciprocal(w1[:], diff[:]))
            go(V.tensor_tensor(w2[:], w2[:], w1[:], ALU.mult))
            flat = "p i e -> p (i e)"
            go(V.tensor_copy(inner[:].rearrange(flat), inner_ps[0:TT, 0:NTT * EXPERTS]))
            go(V.tensor_copy(mark[:].rearrange(flat), total_ps[0:TT, 0:NTT * EXPERTS]))
            for e in range(EXPERTS):
                go(V.tensor_tensor_scan(upto[:, :, e], ones[:, 0:NTT], mark[:, :, e], 0.0, ALU.mult, ALU.add))
            go(V.tensor_scalar(tiles_i[:], upto[:, NTT - 1, :], float(P - 1), None, ALU.add))
            go(V.tensor_single_scalar(tiles_i[:], tiles_i[:], 7, op=ALU.logical_shift_right))
            go(V.tensor_copy(tiles[:], tiles_i[:]))
            go(V.tensor_tensor_scan(ends[:], ones[:, 0:EXPERTS], tiles[:], 0.0, ALU.mult, ALU.add))
            go(V.tensor_tensor(base[:], ends[:], tiles[:], ALU.subtract))
            go(V.tensor_scalar(base[:], base[:], float(P), None, ALU.mult))
            go(V.tensor_tensor(pos[:], upto[:], mark[:], ALU.subtract))
            go(V.tensor_tensor(pos[:], pos[:], inner[:], ALU.add))
            go(V.tensor_tensor(pos[:], pos[:], base[:].unsqueeze(1).to_broadcast(shape), ALU.add))
            for hot, pp, c in ((hot1, p1, 0), (hot2, p2, 1)):
                go(V.tensor_tensor(mark[:], hot[:], pos[:], ALU.mult))
                go(V.tensor_reduce(pp[:], mark[:], AX.X, ALU.add))
                go(V.tensor_tensor(send[c][:], pp[:], invalid[:], ALU.add))
                go(V.tensor_tensor(fetch[c][:], pp[:], valid[:], ALU.mult))
            go(V.tensor_scalar(slot_e[:], slot[:], ends[0:1, 0:1], None, ALU.is_ge))
            for e in range(1, EXPERTS):
                go(V.scalar_tensor_tensor(slot_e[:], slot[:], ends[0:1, e:e + 1], slot_e[:], ALU.is_ge, ALU.add))
            V.tensor_scalar(slot_i[:], slot_e[:], float(EXPERTS - 1), None, ALU.min).then_inc(counted, 1)
            with dve.Fori(0, pairs) as i:
                for q in range(2):
                    dve.wait_ge(sent[q], 16 * TOP * TILES * i)
                    for c in range(TOP):
                        nc.vector.tensor_copy(to[q][:, c, :], send[c][:, bass.ds((i * 2 + q) * TILES, TILES)]).then_inc(to_ok[q], 1)


HID = 1024
HC = HID // P


def stage_experts(nc, a, t):
    with ExitStack() as ctx:
        ident = sb(nc, ctx, "e_ident", [P, P])
        w1 = sb(nc, ctx, "e_w1", [P, EXPERTS, H2 * HID])
        w2 = sb(nc, ctx, "e_w2", [P, EXPERTS, HC * D])
        b1 = sb(nc, ctx, "e_b1", [P, EXPERTS, HID])
        b2 = sb(nc, ctx, "e_b2", [P, EXPERTS, D])
        ln = sb(nc, ctx, "e_ln", [P, EXPERTS, 2 * H2])
        slot_e = sb(nc, ctx, "e_slot_e", [1, XSLOTS], I32)
        rows = [sb(nc, ctx, f"e_rows{q}", [P, D]) for q in range(2)]
        xT = [sb(nc, ctx, f"e_xT{q}", [P, H2, P]) for q in range(2)]
        h = [sb(nc, ctx, f"e_h{q}", [P, HID]) for q in range(2)]
        hT = [sb(nc, ctx, f"e_hT{q}", [P, HC, P]) for q in range(2)]
        y = [sb(nc, ctx, f"e_y{q}", [P, D]) for q in range(2)]
        x_ps = ps(nc, ctx, "e_x_ps", [P, 512])
        h_ps = ps(nc, ctx, "e_h_ps", [P, 4, 512])
        hT_ps = ps(nc, ctx, "e_hT_ps", [P, 2, 512])
        y_ps = ps(nc, ctx, "e_y_ps", [P, 512])
        w_ok, x_mm, x_ok, hT_mm, hT_ok, y_mm, y_ok = sems(nc, ctx, "e", "w_ok x_mm x_ok hT_mm hT_ok y_mm y_ok")
        rows_in, h_mm, biased, gelu_ok, stored = (sems(nc, ctx, "e", f"{n}0 {n}1") for n in "rows_in h_mm biased gelu_ok stored".split())
        pairs = XSLOTS // 2
        block = ctx.enter_context(nc.Block())
        LOADS = 3 + 4 * EXPERTS

        def experts(eng, i):
            return [eng.value_load(slot_e[0:1, bass.ds(i * 2 + q, 1)], min_val=0, max_val=EXPERTS - 1) for q in range(2)]

        @block.sync
        def _(sp):
            for dst, source in ((slot_e[:], t["slot_e"]), (ident[:], a["ident"]), (ln[:], a["ffn_ln"])):
                sp.dma_start(dst, source).then_inc(w_ok, 16)
            for e in range(EXPERTS):
                sp.dma_start(w1[:, e, :].rearrange("p (k n) -> p k n", k=H2), a["ffn_W1"][e].rearrange("(k p) n -> p k n", p=P)).then_inc(w_ok, 16)
                sp.dma_start(w2[:, e, :].rearrange("p (k n) -> p k n", k=HC), a["ffn_W2"][e].rearrange("(k p) n -> p k n", p=P)).then_inc(w_ok, 16)
                sp.dma_start(b1[:, e, :], a["ffn_b1"][e].unsqueeze(0).to_broadcast([P, HID])).then_inc(w_ok, 16)
                sp.dma_start(b2[:, e, :], a["ffn_b2"][e].unsqueeze(0).to_broadcast([P, D])).then_inc(w_ok, 16)
            with sp.Fori(0, pairs) as i:
                for q in range(2):
                    sp.wait_ge(x_mm, 2 * i + q)
                    sp.dma_start(rows[q][:], t["xd"][bass.ds((i * 2 + q) * P, P), :]).then_inc(rows_in[q], 16)
                for q in range(2):
                    sp.wait_ge(y_ok, 2 * i + q + 1)
                    sp.dma_start(t["yd"][bass.ds((i * 2 + q) * P, P), :], y[q][:]).then_inc(stored[q], 16)
            for q in range(2):
                sp.wait_ge(stored[q], 16 * pairs)

        @block.tensor
        def _(pe):
            pe.wait_ge(w_ok, 16 * LOADS)
            with pe.Fori(0, pairs) as i:
                ex = experts(pe, i)
                for q in range(2):
                    pe.wait_ge(rows_in[q], 16 * (i + 1))
                    pe.wait_ge(x_ok, 4 * i + 2 * q)
                    for k in range(H2):
                        last = nc.tensor.transpose(x_ps[:, k * P:(k + 1) * P], rows[q][:, k * P:(k + 1) * P], ident[:])
                    last.then_inc(x_mm, 1)
                    pe.wait_ge(x_ok, 4 * i + 2 * q + 2)
                    for n in range(2):
                        pe.wait_ge(biased[q], 2 * i + n)
                        for k in range(H2):
                            last = nc.tensor.matmul(h_ps[:, 2 * q + n, :], xT[q][:, k, :],
                                                    w1[:, bass.ds(ex[q], 1), k * HID + n * 512:k * HID + (n + 1) * 512].rearrange("p e n -> p (e n)"),
                                                    start=(k == 0), stop=(k == H2 - 1))
                        last.then_inc(h_mm[q], 1)
                for q in range(2):
                    for n in range(2):
                        pe.wait_ge(gelu_ok[q], 2 * i + n + 1)
                        pe.wait_ge(hT_ok, 4 * i + 2 * q + n - (1 if n or q else 0))
                        for c in range(4):
                            cc = n * 4 + c
                            last = nc.tensor.transpose(hT_ps[:, n, c * P:(c + 1) * P], h[q][:, cc * P:(cc + 1) * P], ident[:])
                        last.then_inc(hT_mm, 1)
                for q in range(2):
                    pe.wait_ge(hT_ok, 4 * i + 2 * q + 2)
                    pe.wait_ge(y_ok, 2 * i + q)
                    for c in range(HC):
                        last = nc.tensor.matmul(y_ps[:, 0:D], hT[q][:, c, :],
                                                w2[:, bass.ds(ex[q], 1), c * D:(c + 1) * D].rearrange("p e n -> p (e n)"),
                                                start=(c == 0), stop=(c == HC - 1))
                    last.then_inc(y_mm, 1)

        @block.scalar
        def _(act):
            act.wait_ge(w_ok, 16 * LOADS)
            with act.Fori(0, pairs) as i:
                for q in range(2):
                    for n in range(2):
                        act.wait_ge(biased[q], 2 * i + n + 1)
                        half = h[q][:, n * 512:(n + 1) * 512]
                        nc.scalar.activation(half, half, ACT.Gelu).then_inc(gelu_ok[q], 1)
                for q in range(2):
                    for n in range(2):
                        act.wait_ge(hT_mm, 4 * i + 2 * q + n + 1)
                        act.wait_ge(y_mm, 2 * i + q - (1 if q else 0))
                        nc.scalar.activation(hT[q][:, 4 * n:4 * n + 4, :].rearrange("p c n -> p (c n)"), hT_ps[:, n, :], ACT.Copy).then_inc(hT_ok, 1)

        @block.vector
        def _(dve):
            dve.wait_ge(w_ok, 16 * LOADS)
            with dve.Fori(0, pairs) as i:
                ex = experts(dve, i)
                for q in range(2):
                    dve.wait_ge(x_mm, 2 * i + q + 1)
                    dve.wait_ge(h_mm[q], 2 * i)
                    for k in range(H2):
                        nc.vector.tensor_scalar(xT[q][:, k, :], x_ps[:, k * P:(k + 1) * P],
                                                ln[:, bass.ds(ex[q], 1), k:k + 1].rearrange("p e n -> p (e n)"),
                                                ln[:, bass.ds(ex[q], 1), H2 + k:H2 + k + 1].rearrange("p e n -> p (e n)"),
                                                ALU.mult, ALU.add).then_inc(x_ok, 1)
                    for n in range(2):
                        dve.wait_ge(h_mm[q], 2 * i + n + 1)
                        dve.wait_ge(hT_mm, 4 * i)
                        nc.vector.tensor_tensor(h[q][:, n * 512:(n + 1) * 512], h_ps[:, 2 * q + n, :],
                                                b1[:, bass.ds(ex[q], 1), n * 512:(n + 1) * 512].rearrange("p e n -> p (e n)"),
                                                ALU.add).then_inc(biased[q], 1)
                for q in range(2):
                    dve.wait_ge(y_mm, 2 * i + q + 1)
                    dve.wait_ge(stored[q], 16 * i)
                    nc.vector.tensor_tensor(y[q][:], y_ps[:, 0:D], b2[:, bass.ds(ex[q], 1), :].rearrange("p e n -> p (e n)"), ALU.add).then_inc(y_ok, 1)


def stage_combine(nc, a, t):
    with ExitStack() as ctx:
        fetch = [sb(nc, ctx, f"c_fetch{c}", [TT, NTT], I32) for c in range(TOP)]
        w = [sb(nc, ctx, f"c_w{c}", [TT, NTT]) for c in range(TOP)]
        at = [sb(nc, ctx, f"c_at{q}", [TT, TOP, TILES], I32) for q in range(2)]
        got = [sb(nc, ctx, f"c_got{q}", [TT, TOP, TILES, D]) for q in range(2)]
        acc = [sb(nc, ctx, f"c_acc{q}", [TT, TILES, D]) for q in range(2)]
        token = sb(nc, ctx, "c_token", [P, 2])
        settled, loaded, token_ok = sems(nc, ctx, "c", "settled loaded token_ok")
        x_in, at_ok, got_in, half_ok, sum_ok, stored = (sems(nc, ctx, "c", f"{n}0 {n}1") for n in "x_in at_ok got_in half_ok sum_ok stored".split())
        pairs = NCH // 2
        block = ctx.enter_context(nc.Block())

        @block.sync
        def _(sp):
            for dst, source in ((fetch[0], "fetch0"), (fetch[1], "fetch1"), (w[0], "w1"), (w[1], "w2")):
                sp.dma_start(dst[:], t[source]).then_inc(loaded, 16)
            with sp.Fori(0, pairs) as i:
                for q in range(2):
                    sp.wait_ge(stored[q], 16 * i)
                    sp.dma_start(acc[q][:], t["x2"][bass.ds((i * 2 + q) * CH, CH), :].rearrange("(j p) f -> p j f", p=TT)).then_inc(x_in[q], 16)
                for q in range(2):
                    sp.wait_ge(sum_ok[q], TILES * (i + 1))
                    sp.dma_start(t["out"][bass.ds((i * 2 + q) * CH, CH), :].rearrange("(j p) f -> p j f", p=TT), acc[q][:]).then_inc(stored[q], 16)
            for q in range(2):
                sp.wait_ge(stored[q], 16 * pairs)

        @block.gpsimd
        def _(pool):
            nc.gpsimd.memset(token[:], 0.0).then_inc(token_ok, 1)
            pool.wait_ge(token_ok, 1)
            with pool.Fori(0, pairs) as i:
                for q in range(2):
                    pool.wait_ge(at_ok[q], TOP * (i + 1))
                    pool.wait_ge(sum_ok[q], TILES * i)
                    settle(nc, pool, token, settled, 2 * i + q)
                    for c in range(TOP):
                        for j in range(TILES):
                            nc.gpsimd.indirect_dma_start(
                                out=got[q][:, c, j, :], out_offset=None, in_=t["yd"],
                                in_offset=bass.IndirectOffsetOnAxis(ap=at[q][:, c, j:j + 1], axis=0)).then_inc(got_in[q], 16)

        @block.vector
        def _(dve):
            dve.wait_ge(loaded, 64)

            def where(i, q):
                for c in range(TOP):
                    nc.vector.tensor_copy(at[q][:, c, :], fetch[c][:, bass.ds((i * 2 + q) * TILES, TILES)]).then_inc(at_ok[q], 1)

            with dve.Fori(0, pairs) as i:
                for q in range(2):
                    dve.wait_ge(got_in[q], 16 * TOP * TILES * i)
                    where(i, q)
                for q in range(2):
                    dve.wait_ge(x_in[q], 16 * (i + 1))
                    dve.wait_ge(got_in[q], 16 * TOP * TILES * (i + 1))
                    for j in range(TILES):
                        nc.vector.scalar_tensor_tensor(acc[q][:, j, :], got[q][:, 0, j, :], w[0][:, bass.ds((i * 2 + q) * TILES + j, 1)],
                                                       acc[q][:, j, :], ALU.mult, ALU.add).then_inc(half_ok[q], 1)
                    for j in range(TILES):
                        dve.wait_ge(half_ok[q], TILES * i + j + 1)
                        nc.vector.scalar_tensor_tensor(acc[q][:, j, :], got[q][:, 1, j, :], w[1][:, bass.ds((i * 2 + q) * TILES + j, 1)],
                                                       acc[q][:, j, :], ALU.mult, ALU.add).then_inc(sum_ok[q], 1)


SCRATCH = {
    "xd": (XSLOTS * P, D), "yd": (XSLOTS * P, D), "fetch0": ((TT, NTT), I32), "fetch1": ((TT, NTT), I32),
    "w1": (TT, NTT), "w2": (TT, NTT), "slot_e": ((1, XSLOTS), I32),
    "logit": (NP, EXPERTS), "x2": (NP, D), "xe": (NP, D),
    "agg": (NP, D),
    "y": (NP, D),
    "v": (NP,), "rank": ((NP,), I32), "xs": (NP, D),
    "xnT": (D, NP), "xn": (NP, D), "table": (NP, ROW), "kv": (P, H2, KROW),
}


def build(nc, a, out):
    t = {n: nc.dram_tensor(f"t_{n}", list(s if not isinstance(s[0], tuple) else s[0]),
                           F32 if not isinstance(s[0], tuple) else s[1], kind="Internal").ap()
         for n, s in SCRATCH.items()}
    t["out"] = out
    stages = [stage_project, stage_rank, stage_mamba, stage_attend, stage_mix, stage_route,
              stage_experts, stage_combine]
    for n, stage in enumerate(stages):
        if n < STOP_AFTER and n not in SKIP:
            held = nc.snapshot_sems()
            stage(nc, a, t)
            nc.clear_and_free_semaphores(nc.allocated_since(held))
            nc.all_engine_barrier()


def kernel(**inputs):
    import numpy as np
    import concourse.bacc as bacc
    from concourse.bass_utils import run_bass_kernel_spmd

    g = {k[len("L0_gnn_"):]: np.asarray(v) for k, v in inputs.items() if k.startswith("L0_gnn_")}
    m = {k[len("L0_mix_"):]: np.asarray(v) for k, v in inputs.items() if k.startswith("L0_mix_")}
    f = {k[len("L0_ffn_"):]: np.asarray(v) for k, v in inputs.items() if k.startswith("L0_ffn_")}
    x = np.asarray(inputs["x"])
    feed = {}
    feed["xT"] = np.zeros((D, NP), np.float32)
    feed["xT"][:, :N] = x.T
    feed["gat_w"] = g["gat_w"]
    feed["gat_wT"] = g["gat_w"].T
    blk = np.zeros((D, 2 * HEADS), np.float32)
    for h in range(HEADS):
        blk[h * FO:(h + 1) * FO, h] = g["gat_a_src"][h]
        blk[h * FO:(h + 1) * FO, HEADS + h] = g["gat_a_tgt"][h]
    feed["a_blk"] = blk
    feed["Wk"], feed["Wv"] = m["Wk"], m["Wv"]
    feed["valid"] = (np.arange(NP) < N).astype(np.float32).reshape(NTT, TT).T
    feed["src"] = np.asarray(inputs["src"]).reshape(EP, EC)
    noise = np.full(NP, 3e38, np.float32)
    noise[:N] = np.asarray(inputs["node_vec"])
    feed["noise"] = noise.reshape(NT, P).T
    feed["in_projT"], feed["x_projT"], feed["out_projT"] = g["in_proj_w"].T, g["x_proj_w"].T, g["out_proj_w"].T
    feed["dt_projT"] = np.zeros((DBC, D), np.float32)
    feed["dt_projT"][:STATES] = g["dt_proj_w"].T
    feed["pick"] = np.repeat(np.eye(DBC, dtype=np.float32)[:, STATES:, None], P, axis=2)
    feed["mamba_vecs"] = np.concatenate([g["conv_w"], g["conv_b"][:, None], g["dt_proj_b"][:, None], g["D_param"][:, None]], 1)
    feed["A_log"] = g["A_log"]
    feed["dst"] = np.asarray(inputs["dst"]).reshape(EP, EC)
    edges = np.zeros((E + P, 2), np.int32)
    edges[:, 1] = 1 << 20
    edges[:E, 0], edges[:E, 1] = np.asarray(inputs["src"]), np.asarray(inputs["dst"])
    feed["edges"] = edges
    feed["below"] = np.triu(np.ones((P, P), np.float32), 1)
    feed["wlT"], feed["wgT"], feed["ff1T"], feed["ff2T"] = g["wl"].T, g["wg"].T, g["ff1_w"].T, g["ff2_w"].T
    for n in ("Wq", "Wm", "W1", "W2"):
        feed[n] = m[n]
    feed["ff1_b"], feed["Wr"], feed["br"] = g["ff1_b"].reshape(4, P).T, f["Wr"], f["br"]
    feed["mix_vecs"] = np.stack([g["gat_b"], g["ff2_b"], g["ln_local_g"], g["ln_local_b"], g["ln_global_g"], g["ln_global_b"],
                                 m["g1"], m["b1"], g["ln2_g"], g["ln2_b"], m["g2"], m["b2"]], 1)
    feed["same"] = np.kron(np.eye(4, dtype=np.float32), np.ones((32, 32), np.float32))
    feed["ffn_ln"] = np.concatenate([f["ln_g"].reshape(EXPERTS, H2, P), f["ln_b"].reshape(EXPERTS, H2, P)], 1).transpose(2, 0, 1)
    for n in ("W1", "W2", "b1", "b2"):
        feed["ffn_" + n] = f[n]
    feed["ident"] = np.eye(P, dtype=np.float32)

    nc = bacc.Bacc("TRN2", target_bir_lowering=False, num_devices=1)
    arrays, args = {}, {}
    for name, arr in feed.items():
        arr = np.ascontiguousarray(arr)
        arrays[f"in_{name}"] = arr
        args[name] = nc.dram_tensor(f"in_{name}", arr.shape, mybir.dt.from_np(arr.dtype), kind="ExternalInput").ap()
    out = nc.dram_tensor("out_rows", (NP, D), F32, kind="ExternalOutput").ap()
    build(nc, args, out)
    r = run_bass_kernel_spmd(nc, [arrays], core_ids=[0])
    return r.results[0]["out_rows"][:N]
```

```python
from contextlib import ExitStack

import concourse.bass as bass
from concourse import mybir

F32 = mybir.dt.float32
BF16 = mybir.dt.bfloat16
I32 = mybir.dt.int32
U32 = mybir.dt.uint32
ALU = mybir.AluOpType
ACT = mybir.ActivationFunctionType
AX = mybir.AxisListType

P = 128
N = 6250
D = 256
H2 = D // P
NT = -(-N // P)
NP = NT * P
TT = 112
TILES = 4
CH = TT * TILES
NCH = NP // CH
NTT = NP // TT
E = 100000
EP, EC = 125, 800
HEADS = 4
FO = D // HEADS
ROW = D + 2 * HEADS
KROW = P + 1
LN_EPS = 1e-5
START = 1


FROM_ZERO = ("moved", "sent", "got_in", "y_in")


def sb(nc, ctx, name, shape, dt=F32):
    return ctx.enter_context(nc.sbuf_tensor(name, shape, dt))


def ps(nc, ctx, name, shape, dt=F32):
    return ctx.enter_context(nc.psum_tensor(name, shape, dt))


def sems(nc, ctx, stage, names):
    made = [nc.alloc_semaphore(name=f"{stage}_{n}") for n in names.split()]
    for sem, n in zip(made, names.split()):
        if n.rstrip("0123456789") not in FROM_ZERO:
            nc.sync.sem_inc(sem, START)
    return made


def settle(nc, pool, token, settled, times):
    pool.wait_ge(settled, START + times)
    nc.gpsimd.tensor_tensor(token[:, 1:2], token[:, 0:1], token[:, 0:1], ALU.add).then_inc(settled, 1)


def halves(ap):
    return ap.rearrange("(h p) n -> p h n", p=P)


def over_halves(ap):
    return ap.unsqueeze(1).to_broadcast([P, H2, ap.shape[1]])


def stage_project(nc, a, t):
    with ExitStack() as ctx:
        inv_d = sb(nc, ctx, "p_inv_d", [P, P])
        ident = sb(nc, ctx, "p_ident", [P, P])
        w_gat = sb(nc, ctx, "p_w_gat", [P, H2, ROW])
        w_gat_o = sb(nc, ctx, "p_w_gat_o", [P, H2, D])
        a_blk = sb(nc, ctx, "p_a_blk", [P, H2, 2 * HEADS])
        w_kv = sb(nc, ctx, "p_w_kv", [P, H2, 2 * D])
        valid = sb(nc, ctx, "p_valid", [TT, NTT])
        x_c = sb(nc, ctx, "p_x", [P, H2, CH])
        cent = sb(nc, ctx, "p_cent", [P, H2, CH])
        sq = sb(nc, ctx, "p_sq", [P, H2, CH])
        std = sb(nc, ctx, "p_std", [P, CH])
        rstd = sb(nc, ctx, "p_rstd", [P, CH])
        xn = sb(nc, ctx, "p_xn", [P, H2, CH])
        rows = sb(nc, ctx, "p_rows", [TT, TILES, D])
        tab = sb(nc, ctx, "p_tab", [TT, TILES, ROW])
        kneg = sb(nc, ctx, "p_kneg", [TT, TILES, D])
        kexp = sb(nc, ctx, "p_kexp", [TT, TILES, D])
        k_t = sb(nc, ctx, "p_k", [TT, TILES, D])
        v_t = sb(nc, ctx, "p_v", [TT, TILES, D])
        kv_acc = sb(nc, ctx, "p_kv_acc", [P, H2, KROW])
        eps = sb(nc, ctx, "p_eps", [P, 1])

        mean_ps = ps(nc, ctx, "p_mean_ps", [P, 512])
        var_ps = ps(nc, ctx, "p_var_ps", [P, 512])
        tab_ps = ps(nc, ctx, "p_tab_ps", [P, 2, 512])
        k_ps = ps(nc, ctx, "p_k_ps", [P, 512])
        v_ps = ps(nc, ctx, "p_v_ps", [P, 512])
        rows_ps = ps(nc, ctx, "p_rows_ps", [P, 512])
        kv_ps = ps(nc, ctx, "p_kv_ps", [P, 512])

        (consts, w_in, w_scores, w_scored, x_in, mean_ok, centred, squared, var_ok, std_ok, rstd_ok, xn_ok,
         xn_out, rows_mm, rows_ok, rows_out, tab_out, kexp_ok, k_ok, kneg_ok, kv_mm, kv_ok, kv_out) = sems(
            nc, ctx, "p", "consts w_in w_scores w_scored x_in mean_ok centred squared var_ok std_ok rstd_ok xn_ok "
            "xn_out rows_mm rows_ok rows_out tab_out kexp_ok k_ok kneg_ok kv_mm kv_ok kv_out")
        tab_mm = sems(nc, ctx, "p", "tab_mm0 tab_mm1")
        tab_ok = sems(nc, ctx, "p", "tab_ok0 tab_ok1")
        k_mm, v_mm, v_ok = sems(nc, ctx, "p", "k_mm v_mm v_ok")
        block = ctx.enter_context(nc.Block())

        @block.gpsimd
        def _(pool):
            nc.gpsimd.memset(inv_d[:], 1.0 / D).then_inc(consts, 1)
            nc.gpsimd.memset(eps[:], LN_EPS).then_inc(consts, 1)
            nc.gpsimd.memset(kv_acc[:], 0.0).then_inc(consts, 1)

        @block.sync
        def _(sp):
            sp.dma_start(w_gat_o[:], halves(a["gat_w"])).then_inc(w_in, 16)
            sp.dma_start(w_gat[:, :, 0:D], halves(a["gat_wT"])).then_inc(w_in, 16)
            sp.dma_start(a_blk[:], halves(a["a_blk"])).then_inc(w_in, 16)
            sp.dma_start(w_kv[:, :, 0:D], halves(a["Wk"])).then_inc(w_in, 16)
            sp.dma_start(w_kv[:, :, D:], halves(a["Wv"])).then_inc(w_in, 16)
            sp.dma_start(valid[:], a["valid"]).then_inc(w_in, 16)
            sp.dma_start(ident[:], a["ident"]).then_inc(w_in, 16)
            with sp.Fori(0, NCH) as i:
                sp.wait_ge(centred, START + i)
                sp.dma_start(x_c[:], halves(a["xT"])[:, :, bass.ds(i * CH, CH)]).then_inc(x_in, 16)
                sp.wait_ge(xn_ok, START + i + 1)
                sp.dma_start(halves(t["xnT"])[:, :, bass.ds(i * CH, CH)], xn[:]).then_inc(xn_out, 16)
                sp.wait_ge(rows_ok, START + 4 * i + 4)
                sp.dma_start(t["xn"][bass.ds(i * CH, CH), :].rearrange("(j p) f -> p j f", p=TT), rows[:]).then_inc(rows_out, 16)
                for s in range(2):
                    sp.wait_ge(tab_ok[s], START + 2 * i + 2)
                sp.dma_start(t["table"][bass.ds(i * CH, CH), :].rearrange("(j p) f -> p j f", p=TT), tab[:]).then_inc(tab_out, 16)
            sp.wait_ge(kv_ok, START + NCH)
            sp.dma_start(t["kv"], kv_acc[:]).then_inc(kv_out, 16)
            sp.wait_ge(xn_out, START + 16 * NCH)
            sp.wait_ge(rows_out, START + 16 * NCH)
            sp.wait_ge(tab_out, START + 16 * NCH)
            sp.wait_ge(kv_out, START + 16)

        @block.tensor
        def _(pe):
            pe.wait_ge(consts, START + 3)
            pe.wait_ge(w_in, START + 16 * 7)
            for m in range(H2):
                for k in range(H2):
                    last = nc.tensor.matmul(tab_ps[:, 0, 8 * m:8 * m + 8], w_gat_o[:, k, m * P:(m + 1) * P], a_blk[:, k, :],
                                            start=(k == 0), stop=(k == H2 - 1))
            last.then_inc(w_scores, 1)
            pe.wait_ge(w_scored, START + 1)
            with pe.Fori(0, NCH) as i:
                pe.wait_ge(x_in, START + 16 * i + 16)
                pe.wait_ge(centred, START + i)
                for k in range(H2):
                    last = nc.tensor.matmul(mean_ps[:, 0:CH], inv_d[:], x_c[:, k, :], start=(k == 0), stop=(k == 1))
                last.then_inc(mean_ok, 1)
                pe.wait_ge(squared, START + i + 1)
                pe.wait_ge(std_ok, START + i)
                for k in range(H2):
                    last = nc.tensor.matmul(var_ps[:, 0:CH], inv_d[:], sq[:, k, :], start=(k == 0), stop=(k == 1))
                last.then_inc(var_ok, 1)
                pe.wait_ge(xn_ok, START + i + 1)
                for j in range(TILES):
                    s, u = j % 2, j // 2
                    tok = slice(j * TT, (j + 1) * TT)
                    pe.wait_ge(tab_ok[s], START + 2 * i + u)
                    for k in range(H2):
                        last = nc.tensor.matmul(tab_ps[0:TT, s, 0:ROW], xn[:, k, tok], w_gat[:, k, :],
                                                start=(k == 0), stop=(k == 1))
                    last.then_inc(tab_mm[s], 1)
                    for bank, w, done, read in ((k_ps, 0, k_mm, k_ok), (v_ps, D, v_mm, v_ok)):
                        pe.wait_ge(read, START + 4 * i + j)
                        for k in range(H2):
                            last = nc.tensor.matmul(bank[0:TT, 0:D], xn[:, k, tok], w_kv[:, k, w:w + D],
                                                    start=(k == 0), stop=(k == 1))
                        last.then_inc(done, 1)
                    pe.wait_ge(rows_ok, START + 4 * i + j)
                    for k in range(H2):
                        last = nc.tensor.transpose(rows_ps[0:TT, k * P:(k + 1) * P], xn[:, k, tok], ident[:])
                    last.then_inc(rows_mm, 1)
                pe.wait_ge(k_ok, START + 4 * i + 4)
                pe.wait_ge(v_ok, START + 4 * i + 4)
                pe.wait_ge(kv_ok, START + i)
                for b in range(H2):
                    for j in range(TILES):
                        nc.tensor.matmul(kv_ps[:, b * KROW:b * KROW + P], k_t[:, j, b * P:(b + 1) * P],
                                         v_t[:, j, b * P:(b + 1) * P], start=(j == 0), stop=(j == TILES - 1))
                    for j in range(TILES):
                        last = nc.tensor.matmul(kv_ps[:, b * KROW + P:(b + 1) * KROW], k_t[:, j, b * P:(b + 1) * P],
                                                valid[:, bass.ds(i * TILES + j, 1)], start=(j == 0), stop=(j == TILES - 1))
                last.then_inc(kv_mm, 1)

        @block.scalar
        def _(act):
            with act.Fori(0, NCH) as i:
                act.wait_ge(centred, START + i + 1)
                act.wait_ge(var_ok, START + i)
                nc.scalar.activation(sq[:], cent[:], ACT.Square).then_inc(squared, 1)
                act.wait_ge(var_ok, START + i + 1)
                nc.scalar.activation(std[:], var_ps[:, 0:CH], ACT.Ln, bias=eps[:]).then_inc(std_ok, 1)
                act.wait_ge(std_ok, START + i + 1)
                act.wait_ge(xn_ok, START + i)
                nc.scalar.activation(rstd[:], std[:], ACT.Exp, scale=-0.5).then_inc(rstd_ok, 1)
                act.wait_ge(kv_mm, START + i)
                act.wait_ge(tab_out, START + 16 * i)
                for j in range(TILES):
                    s, u = j % 2, j // 2
                    act.wait_ge(tab_mm[s], START + 2 * i + u + 1)
                    nc.scalar.activation(tab[:, j, :], tab_ps[0:TT, s, 0:ROW], ACT.Copy).then_inc(tab_ok[s], 1)
                    act.wait_ge(v_mm, START + 4 * i + j + 1)
                    nc.scalar.activation(v_t[:, j, :], v_ps[0:TT, 0:D], ACT.Copy).then_inc(v_ok, 1)
                    act.wait_ge(kneg_ok, START + 4 * i + j + 1)
                    act.wait_ge(k_ok, START + 4 * i)
                    nc.scalar.activation(kexp[:, j, :], kneg[:, j, :], ACT.Exp).then_inc(kexp_ok, 1)

        @block.vector
        def _(dve):
            dve.wait_ge(w_scores, START + 1)
            nc.vector.tensor_copy(w_gat[:, :, D:ROW], tab_ps[:, 0, 0:16].rearrange("p (h c) -> p h c", h=H2)).then_inc(w_scored, 1)
            with dve.Fori(0, NCH) as i:
                dve.wait_ge(mean_ok, START + i + 1)
                dve.wait_ge(squared, START + i)
                dve.wait_ge(xn_ok, START + i)
                nc.vector.tensor_tensor(cent[:], x_c[:], over_halves(mean_ps[:, 0:CH]), ALU.subtract).then_inc(centred, 1)
                dve.wait_ge(rstd_ok, START + i + 1)
                dve.wait_ge(centred, START + i + 1)
                dve.wait_ge(rows_mm, START + 4 * i)
                dve.wait_ge(xn_out, START + 16 * i)
                nc.vector.tensor_tensor(xn[:], cent[:], over_halves(rstd[:]), ALU.mult).then_inc(xn_ok, 1)
                dve.wait_ge(rows_out, START + 16 * i)
                dve.wait_ge(kv_mm, START + i)
                for j in range(TILES):
                    dve.wait_ge(k_mm, START + 4 * i + j + 1)
                    dve.wait_ge(kexp_ok, START + 4 * i)
                    nc.vector.tensor_scalar(kneg[:, j, :], k_ps[0:TT, 0:D], 0.0, None, ALU.min).then_inc(kneg_ok, 1)
                    dve.wait_ge(rows_mm, START + 4 * i + j + 1)
                    nc.vector.tensor_copy(rows[:, j, :], rows_ps[0:TT, 0:D]).then_inc(rows_ok, 1)
                    dve.wait_ge(kexp_ok, START + 4 * i + j + 1)
                    nc.vector.scalar_tensor_tensor(k_t[:, j, :], k_ps[0:TT, 0:D], 0.0, kexp[:, j, :],
                                                   ALU.max, ALU.add).then_inc(k_ok, 1)
                dve.wait_ge(kv_mm, START + i + 1)
                dve.wait_ge(kv_ok, START + i)
                nc.vector.tensor_tensor(kv_acc[:], kv_acc[:], kv_ps[:, 0:H2 * KROW].rearrange("p (h c) -> p h c", h=H2),
                                        ALU.add).then_inc(kv_ok, 1)


GRP = 20
TINY = 1e-37


def stage_rank(nc, a, t):
    with ExitStack() as ctx:
        src_i = sb(nc, ctx, "r_src_i", [EP, EC], I32)
        part_i = sb(nc, ctx, "r_part_i", [EP, EC], I32)
        lo = sb(nc, ctx, "r_lo", [EP, EC], BF16)
        hi = sb(nc, ctx, "r_hi", [EP, EC], BF16)
        count = sb(nc, ctx, "r_count", [P, P], BF16)
        hot_lo = sb(nc, ctx, "r_hot_lo", [EP, 2, GRP, P], BF16)
        hot_hi = sb(nc, ctx, "r_hot_hi", [EP, 2, GRP, NT], BF16)
        zero = sb(nc, ctx, "r_zero", [P, P], BF16)
        ident = sb(nc, ctx, "r_ident", [P, P])
        noise = sb(nc, ctx, "r_noise", [P, NT])
        v_col = sb(nc, ctx, "r_v_col", [P, NT])
        v_row = sb(nc, ctx, "r_v_row", [NT, P])
        v_all = sb(nc, ctx, "r_v_all", [P, NP])
        before = sb(nc, ctx, "r_before", [P, 2 * NP], BF16)
        hits = sb(nc, ctx, "r_hits", [P, NP], BF16)
        rank_f = sb(nc, ctx, "r_rank_f", [P, NT])
        rank_i = sb(nc, ctx, "r_rank_i", [P, NT], I32)
        rank_row = sb(nc, ctx, "r_rank_row", [NT, P], I32)
        xrows = sb(nc, ctx, "r_xrows", [P, NT, D])
        deg_ps = ps(nc, ctx, "r_deg_ps", [P, 512])
        row_ps = ps(nc, ctx, "r_row_ps", [P, 512])
        (src_in, other_in, xrows_in, consts, before_ok, part_ok, lo_ok, hi_ok, deg_ok, vcol_ok, vrow_mm, vrow_ok,
         vrow_out, vall_in, rankf_ok, ranki_ok, rank_mm, rankrow_ok, rank_out, moved) = sems(
            nc, ctx, "r", "src_in other_in xrows_in consts before_ok part_ok lo_ok hi_ok deg_ok vcol_ok vrow_mm "
            "vrow_ok vrow_out vall_in rankf_ok ranki_ok rank_mm rankrow_ok rank_out moved")
        hotlo_ok = sems(nc, ctx, "r", "hotlo0 hotlo1")
        hothi_ok = sems(nc, ctx, "r", "hothi0 hothi1")
        hot_used = sems(nc, ctx, "r", "hot_used0 hot_used1")
        steps = EC // GRP // 2
        block = ctx.enter_context(nc.Block())

        @block.sync
        def _(sp):
            sp.dma_start(src_i[:], a["src"]).then_inc(src_in, 16)
            sp.dma_start(ident[:], a["ident"]).then_inc(other_in, 16)
            sp.dma_start(noise[:], a["noise"]).then_inc(other_in, 16)
            sp.dma_start(xrows[:], t["xn"].rearrange("(i p) f -> p i f", p=P)).then_inc(xrows_in, 16)
            sp.wait_ge(vrow_ok, START + 1)
            sp.dma_start(t["v"].rearrange("(i p) -> i p", p=P), v_row[:]).then_inc(vrow_out, 16)
            sp.wait_ge(vrow_out, START + 16)
            sp.dma_start(v_all[:], t["v"].unsqueeze(0).to_broadcast([P, NP])).then_inc(vall_in, 16)
            sp.wait_ge(rankrow_ok, START + 1)
            sp.dma_start(t["rank"].rearrange("(i p) -> i p", p=P), rank_row[:]).then_inc(rank_out, 16)
            sp.wait_ge(rank_out, START + 16)
            sp.wait_ge(moved, 16 * NT)

        @block.gpsimd
        def _(pool):
            nc.gpsimd.iota(count[:], [[1, P]], base=0, channel_multiplier=0,
                           allow_small_or_imprecise_dtypes=True).then_inc(consts, 1)
            nc.gpsimd.memset(zero[:], 0.0).then_inc(consts, 1)
            nc.gpsimd.memset(before[:], TINY).then_inc(before_ok, 1)
            pool.wait_ge(before_ok, START + 1)
            nc.gpsimd.affine_select(out=before[:], in_=before[:], compare_op=ALU.is_gt, fill=0.0, base=NP,
                                    pattern=[[-1, 2 * NP]], channel_multiplier=1).then_inc(before_ok, 1)
            pool.wait_ge(xrows_in, START + 16)
            pool.wait_ge(ranki_ok, START + 1)
            for i in range(NT):
                nc.gpsimd.indirect_dma_start(
                    out=t["xs"], out_offset=bass.IndirectOffsetOnAxis(ap=rank_i[:, i:i + 1], axis=0),
                    in_=xrows[:, i, :], in_offset=None).then_inc(moved, 16)

        @block.vector
        def _(dve):
            dve.wait_ge(src_in, START + 16)
            nc.vector.tensor_single_scalar(part_i[:], src_i[:], P - 1, op=ALU.bitwise_and).then_inc(part_ok, 1)
            dve.wait_ge(part_ok, START + 1)
            nc.vector.tensor_copy(lo[:], part_i[:]).then_inc(lo_ok, 1)
            dve.wait_ge(lo_ok, START + 1)
            nc.vector.tensor_single_scalar(part_i[:], src_i[:], 7, op=ALU.logical_shift_right).then_inc(part_ok, 1)
            dve.wait_ge(part_ok, START + 2)
            nc.vector.tensor_copy(hi[:], part_i[:]).then_inc(hi_ok, 1)
            dve.wait_ge(consts, START + 2)
            dve.wait_ge(hi_ok, START + 1)
            with dve.Fori(0, steps) as i:
                for s in range(2):
                    cols = bass.ds((i * 2 + s) * GRP, GRP)
                    dve.wait_ge(hot_used[s], START + i)
                    for hot, val, n, done in ((hot_lo, lo, P, hotlo_ok), (hot_hi, hi, NT, hothi_ok)):
                        nc.vector.tensor_tensor(hot[:, s], count[0:EP, 0:n].unsqueeze(1).to_broadcast([EP, GRP, n]),
                                                val[:, cols].unsqueeze(2).to_broadcast([EP, GRP, n]),
                                                ALU.is_equal).then_inc(done[s], 1)
            dve.wait_ge(deg_ok, START + 1)
            dve.wait_ge(other_in, START + 32)
            nc.vector.tensor_tensor(v_col[:], deg_ps[:, 0:NT], noise[:], ALU.add).then_inc(vcol_ok, 1)
            dve.wait_ge(vrow_mm, START + 1)
            nc.vector.tensor_copy(v_row[:], row_ps[0:NT, 0:P]).then_inc(vrow_ok, 1)
            dve.wait_ge(vall_in, START + 16)
            dve.wait_ge(before_ok, START + 2)
            dve.wait_ge(vcol_ok, START + 1)
            with dve.Fori(0, NT) as i:
                dve.wait_ge(rankf_ok, START + i)
                nc.vector.scalar_tensor_tensor(hits[:], v_all[:], v_col[:, bass.ds(i, 1)], before[:, bass.ds(i * (-P) + NP, NP)],
                                               ALU.subtract, ALU.is_lt, accum_out=rank_f[:, bass.ds(i, 1)]).then_inc(rankf_ok, 1)
            dve.wait_ge(rankf_ok, START + NT)
            nc.vector.tensor_copy(rank_i[:], rank_f[:]).then_inc(ranki_ok, 1)
            dve.wait_ge(rank_mm, START + 1)
            nc.vector.tensor_copy(rank_row[:], row_ps[0:NT, 0:P]).then_inc(rankrow_ok, 1)

        @block.tensor
        def _(pe):
            pe.wait_ge(consts, START + 2)
            nc.tensor.matmul(deg_ps[:, 0:NT], zero[:], zero[:, 0:NT], start=True, stop=False, skip_group_check=True)
            with pe.Fori(0, steps) as i:
                for s in range(2):
                    pe.wait_ge(hotlo_ok[s], START + i + 1)
                    pe.wait_ge(hothi_ok[s], START + i + 1)
                    for g in range(GRP):
                        last = nc.tensor.matmul(deg_ps[:, 0:NT], hot_lo[:, s, g, :], hot_hi[:, s, g, :],
                                                start=False, stop=False, skip_group_check=True)
                    last.then_inc(hot_used[s], 1)
            nc.tensor.matmul(deg_ps[:, 0:NT], zero[:], zero[:, 0:NT], start=False, stop=True,
                             skip_group_check=True).then_inc(deg_ok, 1)
            pe.wait_ge(other_in, START + 32)
            pe.wait_ge(vcol_ok, START + 1)
            nc.tensor.transpose(row_ps[0:NT, 0:P], v_col[:], ident[:]).then_inc(vrow_mm, 1)
            pe.wait_ge(rankf_ok, START + NT)
            pe.wait_ge(vrow_ok, START + 1)
            nc.tensor.transpose(row_ps[0:NT, 0:P], rank_f[:], ident[:]).then_inc(rank_mm, 1)


STATES = 16
TAPS = 4
BC = 2 * STATES
PARTS = 3
DBC = PARTS * BC + STATES


def stage_mamba(nc, a, t):
    with ExitStack() as ctx:
        def two(name, shape, dt=F32):
            return [sb(nc, ctx, f"m_{name}{c}", shape, dt) for c in range(2)]

        ident = sb(nc, ctx, "m_ident", [P, P])
        w_in = sb(nc, ctx, "m_w_in", [P, H2, 2 * D])
        w_dbc = sb(nc, ctx, "m_w_dbc", [P, H2, DBC])
        w_dt = sb(nc, ctx, "m_w_dt", [DBC, D])
        w_out = sb(nc, ctx, "m_w_out", [P, H2, D])
        pick_f = sb(nc, ctx, "m_pick_f", [PARTS * BC, BC, P])
        pick = sb(nc, ctx, "m_pick", [PARTS * BC, BC, P], BF16)
        vecs = sb(nc, ctx, "m_vecs", [P, H2, TAPS + 3])
        a_log = sb(nc, ctx, "m_a_log", [P, H2, STATES])
        a_exp = sb(nc, ctx, "m_a_exp", [P, H2, STATES])
        a_neg = sb(nc, ctx, "m_a_neg", [P, H2, STATES])
        rows = sb(nc, ctx, "m_rows", [TT, TILES, D])
        xsT = sb(nc, ctx, "m_xsT", [P, H2, CH])
        tail = TAPS - 1
        xpad = sb(nc, ctx, "m_xpad", [P, H2, tail + CH])
        keep = sb(nc, ctx, "m_keep", [P, H2, tail])
        conv = sb(nc, ctx, "m_conv", [P, H2, CH])
        dbc = sb(nc, ctx, "m_dbc", [DBC, CH])
        rest = sb(nc, ctx, "m_rest", [PARTS * BC, CH])
        pre = sb(nc, ctx, "m_pre", [P, H2, CH])
        nabs = sb(nc, ctx, "m_nabs", [P, H2, CH])
        ex = sb(nc, ctx, "m_ex", [P, H2, CH])
        ex1 = sb(nc, ctx, "m_ex1", [P, H2, CH])
        lg = sb(nc, ctx, "m_lg", [P, H2, CH])
        zs, xc, dt, u = two("zs", [P, H2, CH]), two("xc", [P, H2, CH]), two("dt", [P, H2, CH]), two("u", [P, H2, CH])
        parts = two("parts", [PARTS * BC, CH], BF16)
        decay, drive, h_t, hc = (two(n, [P, H2, CH]) for n in ("decay", "drive", "h", "hc"))
        state = sb(nc, ctx, "m_state", [P, H2, STATES])
        ysum = sb(nc, ctx, "m_ysum", [P, H2, CH])
        yg = sb(nc, ctx, "m_yg", [P, H2, CH])
        yrow = sb(nc, ctx, "m_yrow", [TT, TILES, D])
        row_ps = ps(nc, ctx, "m_row_ps", [P, 512])
        lin_ps = ps(nc, ctx, "m_lin_ps", [P, 512])
        b_ps = ps(nc, ctx, "m_b_ps", [P, 2, 512])
        c_ps = ps(nc, ctx, "m_c_ps", [P, 2, 512])
        y_ps = ps(nc, ctx, "m_y_ps", [P, 2, 512])
        (w_ok, pick_ok, aexp_ok, aneg_ok, state0, rows_in, xs_mm, xs_ok, xz_mm, xz_ok, kept, keep_ok, tap, z_ok, xc_ok, dbc_mm,
         dbc_ok, rest_ok, parts_ok, dt_mm, pre_ok, nabs_ok, ex_ok, ex1_ok, lg_ok, resid, sum_ok, dt_ok, u_ok, ysum_ok, yg_ok,
         yrow_mm, yrow_ok, y_out) = sems(
            nc, ctx, "m", "w_ok pick_ok aexp_ok aneg_ok state0 rows_in xs_mm xs_ok xz_mm xz_ok kept keep_ok tap z_ok xc_ok "
            "dbc_mm dbc_ok rest_ok parts_ok dt_mm pre_ok nabs_ok ex_ok ex1_ok lg_ok resid sum_ok dt_ok u_ok ysum_ok yg_ok "
            "yrow_mm yrow_ok y_out")
        b_mm, c_mm, decay_ok, drive_ok, scanned, hc_ok, hc_used, saved = (
            sems(nc, ctx, "m", f"{n}0 {n}1") for n in "b_mm c_mm decay_ok drive_ok scanned hc_ok hc_used saved".split())
        U = STATES // 2
        block = ctx.enter_context(nc.Block())

        def chunks(eng, chunk):
            chunk(0, 0, True, False)
            with eng.Fori(0, NCH // 2 - 1) as i:
                for c in (1, 0):
                    chunk(i * 2 + (1 if c else 2), c, False, False)
            chunk(NCH - 1, 1, False, True)

        @block.sync
        def _(sp):
            loads = [(ident[:], a["ident"]), (w_in[:], halves(a["in_projT"])), (w_dbc[:], halves(a["x_projT"])),
                     (w_dt[:], a["dt_projT"]), (w_out[:], halves(a["out_projT"])), (pick_f[:], a["pick"]),
                     (vecs[:], halves(a["mamba_vecs"])), (a_log[:], halves(a["A_log"]))]
            sp.dma_start(rows[:], t["xs"][0:CH, :].rearrange("(j p) f -> p j f", p=TT)).then_inc(rows_in, 16)
            for dst, source in loads:
                sp.dma_start(dst, source).then_inc(w_ok, 16)
            with sp.Fori(1, NCH) as g:
                sp.wait_ge(xs_mm, START + 4 * g)
                sp.dma_start(rows[:], t["xs"][bass.ds(g * CH, CH), :].rearrange("(j p) f -> p j f", p=TT)).then_inc(rows_in, 16)
                sp.wait_ge(yrow_ok, START + 4 * g)
                sp.dma_start(t["y"][bass.ds((g - 1) * CH, CH), :].rearrange("(j p) f -> p j f", p=TT), yrow[:]).then_inc(y_out, 16)
            sp.wait_ge(yrow_ok, START + 4 * NCH)
            sp.dma_start(t["y"][(NCH - 1) * CH:, :].rearrange("(j p) f -> p j f", p=TT), yrow[:]).then_inc(y_out, 16)
            sp.wait_ge(y_out, START + 16 * NCH)

        @block.tensor
        def _(pe):
            def turn(g, j, outs=True):
                pe.wait_ge(rows_in, START + 16 * (g + 1))
                pe.wait_ge(xs_ok, START + 4 * g + j)
                if outs:
                    pe.wait_ge(yrow_ok, START + 4 * (g - 1))
                for k in range(H2):
                    last = nc.tensor.transpose(row_ps[:, k * TT:(k + 1) * TT], rows[:, j, k * P:(k + 1) * P], ident[0:TT, 0:TT])
                last.then_inc(xs_mm, 1)

            def in_proj(g, m):
                pe.wait_ge(xs_ok, START + 4 * g + 4)
                pe.wait_ge(pre_ok, START + 2 * g) if m == 0 else pe.wait_ge(xz_ok, START + 2 * g + m) if m <= 2 else pe.wait_ge(z_ok, START + 2 * g + 1)
                for k in range(H2):
                    last = nc.tensor.matmul(lin_ps[:, 0:CH], w_in[:, k, m * P:(m + 1) * P], xsT[:, k, :],
                                            start=(k == 0), stop=(k == 1))
                last.then_inc(xz_mm, 1)

            def x_proj(g, c):
                pe.wait_ge(z_ok, START + 2 * g + 2)
                pe.wait_ge(xc_ok, START + 2 * g + 2)
                for k in range(H2):
                    last = nc.tensor.matmul(lin_ps[0:DBC, 0:CH], w_dbc[:, k, :], xc[c][:, k, :], start=(k == 0), stop=(k == 1))
                last.then_inc(dbc_mm, 1)

            def dt_proj(g, k):
                pe.wait_ge(dbc_ok, START + 2 * g + 2)
                pe.wait_ge(pre_ok, START + 2 * g + k)
                nc.tensor.matmul(lin_ps[:, 0:CH], w_dt[:, k * P:(k + 1) * P], dbc[:], start=True, stop=True).then_inc(dt_mm, 1)

            def spread(g, c, s):
                q, n = s % 2, s // 2
                pe.wait_ge(parts_ok, START + 2 * g + 2)
                pe.wait_ge(drive_ok[q], START + U * g + n)
                nc.tensor.matmul(b_ps[:, q, 0:CH], pick[:, s, :], parts[c][:], start=True, stop=True).then_inc(b_mm[q], 1)
                pe.wait_ge(hc_ok[q], START + U * g + n)
                nc.tensor.matmul(c_ps[:, q, 0:CH], pick[:, STATES + s, :], parts[c][:], start=True, stop=True).then_inc(c_mm[q], 1)

            def add(g, s):
                q, n = s % 2, s // 2
                if s == 0:
                    pe.wait_ge(ysum_ok, START + 2 * g)
                pe.wait_ge(hc_ok[q], START + U * g + n + 1)
                for k in range(H2):
                    last = nc.tensor.matmul(y_ps[:, k, 0:CH], ident[:], hc[q][:, k, :], start=(s == 0), stop=(s == STATES - 1))
                last.then_inc(hc_used[q], 1)

            def out_rows(g, j, end=False):
                pe.wait_ge(yg_ok, START + g + 1)
                pe.wait_ge(yrow_ok, START + 4 * g + j)
                if not end:
                    pe.wait_ge(xs_ok, START + 4 * (g + 2))
                for k in range(H2):
                    last = nc.tensor.matmul(row_ps[0:TT, 0:D], yg[:, k, j * TT:(j + 1) * TT], w_out[:, k, :],
                                            start=(k == 0), stop=(k == 1))
                last.then_inc(yrow_mm, 1)

            def chunk(g, c, first, final):
                for s in range(STATES):
                    if s + 1 < STATES:
                        spread(g, c, s + 1)
                    elif not final:
                        spread(g + 1, 1 - c, 0)
                    if s in (1, 2) and not first:
                        out_rows(g - 1, 2 * (s - 1))
                    if s in (3, 4) and not final:
                        turn(g + 1, 2 * (s - 3), not first)
                    if s > 0:
                        add(g, s - 1)
                    elif not first:
                        add(g - 1, STATES - 1)
                    if s in (1, 2) and not first:
                        out_rows(g - 1, 2 * (s - 1) + 1)
                    if s in (3, 4) and not final:
                        turn(g + 1, 2 * (s - 3) + 1, not first)
                    if not final:
                        if 5 <= s <= 8:
                            in_proj(g + 1, s - 5)
                        if s == 9:
                            x_proj(g + 1, 1 - c)
                        if s in (10, 11):
                            dt_proj(g + 1, s - 10)

            pe.wait_ge(w_ok, START + 16 * 8)
            pe.wait_ge(pick_ok, START + 1)
            for j in range(TILES):
                turn(0, j, False)
            for m in range(4):
                in_proj(0, m)
            x_proj(0, 0)
            for k in range(H2):
                dt_proj(0, k)
            spread(0, 0, 0)
            chunks(pe, chunk)
            add(NCH - 1, STATES - 1)
            for j in range(TILES):
                out_rows(NCH - 1, j, True)

        @block.scalar
        def _(act):
            def turned(g, j):
                act.wait_ge(xs_mm, START + 4 * g + j + 1)
                act.wait_ge(xz_mm, START + 4 * g)
                nc.scalar.activation(xsT[:, :, j * TT:(j + 1) * TT],
                                     row_ps[:, 0:H2 * TT].rearrange("p (k n) -> p k n", k=H2), ACT.Copy).then_inc(xs_ok, 1)

            def carry(g):
                act.wait_ge(tap, START + 8 * g)
                act.wait_ge(kept, START + g)
                nc.scalar.activation(xpad[:, :, 0:tail], keep[:], ACT.Copy).then_inc(keep_ok, 1)

            def conv_in(g, m):
                act.wait_ge(xz_mm, START + 4 * g + m + 1)
                act.wait_ge(keep_ok, START + g + 1)
                nc.scalar.activation(xpad[:, m, tail:], lin_ps[:, 0:CH], ACT.Copy).then_inc(xz_ok, 1)
                if m == 1:
                    act.wait_ge(xz_ok, START + 2 * g + 2)
                    nc.scalar.activation(keep[:], xpad[:, :, CH:], ACT.Copy).then_inc(kept, 1)

            def gate(g, c, m, ahead=True):
                act.wait_ge(xz_mm, START + 4 * g + m + 3)
                if ahead:
                    act.wait_ge(yg_ok, START + g - 1)
                nc.scalar.activation(zs[c][:, m, :], lin_ps[:, 0:CH], ACT.Silu).then_inc(z_ok, 1)

            def conv_out(g, c, k, ahead=True):
                act.wait_ge(tap, START + 8 * g + 4 * k + 4)
                if ahead:
                    act.wait_ge(ysum_ok, START + 2 * (g - 1))
                nc.scalar.activation(xc[c][:, k, :], conv[:, k, :], ACT.Silu, bias=vecs[:, k, TAPS:TAPS + 1]).then_inc(xc_ok, 1)

            def split_high(g, c, ahead=True):
                act.wait_ge(dbc_mm, START + g + 1)
                act.wait_ge(dt_mm, START + 2 * g)
                act.wait_ge(parts_ok, START + 2 * g)
                nc.scalar.activation(dbc[:], lin_ps[0:DBC, 0:CH], ACT.Copy).then_inc(dbc_ok, 1)
                if ahead:
                    act.wait_ge(c_mm[1], START + U * (g - 1))
                nc.scalar.activation(parts[c][:], lin_ps[0:PARTS * BC, 0:CH], ACT.Copy).then_inc(dbc_ok, 1)

            def exp_dt(g):
                act.wait_ge(nabs_ok, START + g + 1)
                nc.scalar.activation(ex[:], nabs[:], ACT.Exp).then_inc(ex_ok, 1)

            def log_dt(g):
                act.wait_ge(ex1_ok, START + g + 1)
                nc.scalar.activation(lg[:], ex1[:], ACT.Ln).then_inc(lg_ok, 1)

            def decays(g, c, s):
                q, n = s % 2, s // 2
                if s == 0:
                    act.wait_ge(dt_ok, START + g + 1)
                act.wait_ge(scanned[q], START + 2 * (U * g + n))
                for k in range(H2):
                    nc.scalar.activation(decay[q][:, k, :], dt[c][:, k, :], ACT.Exp, scale=a_neg[:, k, s:s + 1]).then_inc(decay_ok[q], 1)

            def save(g, s):
                q, n = s % 2, s // 2
                act.wait_ge(scanned[q], START + 2 * (U * g + n) + 2)
                nc.scalar.activation(state[:, :, s:s + 1], h_t[q][:, :, CH - 1:CH], ACT.Copy).then_inc(saved[q], 1)

            def out_row(g, j):
                act.wait_ge(yrow_mm, START + 4 * g + j + 1)
                act.wait_ge(y_out, START + 16 * g)
                nc.scalar.activation(yrow[:, j, :], row_ps[0:TT, 0:D], ACT.Copy).then_inc(yrow_ok, 1)

            def chunk(g, c, first, final):
                for s in range(STATES):
                    if s + 1 < STATES:
                        decays(g, c, s + 1)
                    elif not final:
                        decays(g + 1, 1 - c, 0)
                    if s > 0:
                        save(g, s - 1)
                    elif not first:
                        save(g - 1, STATES - 1)
                    if s in (1, 2) and not first:
                        out_row(g - 1, 2 * (s - 1))
                        out_row(g - 1, 2 * (s - 1) + 1)
                    if not final:
                        if s in (3, 4):
                            turned(g + 1, 2 * (s - 3))
                            turned(g + 1, 2 * (s - 3) + 1)
                        if s == 5:
                            carry(g + 1)
                        if s in (5, 6):
                            conv_in(g + 1, s - 5)
                        if s in (7, 8):
                            gate(g + 1, 1 - c, s - 7, not first)
                            conv_out(g + 1, 1 - c, s - 7, not first)
                        if s == 9:
                            split_high(g + 1, 1 - c, not first)
                        if s == 12:
                            exp_dt(g + 1)
                        if s == 13:
                            log_dt(g + 1)

            act.wait_ge(w_ok, START + 16 * 8)
            nc.scalar.activation(pick[:], pick_f[:], ACT.Copy).then_inc(pick_ok, 1)
            nc.scalar.activation(a_exp[:], a_log[:], ACT.Exp).then_inc(aexp_ok, 1)
            act.wait_ge(aneg_ok, START + 1)
            act.wait_ge(state0, START + 2)
            for j in range(TILES):
                turned(0, j)
            carry(0)
            for m in range(2):
                conv_in(0, m)
            for m in range(2):
                gate(0, 0, m, False)
                conv_out(0, 0, m, False)
            split_high(0, 0, False)
            exp_dt(0)
            log_dt(0)
            decays(0, 0, 0)
            chunks(act, chunk)
            for j in range(TILES):
                out_row(NCH - 1, j)

        @block.gpsimd
        def _(pool):
            nc.gpsimd.memset(state[:], 0.0).then_inc(state0, 1)
            nc.gpsimd.memset(keep[:], 0.0).then_inc(state0, 1)

        @block.vector
        def _(dve):
            def convolve(g, k):
                dve.wait_ge(keep_ok, START + g + 1)
                dve.wait_ge(xc_ok, START + 2 * g)
                dve.wait_ge(xz_ok, START + 2 * g + k + 1)
                nc.vector.tensor_scalar(conv[:, k, :], xpad[:, k, 0:CH], vecs[:, k, 0:1], None, ALU.mult).then_inc(tap, 1)
                for c in range(1, TAPS):
                    dve.wait_ge(tap, START + 8 * g + 4 * k + c)
                    nc.vector.scalar_tensor_tensor(conv[:, k, :], xpad[:, k, c:c + CH], vecs[:, k, c:c + 1], conv[:, k, :],
                                                   ALU.mult, ALU.add).then_inc(tap, 1)

            def split_low(g, c):
                mid, low = slice(BC, 2 * BC), slice(2 * BC, 3 * BC)
                dve.wait_ge(dbc_ok, START + 2 * g + 2)
                nc.vector.tensor_tensor(rest[low], dbc[low], parts[c][low], ALU.subtract).then_inc(rest_ok, 1)
                nc.vector.tensor_tensor(parts[c][mid], dbc[mid], parts[c][mid], ALU.subtract).then_inc(parts_ok, 1)
                dve.wait_ge(rest_ok, START + 2 * g + 1)
                nc.vector.tensor_copy(parts[c][low], rest[low]).then_inc(rest_ok, 1)
                dve.wait_ge(rest_ok, START + 2 * g + 2)
                nc.vector.tensor_tensor(parts[c][low], rest[low], parts[c][low], ALU.subtract).then_inc(parts_ok, 1)

            def dt_in(g, k):
                dve.wait_ge(dt_mm, START + 2 * g + k + 1)
                nc.vector.tensor_scalar(pre[:, k, :], lin_ps[:, 0:CH], vecs[:, k, TAPS + 1:TAPS + 2], None, ALU.add).then_inc(pre_ok, 1)

            def dt_abs(g):
                dve.wait_ge(pre_ok, START + 2 * g + 2)
                dve.wait_ge(ex_ok, START + g)
                nc.vector.scalar_tensor_tensor(nabs[:], pre[:], -1.0, pre[:], ALU.mult, ALU.min).then_inc(nabs_ok, 1)

            def dt_one(g):
                dve.wait_ge(ex_ok, START + g + 1)
                nc.vector.tensor_scalar(ex1[:], ex[:], 1.0, None, ALU.add).then_inc(ex1_ok, 1)

            def dt_out(g, c, ahead=True):
                dve.wait_ge(ex1_ok, START + g + 1)
                dve.wait_ge(lg_ok, START + g + 1)
                nc.vector.scalar_tensor_tensor(nabs[:], ex1[:], -1.0, ex[:], ALU.add, ALU.subtract).then_inc(resid, 1)
                dve.wait_ge(resid, START + g + 1)
                nc.vector.tensor_tensor(nabs[:], lg[:], nabs[:], ALU.subtract).then_inc(sum_ok, 1)
                dve.wait_ge(sum_ok, START + g + 1)
                if ahead:
                    dve.wait_ge(decay_ok[1], START + 2 * U * (g - 1))
                nc.vector.scalar_tensor_tensor(dt[c][:], pre[:], 0.0, nabs[:], ALU.max, ALU.add).then_inc(dt_ok, 1)

            def dt_x(g, c):
                dve.wait_ge(dt_ok, START + g + 1)
                dve.wait_ge(xc_ok, START + 2 * g + 2)
                nc.vector.tensor_tensor(u[c][:], dt[c][:], xc[c][:], ALU.mult).then_inc(u_ok, 1)

            def drives(g, c, s):
                q, n = s % 2, s // 2
                if s == 0:
                    dve.wait_ge(u_ok, START + g + 1)
                dve.wait_ge(b_mm[q], START + U * g + n + 1)
                dve.wait_ge(scanned[q], START + 2 * (U * g + n))
                nc.vector.tensor_tensor(drive[q][:], u[c][:], over_halves(b_ps[:, q, 0:CH]), ALU.mult).then_inc(drive_ok[q], 1)

            def scan(g, s):
                q, n = s % 2, s // 2
                dve.wait_ge(drive_ok[q], START + U * g + n + 1)
                dve.wait_ge(saved[q], START + U * g + n)
                dve.wait_ge(hc_ok[q], START + U * g + n)
                for k in range(H2):
                    dve.wait_ge(decay_ok[q], START + 2 * (U * g + n) + k + 1)
                    nc.vector.tensor_tensor_scan(h_t[q][:, k, :], decay[q][:, k, :], drive[q][:, k, :],
                                                 state[:, k, s:s + 1], ALU.mult, ALU.add).then_inc(scanned[q], 1)

            def read_out(g, s):
                q, n = s % 2, s // 2
                dve.wait_ge(c_mm[q], START + U * g + n + 1)
                dve.wait_ge(scanned[q], START + 2 * (U * g + n) + 2)
                dve.wait_ge(hc_used[q], START + U * g + n)
                nc.vector.tensor_tensor(hc[q][:], h_t[q][:], over_halves(c_ps[:, q, 0:CH]), ALU.mult).then_inc(hc_ok[q], 1)

            def gated(g, c):
                dve.wait_ge(hc_used[1], START + U * g + U)
                dve.wait_ge(yg_ok, START + g)
                for k in range(H2):
                    nc.vector.scalar_tensor_tensor(ysum[:, k, :], xc[c][:, k, :], vecs[:, k, TAPS + 2:TAPS + 3], y_ps[:, k, 0:CH],
                                                   ALU.mult, ALU.add).then_inc(ysum_ok, 1)
                dve.wait_ge(ysum_ok, START + 2 * g + 2)
                dve.wait_ge(z_ok, START + 2 * g + 2)
                dve.wait_ge(yrow_mm, START + 4 * g)
                nc.vector.tensor_tensor(yg[:], ysum[:], zs[c][:], ALU.mult).then_inc(yg_ok, 1)

            def chunk(g, c, first, final):
                for s in range(STATES):
                    if s + 1 < STATES:
                        drives(g, c, s + 1)
                    elif not final:
                        drives(g + 1, 1 - c, 0)
                    scan(g, s)
                    read_out(g, s)
                    if s == 0 and not first:
                        gated(g - 1, 1 - c)
                    if not final:
                        if s in (6, 7):
                            convolve(g + 1, s - 6)
                        if s == 10:
                            split_low(g + 1, 1 - c)
                        if s in (10, 11):
                            dt_in(g + 1, s - 10)
                        if s == 11:
                            dt_abs(g + 1)
                        if s == 12:
                            dt_one(g + 1)
                        if s == 13:
                            dt_out(g + 1, 1 - c, not first)
                        if s == 14:
                            dt_x(g + 1, 1 - c)

            dve.wait_ge(aexp_ok, START + 1)
            nc.vector.tensor_scalar(a_neg[:], a_exp[:], -1.0, None, ALU.mult).then_inc(aneg_ok, 1)
            dve.wait_ge(state0, START + 2)
            for k in range(H2):
                convolve(0, k)
            split_low(0, 0)
            for k in range(H2):
                dt_in(0, k)
            dt_abs(0)
            dt_one(0)
            dt_out(0, 0, False)
            dt_x(0, 0)
            drives(0, 0, 0)
            chunks(dve, chunk)
            gated(NCH - 1, 1)


QUAD = 4
RING = 6
SLOTS = -(-(-(-E // P) + NT) // (RING * QUAD)) * RING * QUAD
CODE = HEADS + 1
BIG = 1e30


def stage_attend(nc, a, t):
    with ExitStack() as ctx:
        ident = sb(nc, ctx, "g_ident", [P, P])
        token = sb(nc, ctx, "g_token", [P, 2])
        count = sb(nc, ctx, "g_count", [P, P])
        ones = sb(nc, ctx, "g_ones", [P, P])
        below = sb(nc, ctx, "g_below", [P, P])
        dst_i = sb(nc, ctx, "g_dst_i", [EP, EC], I32)
        dst_f = sb(nc, ctx, "g_dst_f", [EP, EC])
        ones_e = sb(nc, ctx, "g_ones_e", [EP, EC])
        less = sb(nc, ctx, "g_less", [EP, EC])
        bound = sb(nc, ctx, "g_bound", [P, NT + 1])
        part = sb(nc, ctx, "g_part", [EP, NT + 1])
        first = sb(nc, ctx, "g_first", [NT, 4])
        slots_i = sb(nc, ctx, "g_slots_i", [NT, 1], I32)
        tile_no = sb(nc, ctx, "g_tile_no", [NT, P])
        kk = sb(nc, ctx, "g_kk", [NT, SLOTS])
        hot = sb(nc, ctx, "g_hot", [NT, SLOTS])
        hot2 = sb(nc, ctx, "g_hot2", [NT, SLOTS])
        at = sb(nc, ctx, "g_at", [NT, SLOTS])
        slot_at = sb(nc, ctx, "g_slot_at", [1, SLOTS], I32)
        slot_tile = sb(nc, ctx, "g_slot_tile", [1, SLOTS], I32)
        slot_base = sb(nc, ctx, "g_slot_base", [P, SLOTS])
        score = sb(nc, ctx, "g_score", [P, NT, 2 * HEADS])
        code = sb(nc, ctx, "g_code", [P, NT, CODE])
        top = sb(nc, ctx, "g_top", [P, 8])
        top8 = sb(nc, ctx, "g_top8", [8, 1])
        lift = sb(nc, ctx, "g_lift", [1, 8])
        shift = sb(nc, ctx, "g_shift", [P, 1])
        guard = sb(nc, ctx, "g_guard", [P, 1])
        emax = sb(nc, ctx, "g_emax", [P, QUAD * HEADS])
        agg = sb(nc, ctx, "g_agg", [P, NT, D + HEADS])
        den = sb(nc, ctx, "g_den", [P, NT, HEADS])
        idx = sb(nc, ctx, "g_idx", [P, RING, QUAD, 2], I32)
        rel = sb(nc, ctx, "g_rel", [P, RING, QUAD])
        got = sb(nc, ctx, "g_got", [P, RING, QUAD, ROW])
        sel = sb(nc, ctx, "g_sel", [P, RING, QUAD, P])
        selT = sb(nc, ctx, "g_selT", [P, RING, QUAD, P])
        z = sb(nc, ctx, "g_z", [P, RING, QUAD, HEADS])
        pen = sb(nc, ctx, "g_pen", [P, RING, QUAD])
        lr = sb(nc, ctx, "g_lr", [P, RING, QUAD, HEADS])
        logit = sb(nc, ctx, "g_logit", [P, RING, QUAD, HEADS])
        wrow = sb(nc, ctx, "g_wrow", [P, RING, QUAD, D + HEADS])
        selT_ps = ps(nc, ctx, "g_selT_ps", [P, 2, 512])
        st_ps = ps(nc, ctx, "g_st_ps", [P, 2, 512])
        acc_ps = ps(nc, ctx, "g_acc_ps", [P, QUAD, 512])
        set_ps = acc_ps[:, 0:2, :]
        (settled, w_ok, score_in, consts, zeroed, dve_set, pe_set, act_set, emax_ok, fin, stored) = sems(
            nc, ctx, "g", "settled w_ok score_in consts zeroed dve_set pe_set act_set emax_ok fin stored")
        (idx_in, rel_ok, got_in, sel_ok, selT_mm, selT_ok, st_mm, z_ok, pen_ok, lr_ok, logit_ok, exp_ok, w_row_ok) = (
            sems(nc, ctx, "g", " ".join(f"{n}{q}" for q in range(RING))) for n in
            "idx_in rel_ok got_in sel_ok selT_mm selT_ok st_mm z_ok pen_ok lr_ok logit_ok exp_ok w_row_ok".split())
        acc_mm, acc_ok = (sems(nc, ctx, "g", " ".join(f"{n}{m}" for m in range(QUAD))) for n in ("acc_mm", "acc_ok"))
        HS = SLOTS // 2
        quads = SLOTS // QUAD
        block = ctx.enter_context(nc.Block())

        def there(i, j):
            return not isinstance(i, int) or 0 <= RING * i + j < quads

        def done(eng, sem, i, j, each=1):
            if there(i, j):
                eng.wait_ge(sem[j % RING], START + each * (i + j // RING + 1))

        def steps(eng, step, ahead):
            for k in range(-ahead, RING):
                step(k // RING, k % RING)
            with eng.Fori(1, quads // RING - 1) as i:
                for j in range(RING):
                    step(i, j)
            for k in range(quads - RING, quads + 1):
                step(k // RING, k % RING)

        @block.sync
        def _(sp):
            for dst, source in ((ident[:], a["ident"]), (below[:], a["below"]), (dst_i[:], a["dst"])):
                sp.dma_start(dst, source).then_inc(w_ok, 16)
            sp.dma_start(score[:], t["table"].rearrange("(i p) f -> p i f", p=P)[:, :, D:ROW]).then_inc(score_in, 16)
            sp.wait_ge(dve_set, START + 13)

            def step(i, j):
                if not there(i, j):
                    return
                q = j % RING
                done(sp, rel_ok, i, j - RING)
                if there(i, j - RING):
                    sp.wait_ge(got_in[q], 16 * QUAD * (i - 1) + 16 * QUAD)
                for m in range(QUAD):
                    e0 = sp.value_load(slot_at[0:1, bass.ds((i * RING + j) * QUAD + m, 1)], min_val=0, max_val=E)
                    sp.dma_start(idx[:, q, m, :], a["edges"][bass.ds(e0, P), :]).then_inc(idx_in[q], 16)

            steps(sp, step, 0)
            sp.wait_ge(fin, START + 3)
            sp.dma_start(t["agg"].rearrange("(i p) f -> p i f", p=P), agg[:, :, 0:D]).then_inc(stored, 16)
            sp.wait_ge(stored, START + 16)

        @block.gpsimd
        def _(pool):
            nc.gpsimd.iota(count[:], [[1, P]], base=0, channel_multiplier=0, allow_small_or_imprecise_dtypes=True).then_inc(consts, 1)
            nc.gpsimd.iota(bound[:], [[P, NT + 1]], base=0, channel_multiplier=0, allow_small_or_imprecise_dtypes=True).then_inc(consts, 1)
            nc.gpsimd.iota(tile_no[:], [[0, P]], base=0, channel_multiplier=1, allow_small_or_imprecise_dtypes=True).then_inc(consts, 1)
            nc.gpsimd.iota(kk[:], [[1, SLOTS]], base=0, channel_multiplier=0, allow_small_or_imprecise_dtypes=True).then_inc(consts, 1)
            nc.gpsimd.memset(ones[:], 1.0).then_inc(consts, 1)
            nc.gpsimd.memset(ones_e[:], 1.0).then_inc(consts, 1)
            nc.gpsimd.memset(code[:], 1.0).then_inc(consts, 1)
            nc.gpsimd.memset(emax[:], -BIG).then_inc(zeroed, 1)
            nc.gpsimd.memset(agg[:], 0.0).then_inc(zeroed, 1)
            nc.gpsimd.memset(token[:], 0.0).then_inc(zeroed, 1)
            pool.wait_ge(zeroed, START + 3)

            def step(i, j):
                if not there(i, j):
                    return
                q = j % RING
                done(pool, w_row_ok, i, j - RING)
                done(pool, idx_in, i, j, 16 * QUAD)
                settle(nc, pool, token, settled, i * RING + j)
                for m in range(QUAD):
                    nc.gpsimd.indirect_dma_start(
                        out=got[:, q, m, :], out_offset=None, in_=t["table"],
                        in_offset=bass.IndirectOffsetOnAxis(ap=idx[:, q, m, 0:1], axis=0)).then_inc(got_in[q], 16)

            steps(pool, step, 0)

        @block.tensor
        def _(pe):
            pe.wait_ge(w_ok, START + 48)
            pe.wait_ge(consts, START + 7)
            pe.wait_ge(dve_set, START + 2)
            nc.tensor.matmul(set_ps[0:NT, 0, 0:1], part[:, 0:NT], ones[0:EP, 0:1], start=True, stop=True)
            nc.tensor.matmul(set_ps[0:NT, 0, 1:2], part[:, 1:NT + 1], ones[0:EP, 0:1], start=True, stop=True).then_inc(pe_set, 1)
            pe.wait_ge(dve_set, START + 7)
            nc.tensor.matmul(set_ps[0:NT, 0, 2:3], below[0:NT, 0:NT], first[:, 2:3], start=True, stop=True).then_inc(pe_set, 1)
            pe.wait_ge(dve_set, START + 12)
            for c in range(2):
                cols = slice(c * HS, (c + 1) * HS)
                pe.wait_ge(dve_set, START + (12 if c == 0 else 13))
                nc.tensor.matmul(set_ps[0:1, 0, 0:HS], ones[0:NT, 0:1], at[:, cols], start=True, stop=True).then_inc(pe_set, 1)
                nc.tensor.matmul(set_ps[:, 1, 0:HS], tile_no[:], hot2[:, cols], start=True, stop=True).then_inc(pe_set, 1)
                pe.wait_ge(dve_set, START + 13 + 3 * c + 2)
            pe.wait_ge(dve_set, START + 20)
            nc.tensor.transpose(set_ps[0:8, 0, 0:P], top[:], ident[:]).then_inc(pe_set, 1)
            pe.wait_ge(dve_set, START + 21)
            nc.tensor.matmul(set_ps[0:1, 1, 0:8], top8[:], ident[0:8, 0:8], start=True, stop=True).then_inc(pe_set, 1)
            pe.wait_ge(dve_set, START + 26)
            nc.tensor.matmul(set_ps[:, 0, 0:1], ones[0:1, :], lift[:, 7:8], start=True, stop=True).then_inc(pe_set, 1)

            def turn(i, j):
                q, b = j % RING, j % 2
                done(pe, sel_ok, i, j)
                done(pe, selT_ok, i, j - 2)
                for m in range(QUAD):
                    last = nc.tensor.transpose(selT_ps[:, b, m * P:(m + 1) * P], sel[:, q, m, :], ident[:])
                last.then_inc(selT_mm[q], 1)

            def target_scores(i, j):
                q, b = j % RING, j % 2
                tiles = [pe.value_load(slot_tile[0:1, bass.ds((i * RING + j) * QUAD + m, 1)], min_val=0, max_val=NT - 1)
                         for m in range(QUAD)]
                done(pe, selT_ok, i, j)
                done(pe, pen_ok, i, j - 2)
                for m in range(QUAD):
                    last = nc.tensor.matmul(st_ps[:, b, m * CODE:(m + 1) * CODE], selT[:, q, m, :],
                                            code[:, bass.ds(tiles[m], 1), :], start=True, stop=True)
                last.then_inc(st_mm[q], 1)

            def sum_rows(i, j):
                q = j % RING
                done(pe, w_row_ok, i, j)
                for m in range(QUAD):
                    pe.wait_ge(acc_ok[m], START + i * RING + j)
                    nc.tensor.matmul(acc_ps[:, m, 0:D + HEADS], sel[:, q, m, :], wrow[:, q, m, :],
                                     start=True, stop=True).then_inc(acc_mm[m], 1)

            def step(i, j):
                for run, ahead in ((target_scores, 1), (turn, 2), (sum_rows, -1)):
                    if there(i, j + ahead):
                        run(i, j + ahead)

            steps(pe, step, 2)
            pe.wait_ge(fin, START + 1)
            nc.tensor.transpose(set_ps[0:1, 0, 0:P], top[:, 0:1], ident[:]).then_inc(pe_set, 1)
            pe.wait_ge(act_set, START + 1)
            nc.tensor.matmul(set_ps[:, 1, 0:1], ones[0:1, :], lift[:, 6:7], start=True, stop=True).then_inc(pe_set, 1)

        @block.scalar
        def _(act):
            act.wait_ge(dve_set, START + 27)

            def copy_turned(i, j):
                q, b = j % RING, j % 2
                done(act, selT_mm, i, j)
                done(act, st_mm, i, j - RING)
                nc.scalar.activation(selT[:, q].rearrange("p j n -> p (j n)"), selT_ps[:, b, :], ACT.Copy).then_inc(selT_ok[q], 1)

            def exponential(i, j):
                q = j % RING
                done(act, logit_ok, i, j)
                if there(i, j - RING):
                    act.wait_ge(acc_mm[QUAD - 1], START + i * RING + j - RING + 1)
                nc.scalar.activation(wrow[:, q, :, D:], logit[:, q], ACT.Exp, bias=shift[:]).then_inc(exp_ok[q], 1)

            def step(i, j):
                for run, ahead in ((exponential, 1), (copy_turned, 2)):
                    if there(i, j + ahead):
                        run(i, j + ahead)

            steps(act, step, 2)
            act.wait_ge(fin, START + 2)
            nc.scalar.activation(lift[:, 6:7], lift[:, 5:6], ACT.Exp, bias=shift[0:1, :]).then_inc(act_set, 1)

        @block.vector
        def _(dve):
            step = [0]

            def set_up(ins):
                step[0] += 1
                ins.then_inc(dve_set, 1)
                dve.wait_ge(dve_set, START + step[0])

            dve.wait_ge(w_ok, START + 48)
            dve.wait_ge(consts, START + 7)
            set_up(nc.vector.tensor_copy(dst_f[:], dst_i[:]))
            for b in range(NT + 1):
                last = nc.vector.scalar_tensor_tensor(less[:], dst_f[:], bound[0:EP, b:b + 1], ones_e[:], ALU.is_lt, ALU.mult,
                                                      accum_out=part[:, b:b + 1])
                if b < NT:
                    last.then_inc(emax_ok, 1)
                    dve.wait_ge(emax_ok, START + b + 1)
            set_up(last)
            dve.wait_ge(pe_set, START + 1)
            set_up(nc.vector.tensor_copy(first[:, 0:2], set_ps[0:NT, 0, 0:2]))
            set_up(nc.vector.scalar_tensor_tensor(first[:, 1:2], first[:, 0:1], -1.0, first[:, 1:2], ALU.mult, ALU.add))
            set_up(nc.vector.tensor_scalar(slots_i[:], first[:, 1:2], float(P - 1), None, ALU.add))
            set_up(nc.vector.tensor_single_scalar(slots_i[:], slots_i[:], 7, op=ALU.logical_shift_right))
            set_up(nc.vector.tensor_copy(first[:, 2:3], slots_i[:]))
            dve.wait_ge(pe_set, START + 2)
            set_up(nc.vector.tensor_copy(first[:, 3:4], set_ps[0:NT, 0, 2:3]))
            set_up(nc.vector.tensor_scalar(hot[:], kk[:], first[:, 3:4], None, ALU.is_ge))
            set_up(nc.vector.tensor_scalar(at[:], kk[:], first[:, 3:4], first[:, 2:3], ALU.subtract, ALU.subtract))
            set_up(nc.vector.scalar_tensor_tensor(hot2[:], at[:], 0.0, hot[:], ALU.is_lt, ALU.mult))
            nc.vector.tensor_scalar(hot[:], kk[:], first[:, 3:4], float(P), ALU.subtract, ALU.mult).then_inc(emax_ok, 1)
            dve.wait_ge(emax_ok, START + NT + 1)
            nc.vector.tensor_scalar(at[:], hot[:], first[:, 0:1], float(-E), ALU.add, ALU.add).then_inc(emax_ok, 1)
            dve.wait_ge(emax_ok, START + NT + 2)
            set_up(nc.vector.tensor_tensor(at[:], at[:], hot2[:], ALU.mult))
            for c in range(2):
                cols = slice(c * HS, (c + 1) * HS)
                dve.wait_ge(pe_set, START + 4 + 2 * c)
                set_up(nc.vector.tensor_scalar(slot_at[:, cols], set_ps[0:1, 0, 0:HS], float(E), None, ALU.add))
                set_up(nc.vector.tensor_scalar(slot_base[:, cols], set_ps[:, 1, 0:HS], float(P), None, ALU.mult))
                set_up(nc.vector.tensor_copy(slot_tile[:, cols], set_ps[0:1, 1, 0:HS]))
            dve.wait_ge(score_in, START + 16)
            set_up(nc.vector.tensor_copy(code[:, :, 0:HEADS], score[:, :, HEADS:]))
            set_up(nc.vector.tensor_reduce(top[:], score[:].rearrange("p i h -> p h i"), AX.X, ALU.max))
            dve.wait_ge(pe_set, START + 7)
            set_up(nc.vector.tensor_reduce(top8[:], set_ps[0:8, 0, 0:P], AX.X, ALU.max))
            dve.wait_ge(pe_set, START + 8)
            set_up(nc.vector.tensor_copy(lift[:], set_ps[0:1, 1, 0:8]))
            set_up(nc.vector.tensor_tensor(lift[:, 0:4], lift[:, 0:4], lift[:, 4:8], ALU.add))
            set_up(nc.vector.scalar_tensor_tensor(lift[:, 0:4], lift[:, 0:4], 0.2, lift[:, 0:4], ALU.mult, ALU.max))
            set_up(nc.vector.tensor_reduce(lift[:, 4:5], lift[:, 0:4], AX.X, ALU.max))
            set_up(nc.vector.tensor_scalar(lift[:, 7:8], lift[:, 4:5], -1.0, None, ALU.mult))
            dve.wait_ge(pe_set, START + 9)
            set_up(nc.vector.tensor_copy(shift[:], set_ps[:, 0, 0:1]))
            dve.wait_ge(zeroed, START + 2)

            def select(i, j):
                q = j % RING
                done(dve, idx_in, i, j, 16 * QUAD)
                nc.vector.tensor_tensor(rel[:, q], idx[:, q, :, 1], slot_base[:, bass.ds((i * RING + j) * QUAD, QUAD)],
                                        ALU.subtract).then_inc(rel_ok[q], 1)
                done(dve, rel_ok, i, j)
                if there(i, j - RING):
                    dve.wait_ge(acc_mm[QUAD - 1], START + i * RING + j - RING + 1)
                nc.vector.tensor_tensor(sel[:, q], count[:].unsqueeze(1).to_broadcast([P, QUAD, P]),
                                        rel[:, q].unsqueeze(2).to_broadcast([P, QUAD, P]), ALU.is_equal).then_inc(sel_ok[q], 1)

            def logits(i, j):
                q, b = j % RING, j % 2
                done(dve, st_mm, i, j)
                dve.wait_ge(got_in[q], 16 * QUAD * (i + j // RING + 1))
                st = st_ps[:, b, 0:QUAD * CODE].rearrange("p (j c) -> p j c", c=CODE)
                nc.vector.tensor_tensor(z[:, q], got[:, q, :, D:D + HEADS], st[:, :, 0:HEADS], ALU.add).then_inc(z_ok[q], 1)
                nc.vector.tensor_scalar(pen[:, q], st[:, :, HEADS], BIG, -BIG, ALU.mult, ALU.add).then_inc(pen_ok[q], 1)
                done(dve, z_ok, i, j)
                nc.vector.scalar_tensor_tensor(lr[:, q], z[:, q], 0.2, z[:, q], ALU.mult, ALU.max).then_inc(lr_ok[q], 1)
                done(dve, lr_ok, i, j)
                done(dve, pen_ok, i, j)
                done(dve, exp_ok, i, j - RING)
                nc.vector.tensor_tensor(logit[:, q], lr[:, q], pen[:, q].unsqueeze(2).to_broadcast([P, QUAD, HEADS]),
                                        ALU.add).then_inc(logit_ok[q], 1)
                done(dve, logit_ok, i, j)
                dve.wait_ge(emax_ok, START + i * RING + j + NT + 2)
                nc.vector.tensor_tensor(emax[:], emax[:], logit[:, q].rearrange("p j h -> p (j h)"), ALU.max).then_inc(emax_ok, 1)

            def weigh(i, j, m):
                q = j % RING
                done(dve, exp_ok, i, j)
                last = nc.vector.tensor_tensor(wrow[:, q, m, 0:D].rearrange("p (h f) -> p h f", h=HEADS),
                                               got[:, q, m, 0:D].rearrange("p (h f) -> p h f", h=HEADS),
                                               wrow[:, q, m, D:].unsqueeze(2).to_broadcast([P, HEADS, FO]), ALU.mult)
                if m == QUAD - 1:
                    last.then_inc(w_row_ok[q], 1)

            def add(i, j, m):
                n = i * RING + j
                tile = dve.value_load(slot_tile[0:1, bass.ds((i * RING + j) * QUAD + m, 1)], min_val=0, max_val=NT - 1)
                dve.wait_ge(acc_mm[m], START + n + 1)
                dve.wait_ge(acc_ok[m - 1], START + n + (1 if m else 0))
                here = agg[:, bass.ds(tile, 1), :].rearrange("p i f -> p (i f)")
                nc.vector.tensor_tensor(here, here, acc_ps[:, m, 0:D + HEADS], ALU.add).then_inc(acc_ok[m], 1)

            def step(i, j):
                for run, ahead in ((logits, 1), (select, 3)):
                    if there(i, j + ahead):
                        run(i, j + ahead)
                for m in range(QUAD):
                    if there(i, j - 1):
                        add(i, j - 1, m)
                    if there(i, j):
                        weigh(i, j, m)

            steps(dve, step, 3)
            dve.wait_ge(emax_ok, START + quads + NT + 2)
            nc.vector.tensor_reduce(top[:, 0:1], emax[:], AX.X, ALU.max).then_inc(fin, 1)
            dve.wait_ge(pe_set, START + 10)
            nc.vector.tensor_reduce(lift[:, 5:6], set_ps[0:1, 0, 0:P], AX.X, ALU.max).then_inc(fin, 1)
            dve.wait_ge(pe_set, START + 11)
            nc.vector.tensor_scalar(guard[:], set_ps[:, 1, 0:1], 1e-16, None, ALU.mult).then_inc(dve_set, 1)
            dve.wait_ge(dve_set, START + 28)
            for m in range(QUAD):
                dve.wait_ge(acc_ok[m], START + quads)
            nc.vector.tensor_scalar(den[:], agg[:, :, D:], guard[:], None, ALU.add).then_inc(dve_set, 1)
            dve.wait_ge(dve_set, START + 29)
            nc.vector.reciprocal(den[:], den[:]).then_inc(dve_set, 1)
            dve.wait_ge(dve_set, START + 30)
            for i in range(NT):
                mean = agg[:, i, 0:D].rearrange("p (h f) -> p h f", h=HEADS)
                last = nc.vector.tensor_tensor(mean, mean, den[:, i, :].unsqueeze(2).to_broadcast([P, HEADS, FO]), ALU.mult)
            last.then_inc(fin, 1)


EXPERTS = 8
ATT_EPS = 1e-6
LNS = 7
(LN_LOCAL, LN_GLOBAL, LN_MSG, LN_GNN, LN_MIX, LN_ROUTER, LN_EXPERT) = range(LNS)
LIN_USES = 22


def stage_mix(nc, a, t):
    with ExitStack() as ctx:
        ident = sb(nc, ctx, "x_ident", [P, P])
        inv_d = sb(nc, ctx, "x_inv_d", [P, P])
        w2 = {n: sb(nc, ctx, f"x_{n}", [P, H2, D]) for n in ("wlT", "wgT", "Wq", "Wm")}
        w_ff1 = sb(nc, ctx, "x_ff1", [P, H2, 2 * D])
        w_ff2 = sb(nc, ctx, "x_ff2", [P, 4, D])
        w_m1 = sb(nc, ctx, "x_m1", [P, 4, 2 * D])
        w_m2 = sb(nc, ctx, "x_m2", [P, 4, D])
        w_r = sb(nc, ctx, "x_wr", [P, H2, EXPERTS])
        b_r = sb(nc, ctx, "x_br", [TT, EXPERTS])
        vecs = sb(nc, ctx, "x_vecs", [P, H2, 12])
        b_ff1 = sb(nc, ctx, "x_bff1", [P, 4])
        eps = sb(nc, ctx, "x_eps", [P, 1])
        att_eps = sb(nc, ctx, "x_att_eps", [P, 1])
        same = sb(nc, ctx, "x_same", [P, P])
        kv = sb(nc, ctx, "x_kv", [P, H2, KROW])
        kv_blk = sb(nc, ctx, "x_kv_blk", [P, H2, P])
        ks_blk = sb(nc, ctx, "x_ks_blk", [P, H2, P])
        rank = sb(nc, ctx, "x_rank", [TT, NTT], I32)

        def two(name, shape):
            return [sb(nc, ctx, f"x_{name}{q}", shape) for q in range(2)]

        x, xn, low, up, hl, ha, cent, sq, qp, msg, gate, h, res, mix = (
            two(n, [P, H2, CH]) for n in "x xn low up hl ha cent sq qp msg gate h res mix".split())
        std, den = two("std", [P, CH]), two("den", [P, H2, CH])
        y_at = [sb(nc, ctx, f"x_y_at{q}", [TT, TILES], I32) for q in range(2)]
        arow, yrow, x2row, xerow = (two(n, [TT, TILES, D]) for n in ("arow", "yrow", "x2row", "xerow"))
        wide = two("wide", [P, 4, CH])
        logit = two("logit", [TT, TILES, EXPERTS])
        mean_ps = [ps(nc, ctx, f"x_mean_ps{q}", [P, 512]) for q in range(2)]
        var_ps = [ps(nc, ctx, f"x_var_ps{q}", [P, 512]) for q in range(2)]
        lin_ps = [[ps(nc, ctx, f"x_lin_ps{q}{b}", [P, 512]) for b in range(2)] for q in range(2)]
        token = sb(nc, ctx, "x_token", [P, 2])
        settled, passed, w_ok, consts, token_ok, blk_ok = sems(nc, ctx, "x", "settled passed w_ok consts token_ok blk_ok")
        (arow_in, xn_in, x_in, y_at_ok, y_in, low_ok, up_ok, exp_ok, elu_ok, qlow_ok, qexp_ok, den_ok, diff_ok, gated_ok, h_ok,
         sum1_ok, sum2_ok, x2_ok, sq_ok, log_ok, norm_ok, gain_ok, stored) = (
            sems(nc, ctx, "x", f"{n}0 {n}1") for n in
            "arow_in xn_in x_in y_at_ok y_in low_ok up_ok exp_ok elu_ok qlow_ok qexp_ok den_ok diff_ok gated_ok h_ok "
            "sum1_ok sum2_ok x2_ok sq_ok log_ok norm_ok gain_ok stored".split())
        mean_full, mean_read, var_full, var_read = (
            sems(nc, ctx, "x", f"{n}0 {n}1") for n in "mean_full mean_read var_full var_read".split())
        lin_full = [sems(nc, ctx, "x", f"lin_full{q}0 lin_full{q}1") for q in range(2)]
        lin_read = [sems(nc, ctx, "x", f"lin_read{q}0 lin_read{q}1") for q in range(2)]
        MEAN_USES = 1 + LNS + 1
        VAR_USES = 1 + LNS
        BANK_USES = 1 + LIN_USES // 2 + TILES
        pairs = NCH // 2
        Q_, Y_ROWS, DEN, NUM, GATE, WM, FF1, FF2, M1, M2 = -2, 0, 2, 4, 6, 8, 10, 14, 16, 20
        block = ctx.enter_context(nc.Block())

        def v(n, k):
            return vecs[:, k, n:n + 1]

        def chunk(i, q):
            return bass.ds((i * 2 + q) * CH, CH)

        @block.sync
        def _(sp):
            loads = [(ident[:], a["ident"]), (w_ff1[:], halves(a["ff1T"])), (w_ff2[:], a["ff2T"].rearrange("(h p) n -> p h n", p=P)),
                     (w_m1[:], a["W1"].rearrange("(h p) n -> p h n", p=P)), (w_m2[:], a["W2"].rearrange("(h p) n -> p h n", p=P)),
                     (w_r[:], halves(a["Wr"])), (b_r[:], a["br"].unsqueeze(0).to_broadcast([TT, EXPERTS])),
                     (vecs[:], halves(a["mix_vecs"])), (b_ff1[:], a["ff1_b"]),
                     (same[:], a["same"]), (kv[:], t["kv"])]
            loads += [(w2[n][:], halves(a[n])) for n in w2]
            assert len(loads) == 15
            for dst, source in loads:
                sp.dma_start(dst, source).then_inc(w_ok, 16)
            with nc.allow_non_contiguous_dma(reason="one rank per partition and token tile"):
                sp.dma_start(rank[:], t["rank"].rearrange("(i p) -> p i", p=TT)).then_inc(w_ok, 16)

            def load(i, q, buf, source, done):
                sp.dma_start(buf[q][:], source).then_inc(done[q], 16)

            def load_agg(i, q):
                load(i, q, arow, t["agg"][chunk(i, q), :].rearrange("(j p) f -> p j f", p=TT), arow_in)

            def load_xn(i, q):
                load(i, q, xn, halves(t["xnT"])[:, :, chunk(i, q)], xn_in)

            def load_x(i, q):
                load(i, q, x, halves(a["xT"])[:, :, chunk(i, q)], x_in)

            def store(i):
                for q in range(2):
                    sp.wait_ge(mean_read[q], START + MEAN_USES * (i + 1))
                    sp.dma_start(t["logit"][chunk(i, q), :].rearrange("(j p) f -> p j f", p=TT), logit[q][:]).then_inc(stored[q], 16)
                    sp.wait_ge(lin_read[q][0], START + BANK_USES * (i + 1))
                    sp.dma_start(t["x2"][chunk(i, q), :].rearrange("(j p) f -> p j f", p=TT), x2row[q][:]).then_inc(stored[q], 16)
                    sp.wait_ge(lin_read[q][1], START + BANK_USES * (i + 1))
                    sp.dma_start(t["xe"][chunk(i, q), :].rearrange("(j p) f -> p j f", p=TT), xerow[q][:]).then_inc(stored[q], 16)

            for q in range(2):
                load_agg(0, q)
                load_xn(0, q)
                load_x(0, q)
            with sp.Fori(0, pairs - 1) as i:
                for q in range(2):
                    sp.wait_ge(var_full[q], START + VAR_USES * i + 1)
                    sp.sem_inc(passed, 1)
                    load_agg(i + 1, q)
                for q in range(2):
                    sp.wait_ge(norm_ok[q], START + LNS * i + LN_MIX + 1)
                    sp.sem_inc(passed, 1)
                    load_xn(i + 1, q)
                for q in range(2):
                    sp.wait_ge(lin_full[q][0], START + BANK_USES * (i + 1))
                    sp.sem_inc(passed, 1)
                    load_x(i + 1, q)
                store(i)
            store(pairs - 1)
            for q in range(2):
                sp.wait_ge(stored[q], START + 48 * pairs)

        @block.gpsimd
        def _(pool):
            nc.gpsimd.memset(inv_d[:], 1.0 / D).then_inc(consts, 1)
            nc.gpsimd.memset(eps[:], LN_EPS).then_inc(consts, 1)
            nc.gpsimd.memset(att_eps[:], ATT_EPS).then_inc(consts, 1)
            nc.gpsimd.memset(token[:], 0.0).then_inc(token_ok, 1)
            pool.wait_ge(token_ok, START + 1)
            with pool.Fori(0, pairs) as i:
                for q in range(2):
                    pool.wait_ge(y_at_ok[q], START + i + 1)
                    settle(nc, pool, token, settled, 2 * i + q)
                    for j in range(TILES):
                        nc.gpsimd.indirect_dma_start(
                            out=yrow[q][:, j, :], out_offset=None, in_=t["y"],
                            in_offset=bass.IndirectOffsetOnAxis(ap=y_at[q][:, j:j + 1], axis=0)).then_inc(y_in[q], 16)

        @block.tensor
        def _(pe):
            pe.wait_ge(w_ok, START + 256)
            pe.wait_ge(consts, START + 3)
            pe.wait_ge(blk_ok, START + 4)
            with pe.Fori(0, pairs) as i:
                def lin(q, u, products):
                    b, n = u % 2, u // 2 + 1
                    pe.wait_ge(lin_read[q][b], START + BANK_USES * i + n)
                    for m, (w, r) in enumerate(products):
                        last = nc.tensor.matmul(lin_ps[q][b][:, 0:CH], w, r, start=(m == 0), stop=(m == len(products) - 1))
                    last.then_inc(lin_full[q][b], 1)

                def dense(q, u, weights, inputs, outs):
                    for m in range(outs):
                        lin(q, u + m, [(w[:, k, m * P:(m + 1) * P], r) for (w, k), r in zip(weights, inputs)])

                def written(q, u):
                    pe.wait_ge(lin_read[q][u % 2], START + BANK_USES * i + u // 2 + 2)

                def mean_of(q, n, src):
                    pe.wait_ge(mean_read[q], START + MEAN_USES * i + 1 + n)
                    for k in range(H2):
                        last = nc.tensor.matmul(mean_ps[q][:, 0:CH], inv_d[:], src[q][:, k, :], start=(k == 0), stop=(k == 1))
                    last.then_inc(mean_full[q], 1)

                def var_of(n):
                    for q in TWO:
                        pe.wait_ge(sq_ok[q], START + LNS * i + n + 1)
                        pe.wait_ge(var_read[q], START + VAR_USES * i + 1 + n)
                        for k in range(H2):
                            last = nc.tensor.matmul(var_ps[q][:, 0:CH], inv_d[:], sq[q][:, k, :], start=(k == 0), stop=(k == 1))
                        last.then_inc(var_full[q], 1)

                def xh(buf, q):
                    return [buf[q][:, k, :] for k in range(buf[q].shape[1])]

                TWO = range(2)
                for q in TWO:
                    pe.wait_ge(arow_in[q], START + 16 * (i + 1))
                    for k, (bank, read, uses, full) in enumerate(((mean_ps, mean_read, MEAN_USES, mean_full),
                                                                  (var_ps, var_read, VAR_USES, var_full))):
                        pe.wait_ge(read[q], START + uses * i)
                        for j in range(TILES):
                            last = nc.tensor.transpose(bank[q][:, j * TT:(j + 1) * TT], arow[q][:, j, k * P:(k + 1) * P], ident[0:TT, 0:TT])
                        last.then_inc(full[q], 1)
                for q in TWO:
                    pe.wait_ge(xn_in[q], START + 16 * (i + 1))
                    dense(q, Q_, [(w2["Wq"], 0), (w2["Wq"], 1)], xh(xn, q), 2)
                for q in TWO:
                    pe.wait_ge(elu_ok[q], START + i + 1)
                    mean_of(q, LN_LOCAL, hl)
                var_of(LN_LOCAL)
                for q in TWO:
                    pe.wait_ge(y_in[q], 64 * (i + 1))
                    for k in range(H2):
                        pe.wait_ge(lin_read[q][k], START + BANK_USES * i + Y_ROWS // 2 + 1)
                        for j in range(TILES):
                            last = nc.tensor.transpose(lin_ps[q][k][:, j * TT:(j + 1) * TT], yrow[q][:, j, k * P:(k + 1) * P], ident[0:TT, 0:TT])
                        last.then_inc(lin_full[q][k], 1)
                for q in TWO:
                    for k in range(H2):
                        written(q, Y_ROWS + k)
                    mean_of(q, LN_GLOBAL, ha)
                for q in TWO:
                    for k in range(H2):
                        lin(q, DEN + k, [(ks_blk[:, k, :], qp[q][:, k, :])])
                for q in TWO:
                    for k in range(H2):
                        lin(q, NUM + k, [(kv_blk[:, k, :], qp[q][:, k, :])])
                var_of(LN_GLOBAL)
                for q in TWO:
                    pe.wait_ge(gain_ok[q], START + 5 * i + 2)
                    dense(q, GATE, [(w2["wlT"], 0), (w2["wlT"], 1), (w2["wgT"], 0), (w2["wgT"], 1)], xh(hl, q) + xh(ha, q), 2)
                for q in TWO:
                    for k in range(H2):
                        written(q, NUM + k)
                    dense(q, WM, [(w2["Wm"], 0), (w2["Wm"], 1)], xh(msg, q), 2)
                for q in TWO:
                    pe.wait_ge(h_ok[q], START + i + 1)
                    dense(q, FF1, [(w_ff1, 0), (w_ff1, 1)], xh(h, q), 4)
                for q in TWO:
                    written(q, WM)
                    written(q, WM + 1)
                    mean_of(q, LN_MSG, qp)
                for q in TWO:
                    for u in (FF1 + 2, FF1 + 3):
                        written(q, u)
                    dense(q, FF2, [(w_ff2, k) for k in range(4)], xh(wide, q), 2)
                var_of(LN_MSG)
                for q in TWO:
                    for u in (FF2, FF2 + 1):
                        written(q, u)
                    mean_of(q, LN_GNN, res)
                for q in TWO:
                    pe.wait_ge(gain_ok[q], START + 5 * i + 3)
                    dense(q, M1, [(w_m1, k) for k in range(4)], xh(xn, q) + xh(msg, q), 4)
                var_of(LN_GNN)
                for q in TWO:
                    for u in (M1 + 2, M1 + 3):
                        written(q, u)
                    dense(q, M2, [(w_m2, k) for k in range(4)], xh(wide, q), 2)
                for q in TWO:
                    for u in (M2, M2 + 1):
                        written(q, u)
                    mean_of(q, LN_MIX, mix)
                var_of(LN_MIX)
                for q in TWO:
                    pe.wait_ge(x2_ok[q], START + i + 1)
                    mean_of(q, LN_ROUTER, x)
                var_of(LN_ROUTER)
                for q in TWO:
                    pe.wait_ge(norm_ok[q], START + LNS * i + LN_ROUTER + 1)
                    mean_of(q, LN_EXPERT, ha)
                var_of(LN_EXPERT)
                for q in TWO:
                    pe.wait_ge(mean_read[q], START + MEAN_USES * i + 1 + LNS)
                    for j in range(TILES):
                        for k in range(H2):
                            last = nc.tensor.matmul(mean_ps[q][0:TT, j * EXPERTS:(j + 1) * EXPERTS], ha[q][:, k, j * TT:(j + 1) * TT],
                                                    w_r[:, k, :], start=(k == 0), stop=(k == 1))
                    last.then_inc(mean_full[q], 1)
                for q in TWO:
                    pe.wait_ge(norm_ok[q], START + LNS * i + LNS)
                    for j in range(TILES):
                        for n, src in enumerate((x, hl)):
                            pe.wait_ge(lin_read[q][n], START + BANK_USES * i + 1 + LIN_USES // 2 + j)
                            for k in range(H2):
                                last = nc.tensor.transpose(lin_ps[q][n][0:TT, k * P:(k + 1) * P], src[q][:, k, j * TT:(j + 1) * TT], ident[:])
                            last.then_inc(lin_full[q][n], 1)

        def full(eng, q, u, i):
            eng.wait_ge(lin_full[q][u % 2], START + BANK_USES * i + u // 2 + 2)

        @block.scalar
        def _(act):
            act.wait_ge(consts, START + 3)
            act.wait_ge(w_ok, START + 256)
            with act.Fori(0, pairs) as i:
                TWO = range(2)

                def square(n):
                    for q in TWO:
                        act.wait_ge(mean_read[q], START + MEAN_USES * i + n + 2)
                        act.wait_ge(var_full[q], START + VAR_USES * i + 1 + n)
                        nc.scalar.activation(sq[q][:], cent[q][:], ACT.Square).then_inc(sq_ok[q], 1)

                def root(n):
                    for q in TWO:
                        act.wait_ge(var_full[q], START + VAR_USES * i + n + 2)
                        act.wait_ge(norm_ok[q], START + LNS * i + n)
                        nc.scalar.activation(std[q][:], var_ps[q][:, 0:CH], ACT.Ln, bias=eps[:]).then_inc(log_ok[q], 1)
                    for q in TWO:
                        act.wait_ge(log_ok[q], START + LNS * i + n + 1)
                        nc.scalar.activation(std[q][:], std[q][:], ACT.Exp, scale=-0.5).then_inc(var_read[q], 1)

                def affine(n, buf, gained):
                    for q in TWO:
                        act.wait_ge(norm_ok[q], START + LNS * i + n + 1)
                        for k in range(H2):
                            last = nc.scalar.activation(buf[q][:, k, :], buf[q][:, k, :], ACT.Identity,
                                                        scale=v(2 + 2 * gained, k), bias=v(3 + 2 * gained, k))
                        last.then_inc(gain_ok[q], 1)

                def drain(u, outs, dst, func, bias=None):
                    for q in TWO:
                        for m in range(outs):
                            full(act, q, u + m, i)
                            kw = {} if bias is None else {"bias": bias[:, m:m + 1]}
                            nc.scalar.activation(dst[q][:, m, :], lin_ps[q][(u + m) % 2][:, 0:CH], func, **kw).then_inc(
                                lin_read[q][(u + m) % 2], 1)

                for q in TWO:
                    act.wait_ge(low_ok[q], START + i + 1)
                    nc.scalar.activation(low[q][:], low[q][:], ACT.Exp).then_inc(exp_ok[q], 1)
                for q in TWO:
                    act.wait_ge(qlow_ok[q], START + 2 * i + 2)
                    nc.scalar.activation(msg[q][:], msg[q][:], ACT.Exp).then_inc(qexp_ok[q], 1)
                square(LN_LOCAL)
                root(LN_LOCAL)
                affine(LN_LOCAL, hl, 0)
                square(LN_GLOBAL)
                for q in TWO:
                    for k in range(H2):
                        full(act, q, DEN + k, i)
                        nc.scalar.activation(den[q][:, k, :], lin_ps[q][k][:, 0:CH], ACT.Ln, bias=att_eps[:]).then_inc(lin_read[q][k], 1)
                for q in TWO:
                    for k in range(H2):
                        act.wait_ge(lin_read[q][k], START + BANK_USES * i + DEN // 2 + 2)
                    nc.scalar.activation(den[q][:], den[q][:], ACT.Exp, scale=-1.0).then_inc(den_ok[q], 1)
                root(LN_GLOBAL)
                affine(LN_GLOBAL, ha, 1)
                drain(GATE, 2, gate, ACT.Sigmoid)
                drain(WM, 2, qp, ACT.Copy)
                drain(FF1, 4, wide, ACT.Relu, b_ff1)
                square(LN_MSG)
                root(LN_MSG)
                affine(LN_MSG, msg, 2)
                square(LN_GNN)
                for q in TWO:
                    full(act, q, FF2 + 1, i)
                drain(M1, 4, wide, ACT.Relu)
                root(LN_GNN)
                affine(LN_GNN, res, 3)
                drain(M2, 2, mix, ACT.Copy)
                square(LN_MIX)
                root(LN_MIX)
                affine(LN_MIX, mix, 4)
                square(LN_ROUTER)
                root(LN_ROUTER)
                square(LN_EXPERT)
                root(LN_EXPERT)
                for q in TWO:
                    for j in range(TILES):
                        act.wait_ge(lin_full[q][1], START + BANK_USES * i + 1 + LIN_USES // 2 + j + 1)
                        act.wait_ge(stored[q], START + 48 * i)
                        nc.scalar.activation(xerow[q][:, j, :], lin_ps[q][1][0:TT, 0:D], ACT.Copy).then_inc(lin_read[q][1], 1)

        @block.vector
        def _(dve):
            dve.wait_ge(w_ok, START + 256)
            for k in range(H2):
                nc.vector.tensor_tensor(kv_blk[:, k, :], kv[:, k, 0:P], same[:], ALU.mult).then_inc(blk_ok, 1)
                nc.vector.tensor_scalar(ks_blk[:, k, :], same[:], kv[:, k, P:KROW], None, ALU.mult).then_inc(blk_ok, 1)
            with dve.Fori(0, pairs) as i:
                TWO = range(2)

                def centre(n, src):
                    for q in TWO:
                        dve.wait_ge(mean_full[q], START + MEAN_USES * i + n + 2)
                        dve.wait_ge(norm_ok[q], START + LNS * i + n)
                        nc.vector.tensor_tensor(cent[q][:], src[q][:], over_halves(mean_ps[q][:, 0:CH]), ALU.subtract).then_inc(mean_read[q], 1)

                def norm(n, dst):
                    for q in TWO:
                        dve.wait_ge(var_read[q], START + VAR_USES * i + n + 2)
                        nc.vector.tensor_tensor(dst[q][:], cent[q][:], over_halves(std[q][:]), ALU.mult).then_inc(norm_ok[q], 1)

                for q in TWO:
                    nc.vector.tensor_copy(y_at[q][:], rank[:, bass.ds((i * 2 + q) * TILES, TILES)]).then_inc(y_at_ok[q], 1)
                for q in TWO:
                    dve.wait_ge(xn_in[q], START + 16 * (i + 1))
                    for k, (bank, ready, uses, read) in enumerate(((mean_ps, mean_full, MEAN_USES, mean_read),
                                                                   (var_ps, var_full, VAR_USES, var_read))):
                        dve.wait_ge(ready[q], START + uses * i + 1)
                        nc.vector.scalar_tensor_tensor(up[q][:, k, :], bank[q][:, 0:CH], v(0, k), xn[q][:, k, :],
                                                       ALU.add, ALU.add).then_inc(read[q], 1)
                for q in TWO:
                    dve.wait_ge(mean_read[q], START + MEAN_USES * i + 1)
                    dve.wait_ge(var_read[q], START + VAR_USES * i + 1)
                    nc.vector.tensor_scalar(low[q][:], up[q][:], 0.0, None, ALU.min).then_inc(low_ok[q], 1)
                    dve.wait_ge(low_ok[q], START + i + 1)
                    nc.vector.tensor_scalar(up[q][:], up[q][:], 0.0, -1.0, ALU.max, ALU.add).then_inc(up_ok[q], 1)
                for q in TWO:
                    for k in range(H2):
                        full(dve, q, Q_ + k, i)
                        nc.vector.tensor_scalar(msg[q][:, k, :], lin_ps[q][k][:, 0:CH], 0.0, None, ALU.min).then_inc(qlow_ok[q], 1)
                for q in TWO:
                    dve.wait_ge(up_ok[q], START + i + 1)
                    dve.wait_ge(exp_ok[q], START + i + 1)
                    nc.vector.tensor_tensor(hl[q][:], up[q][:], low[q][:], ALU.add).then_inc(elu_ok[q], 1)
                for q in TWO:
                    dve.wait_ge(qexp_ok[q], START + i + 1)
                    for k in range(H2):
                        nc.vector.scalar_tensor_tensor(qp[q][:, k, :], lin_ps[q][k][:, 0:CH], 0.0, msg[q][:, k, :],
                                                       ALU.max, ALU.add).then_inc(lin_read[q][k], 1)
                centre(LN_LOCAL, hl)
                for q in TWO:
                    for k in range(H2):
                        full(dve, q, Y_ROWS + k, i)
                        nc.vector.tensor_tensor(ha[q][:, k, :], lin_ps[q][k][:, 0:CH], xn[q][:, k, :], ALU.add).then_inc(lin_read[q][k], 1)
                norm(LN_LOCAL, hl)
                centre(LN_GLOBAL, ha)
                for q in TWO:
                    for k in range(H2):
                        dve.wait_ge(den_ok[q], START + i + 1)
                        full(dve, q, NUM + k, i)
                        nc.vector.tensor_tensor(msg[q][:, k, :], lin_ps[q][k][:, 0:CH], den[q][:, k, :], ALU.mult).then_inc(lin_read[q][k], 1)
                norm(LN_GLOBAL, ha)
                for q in TWO:
                    dve.wait_ge(gain_ok[q], START + 5 * i + 2)
                    nc.vector.tensor_tensor(low[q][:], hl[q][:], ha[q][:], ALU.subtract).then_inc(diff_ok[q], 1)
                    for k in range(H2):
                        dve.wait_ge(lin_read[q][k], START + BANK_USES * i + GATE // 2 + 2)
                    dve.wait_ge(diff_ok[q], START + i + 1)
                    nc.vector.tensor_tensor(gate[q][:], gate[q][:], low[q][:], ALU.mult).then_inc(gated_ok[q], 1)
                    dve.wait_ge(gated_ok[q], START + i + 1)
                    nc.vector.tensor_tensor(h[q][:], gate[q][:], ha[q][:], ALU.add).then_inc(h_ok[q], 1)
                centre(LN_MSG, qp)
                for q in TWO:
                    for k in range(H2):
                        full(dve, q, FF2 + k, i)
                        nc.vector.scalar_tensor_tensor(res[q][:, k, :], lin_ps[q][k][:, 0:CH], v(1, k), h[q][:, k, :],
                                                       ALU.add, ALU.add).then_inc(lin_read[q][k], 1)
                norm(LN_MSG, msg)
                centre(LN_GNN, res)
                norm(LN_GNN, res)
                for q in TWO:
                    dve.wait_ge(x_in[q], START + 16 * (i + 1))
                    nc.vector.tensor_tensor(x[q][:], x[q][:], xn[q][:], ALU.add).then_inc(sum1_ok[q], 1)
                    dve.wait_ge(gain_ok[q], START + 5 * i + 4)
                    dve.wait_ge(sum1_ok[q], START + i + 1)
                    nc.vector.tensor_tensor(x[q][:], x[q][:], res[q][:], ALU.add).then_inc(sum2_ok[q], 1)
                centre(LN_MIX, mix)
                norm(LN_MIX, mix)
                for q in TWO:
                    dve.wait_ge(gain_ok[q], START + 5 * i + 5)
                    dve.wait_ge(sum2_ok[q], START + i + 1)
                    nc.vector.tensor_tensor(x[q][:], x[q][:], mix[q][:], ALU.add).then_inc(x2_ok[q], 1)
                centre(LN_ROUTER, x)
                norm(LN_ROUTER, ha)
                centre(LN_EXPERT, ha)
                norm(LN_EXPERT, hl)
                for q in TWO:
                    dve.wait_ge(mean_full[q], START + MEAN_USES * (i + 1))
                    dve.wait_ge(stored[q], START + 48 * i)
                    nc.vector.tensor_tensor(logit[q][:], mean_ps[q][0:TT, 0:TILES * EXPERTS].rearrange("p (j e) -> p j e", j=TILES),
                                            b_r[:].unsqueeze(1).to_broadcast([TT, TILES, EXPERTS]), ALU.add).then_inc(mean_read[q], 1)
                for q in TWO:
                    for j in range(TILES):
                        dve.wait_ge(lin_full[q][0], START + BANK_USES * i + 1 + LIN_USES // 2 + j + 1)
                        nc.vector.tensor_copy(x2row[q][:, j, :], lin_ps[q][0][0:TT, 0:D]).then_inc(lin_read[q][0], 1)


TOP = 2
XSLOTS = -(-((N * TOP + EXPERTS * (P - 1)) // P) // 2) * 2
FAR = 1e6


def stage_route(nc, a, t):
    with ExitStack() as ctx:
        shape = [TT, NTT, EXPERTS]
        logit, rest, mark, hot1, hot2, both, inner, upto, pos = (
            sb(nc, ctx, f"o_{n}", shape) for n in "logit rest mark hot1 hot2 both inner upto pos".split())
        valid, first, second, m1, m2, diff, w1, w2, invalid, p1, p2 = (
            sb(nc, ctx, f"o_{n}", [TT, NTT]) for n in "valid first second m1 m2 diff w1 w2 invalid p1 p2".split())
        below = sb(nc, ctx, "o_below", [P, P])
        ones = sb(nc, ctx, "o_ones", [TT, NTT * EXPERTS])
        order = sb(nc, ctx, "o_order", [TT, EXPERTS])
        tiles_i = sb(nc, ctx, "o_tiles_i", [TT, EXPERTS], I32)
        tiles, ends, base = (sb(nc, ctx, f"o_{n}", [TT, EXPERTS]) for n in ("tiles", "ends", "base"))
        slot = sb(nc, ctx, "o_slot", [1, XSLOTS])
        slot_e = sb(nc, ctx, "o_slot_e", [1, XSLOTS])
        slot_i = sb(nc, ctx, "o_slot_i", [1, XSLOTS], I32)
        send = [sb(nc, ctx, f"o_send{c}", [TT, NTT], I32) for c in range(TOP)]
        fetch = [sb(nc, ctx, f"o_fetch{c}", [TT, NTT], I32) for c in range(TOP)]
        to = [sb(nc, ctx, f"o_to{q}", [TT, TOP, TILES], I32) for q in range(2)]
        rows = [sb(nc, ctx, f"o_rows{q}", [TT, TILES, D]) for q in range(2)]
        zeros = sb(nc, ctx, "o_zeros", [P, D])
        inner_ps = ps(nc, ctx, "o_inner_ps", [P, 512])
        total_ps = ps(nc, ctx, "o_total_ps", [P, 512])
        token = sb(nc, ctx, "o_token", [P, 2])
        settled, loaded, consts, token_ok, step_ok, counted, emptied, exp_ok, saved = sems(
            nc, ctx, "o", "settled loaded consts token_ok step_ok counted emptied exp_ok saved")
        rows_in, to_ok, sent = (sems(nc, ctx, "o", f"{n}0 {n}1") for n in "rows_in to_ok sent".split())
        pairs = NCH // 2
        XSTEPS = 14
        block = ctx.enter_context(nc.Block())

        def each(ap):
            return ap.unsqueeze(2).to_broadcast(shape)

        @block.sync
        def _(sp):
            for dst, source in ((logit[:], t["logit"].rearrange("(i p) e -> p i e", p=TT)), (valid[:], a["valid"]), (below[:], a["below"])):
                sp.dma_start(dst, source).then_inc(loaded, 16)
            sp.wait_ge(consts, START + 4)
            sp.dma_start(t["xd"].rearrange("(s p) f -> p s f", p=P), zeros[:].unsqueeze(1).to_broadcast([P, XSLOTS, D])).then_inc(emptied, 16)
            for q in range(2):
                sp.dma_start(rows[q][:], t["xe"][q * CH:(q + 1) * CH, :].rearrange("(j p) f -> p j f", p=TT)).then_inc(rows_in[q], 16)
            with sp.Fori(1, pairs) as i:
                for q in range(2):
                    sp.wait_ge(sent[q], 16 * TOP * TILES * i)
                    sp.dma_start(rows[q][:], t["xe"][bass.ds((i * 2 + q) * CH, CH), :].rearrange("(j p) f -> p j f", p=TT)).then_inc(rows_in[q], 16)
            sp.wait_ge(counted, START + 2)
            for dst, source in ((t["fetch0"], fetch[0]), (t["fetch1"], fetch[1]), (t["w1"], w1), (t["w2"], w2), (t["slot_e"], slot_i)):
                sp.dma_start(dst, source[:]).then_inc(saved, 16)
            sp.wait_ge(saved, START + 80)
            for q in range(2):
                sp.wait_ge(sent[q], 16 * TOP * TILES * pairs)

        @block.gpsimd
        def _(pool):
            nc.gpsimd.iota(order[:], [[-1, EXPERTS]], base=EXPERTS, channel_multiplier=0, allow_small_or_imprecise_dtypes=True).then_inc(consts, 1)
            nc.gpsimd.iota(slot[:], [[1, XSLOTS]], base=0, channel_multiplier=0, allow_small_or_imprecise_dtypes=True).then_inc(consts, 1)
            nc.gpsimd.memset(ones[:], 1.0).then_inc(consts, 1)
            nc.gpsimd.memset(zeros[:], 0.0).then_inc(consts, 1)
            nc.gpsimd.memset(token[:], 0.0).then_inc(token_ok, 1)
            pool.wait_ge(token_ok, START + 1)
            pool.wait_ge(emptied, START + 16)
            with pool.Fori(0, pairs) as i:
                for q in range(2):
                    pool.wait_ge(rows_in[q], START + 16 * (i + 1))
                    pool.wait_ge(to_ok[q], START + TOP * (i + 1))
                    settle(nc, pool, token, settled, 2 * i + q)
                    for c in range(TOP):
                        for j in range(TILES):
                            nc.gpsimd.indirect_dma_start(
                                out=t["xd"], out_offset=bass.IndirectOffsetOnAxis(ap=to[q][:, c, j:j + 1], axis=0),
                                in_=rows[q][:, j, :], in_offset=None, bounds_check=XSLOTS * P - 1, oob_is_err=False).then_inc(sent[q], 16)

        @block.tensor
        def _(pe):
            pe.wait_ge(loaded, START + 48)
            pe.wait_ge(counted, START + 1)
            flat = both[:].rearrange("p i e -> p (i e)")
            nc.tensor.matmul(inner_ps[0:TT, 0:NTT * EXPERTS], below[0:TT, 0:TT], flat, start=True, stop=True)
            nc.tensor.matmul(total_ps[0:TT, 0:NTT * EXPERTS], ones[:, 0:TT], flat, start=True, stop=True).then_inc(exp_ok, 1)

        @block.scalar
        def _(act):
            act.wait_ge(step_ok, START + XSTEPS)
            nc.scalar.activation(w2[:], diff[:], ACT.Exp).then_inc(exp_ok, 1)

        @block.vector
        def _(dve):
            n = [0]

            def go(ins):
                n[0] += 1
                ins.then_inc(step_ok, 1)
                dve.wait_ge(step_ok, START + n[0])

            V = nc.vector
            dve.wait_ge(loaded, START + 48)
            dve.wait_ge(consts, START + 4)
            rank_of = order[:].unsqueeze(1).to_broadcast(shape)
            for l, m, f, hot in ((logit, m1, first, hot1), (rest, m2, second, hot2)):
                go(V.tensor_reduce(m[:], l[:], AX.X, ALU.max))
                go(V.tensor_tensor(mark[:], l[:], each(m[:]), ALU.is_equal))
                go(V.tensor_tensor(mark[:], mark[:], rank_of, ALU.mult))
                go(V.tensor_reduce(f[:], mark[:], AX.X, ALU.max))
                go(V.tensor_tensor(hot[:], each(f[:]), rank_of, ALU.is_equal))
                if hot is hot1:
                    go(V.scalar_tensor_tensor(rest[:].rearrange("p i e -> p (i e)"), hot1[:].rearrange("p i e -> p (i e)"), -BIG,
                                              logit[:].rearrange("p i e -> p (i e)"), ALU.mult, ALU.add))
            go(V.tensor_tensor(both[:], hot1[:], hot2[:], ALU.add))
            both_done = V.tensor_tensor(both[:], both[:], each(valid[:]), ALU.mult)
            both_done.then_inc(counted, 1)
            go(V.tensor_tensor(diff[:], m2[:], m1[:], ALU.subtract))
            go(V.tensor_scalar(invalid[:], valid[:], -FAR, FAR, ALU.mult, ALU.add))
            dve.wait_ge(exp_ok, START + 2)
            go(V.tensor_scalar(diff[:], w2[:], 1.0, None, ALU.add))
            go(V.reciprocal(w1[:], diff[:]))
            go(V.tensor_tensor(w2[:], w2[:], w1[:], ALU.mult))
            flat = "p i e -> p (i e)"
            go(V.tensor_copy(inner[:].rearrange(flat), inner_ps[0:TT, 0:NTT * EXPERTS]))
            go(V.tensor_copy(mark[:].rearrange(flat), total_ps[0:TT, 0:NTT * EXPERTS]))
            for e in range(EXPERTS):
                go(V.tensor_tensor_scan(upto[:, :, e], ones[:, 0:NTT], mark[:, :, e], 0.0, ALU.mult, ALU.add))
            go(V.tensor_scalar(tiles_i[:], upto[:, NTT - 1, :], float(P - 1), None, ALU.add))
            go(V.tensor_single_scalar(tiles_i[:], tiles_i[:], 7, op=ALU.logical_shift_right))
            go(V.tensor_copy(tiles[:], tiles_i[:]))
            go(V.tensor_tensor_scan(ends[:], ones[:, 0:EXPERTS], tiles[:], 0.0, ALU.mult, ALU.add))
            go(V.tensor_tensor(base[:], ends[:], tiles[:], ALU.subtract))
            go(V.tensor_scalar(base[:], base[:], float(P), None, ALU.mult))
            go(V.tensor_tensor(pos[:], upto[:], mark[:], ALU.subtract))
            go(V.tensor_tensor(pos[:], pos[:], inner[:], ALU.add))
            go(V.tensor_tensor(pos[:], pos[:], base[:].unsqueeze(1).to_broadcast(shape), ALU.add))
            for hot, pp, c in ((hot1, p1, 0), (hot2, p2, 1)):
                go(V.tensor_tensor(mark[:], hot[:], pos[:], ALU.mult))
                go(V.tensor_reduce(pp[:], mark[:], AX.X, ALU.add))
                go(V.tensor_tensor(send[c][:], pp[:], invalid[:], ALU.add))
                go(V.tensor_tensor(fetch[c][:], pp[:], valid[:], ALU.mult))
            go(V.tensor_scalar(slot_e[:], slot[:], ends[0:1, 0:1], None, ALU.is_ge))
            for e in range(1, EXPERTS):
                go(V.scalar_tensor_tensor(slot_e[:], slot[:], ends[0:1, e:e + 1], slot_e[:], ALU.is_ge, ALU.add))
            V.tensor_scalar(slot_i[:], slot_e[:], float(EXPERTS - 1), None, ALU.min).then_inc(counted, 1)
            for q in range(2):
                for c in range(TOP):
                    nc.vector.tensor_copy(to[q][:, c, :], send[c][:, q * TILES:(q + 1) * TILES]).then_inc(to_ok[q], 1)
            with dve.Fori(1, pairs) as i:
                for q in range(2):
                    dve.wait_ge(sent[q], 16 * TOP * TILES * i)
                    for c in range(TOP):
                        nc.vector.tensor_copy(to[q][:, c, :], send[c][:, bass.ds((i * 2 + q) * TILES, TILES)]).then_inc(to_ok[q], 1)


HID = 1024
HC = HID // P


def stage_experts(nc, a, t):
    with ExitStack() as ctx:
        ident = sb(nc, ctx, "e_ident", [P, P])
        w1 = sb(nc, ctx, "e_w1", [P, EXPERTS, H2 * HID])
        w2 = sb(nc, ctx, "e_w2", [P, EXPERTS, HC * D])
        b1 = sb(nc, ctx, "e_b1", [P, EXPERTS, HID])
        b2 = sb(nc, ctx, "e_b2", [P, EXPERTS, D])
        ln = sb(nc, ctx, "e_ln", [P, EXPERTS, 2 * H2])
        slot_e = sb(nc, ctx, "e_slot_e", [1, XSLOTS], I32)
        rows = [sb(nc, ctx, f"e_rows{q}", [P, D]) for q in range(2)]
        xT = [sb(nc, ctx, f"e_xT{q}", [P, H2, P]) for q in range(2)]
        h = [sb(nc, ctx, f"e_h{q}", [P, HID]) for q in range(2)]
        hT = [sb(nc, ctx, f"e_hT{q}", [P, HC, P]) for q in range(2)]
        y = [sb(nc, ctx, f"e_y{q}", [P, D]) for q in range(2)]
        x_ps = ps(nc, ctx, "e_x_ps", [P, 512])
        h_ps = ps(nc, ctx, "e_h_ps", [P, 4, 512])
        hT_ps = ps(nc, ctx, "e_hT_ps", [P, 2, 512])
        y_ps = ps(nc, ctx, "e_y_ps", [P, 512])
        w_ok, x_mm, x_ok, hT_mm, hT_ok, y_mm, y_ok = sems(nc, ctx, "e", "w_ok x_mm x_ok hT_mm hT_ok y_mm y_ok")
        rows_in, h_mm, biased, gelu_ok, stored = (sems(nc, ctx, "e", f"{n}0 {n}1") for n in "rows_in h_mm biased gelu_ok stored".split())
        LOADS = 3 + 4 * EXPERTS
        block = ctx.enter_context(nc.Block())

        def steps(eng, runs):
            def step(i, j):
                for run, ahead in runs:
                    if not isinstance(i, int) or 0 <= 2 * i + j + ahead < XSLOTS:
                        run(i, j + ahead)

            for s in range(-2, 2):
                step(s // 2, s % 2)
            with eng.Fori(1, XSLOTS // 2 - 1) as i:
                for j in range(2):
                    step(i, j)
            for s in range(XSLOTS - 2, XSLOTS + 2):
                step(s // 2, s % 2)

        def begun(i, j):
            return not isinstance(i, int) or 2 * i + j >= 0

        def expert(eng, i, j):
            return bass.ds(eng.value_load(slot_e[0:1, bass.ds(i * 2 + j, 1)], min_val=0, max_val=EXPERTS - 1), 1)

        @block.sync
        def _(sp):
            for dst, source in ((slot_e[:], t["slot_e"]), (ident[:], a["ident"]), (ln[:], a["ffn_ln"])):
                sp.dma_start(dst, source).then_inc(w_ok, 16)
            for e in range(EXPERTS):
                sp.dma_start(w1[:, e, :].rearrange("p (k n) -> p k n", k=H2), a["ffn_W1"][e].rearrange("(k p) n -> p k n", p=P)).then_inc(w_ok, 16)
                sp.dma_start(w2[:, e, :].rearrange("p (k n) -> p k n", k=HC), a["ffn_W2"][e].rearrange("(k p) n -> p k n", p=P)).then_inc(w_ok, 16)
                sp.dma_start(b1[:, e, :], a["ffn_b1"][e].unsqueeze(0).to_broadcast([P, HID])).then_inc(w_ok, 16)
                sp.dma_start(b2[:, e, :], a["ffn_b2"][e].unsqueeze(0).to_broadcast([P, D])).then_inc(w_ok, 16)

            def load(i, j):
                if begun(i, j - 2):
                    sp.wait_ge(x_mm, START + 2 * i + j - 1)
                sp.dma_start(rows[j % 2][:], t["xd"][bass.ds((i * 2 + j) * P, P), :]).then_inc(rows_in[j % 2], 16)

            def store(i, j):
                sp.wait_ge(y_ok, START + 2 * i + j + 1)
                sp.dma_start(t["yd"][bass.ds((i * 2 + j) * P, P), :], y[j % 2][:]).then_inc(stored[j % 2], 16)

            steps(sp, ((load, 2), (store, -2)))
            for q in range(2):
                sp.wait_ge(stored[q], START + 16 * (XSLOTS // 2))

        @block.tensor
        def _(pe):
            def turn_rows(i, j):
                q = j % 2
                pe.wait_ge(rows_in[q], START + 16 * (i + j // 2 + 1))
                pe.wait_ge(x_ok, START + 2 * (2 * i + j))
                for k in range(H2):
                    last = nc.tensor.transpose(x_ps[:, k * P:(k + 1) * P], rows[q][:, k * P:(k + 1) * P], ident[:])
                last.then_inc(x_mm, 1)

            def hidden(n):
                def run(i, j):
                    q, u = j % 2, i + j // 2
                    e = expert(pe, i, j)
                    pe.wait_ge(x_ok, START + 2 * (2 * i + j) + 2)
                    if begun(i, j - 2):
                        pe.wait_ge(biased[q], START + 2 * u + n - 1)
                    for k in range(H2):
                        last = nc.tensor.matmul(h_ps[:, 2 * q + n, :], xT[q][:, k, :],
                                                w1[:, e, k * HID + n * 512:k * HID + (n + 1) * 512].rearrange("p e n -> p (e n)"),
                                                start=(k == 0), stop=(k == H2 - 1))
                    last.then_inc(h_mm[q], 1)
                return run

            def turn_hidden(n):
                def run(i, j):
                    q, u = j % 2, i + j // 2
                    pe.wait_ge(gelu_ok[q], START + 2 * u + n + 1)
                    if begun(i, j - 1):
                        pe.wait_ge(hT_ok, START + 2 * (2 * i + j) + n - 1)
                    for c in range(4):
                        cc = n * 4 + c
                        last = nc.tensor.transpose(hT_ps[:, n, c * P:(c + 1) * P], h[q][:, cc * P:(cc + 1) * P], ident[:])
                    last.then_inc(hT_mm, 1)
                return run

            def output(i, j):
                e = expert(pe, i, j)
                pe.wait_ge(hT_ok, START + 2 * (2 * i + j) + 2)
                pe.wait_ge(y_ok, START + 2 * i + j)
                for c in range(HC):
                    last = nc.tensor.matmul(y_ps[:, 0:D], hT[j % 2][:, c, :], w2[:, e, c * D:(c + 1) * D].rearrange("p e n -> p (e n)"),
                                            start=(c == 0), stop=(c == HC - 1))
                last.then_inc(y_mm, 1)

            pe.wait_ge(w_ok, START + 16 * LOADS)
            steps(pe, ((turn_rows, 1), (hidden(0), 0), (turn_hidden(0), -1), (hidden(1), 0), (turn_hidden(1), -1), (output, -2)))

        @block.scalar
        def _(act):
            def gelu(n):
                def run(i, j):
                    q = j % 2
                    act.wait_ge(biased[q], START + 2 * (i + j // 2) + n + 1)
                    half = h[q][:, n * 512:(n + 1) * 512]
                    nc.scalar.activation(half, half, ACT.Gelu).then_inc(gelu_ok[q], 1)
                return run

            def copy_turned(n):
                def run(i, j):
                    act.wait_ge(hT_mm, START + 2 * (2 * i + j) + n + 1)
                    if begun(i, j - 2):
                        act.wait_ge(y_mm, START + 2 * i + j - 1)
                    nc.scalar.activation(hT[j % 2][:, 4 * n:4 * n + 4, :].rearrange("p c n -> p (c n)"), hT_ps[:, n, :],
                                         ACT.Copy).then_inc(hT_ok, 1)
                return run

            act.wait_ge(w_ok, START + 16 * LOADS)
            steps(act, ((copy_turned(0), -1), (gelu(0), 0), (copy_turned(1), -1), (gelu(1), 0)))

        @block.vector
        def _(dve):
            def gain(i, j):
                q = j % 2
                e = expert(dve, i, j)
                dve.wait_ge(x_mm, START + 2 * i + j + 1)
                dve.wait_ge(h_mm[q], START + 2 * (i + j // 2))
                for k in range(H2):
                    nc.vector.tensor_scalar(xT[q][:, k, :], x_ps[:, k * P:(k + 1) * P],
                                            ln[:, e, k:k + 1].rearrange("p e n -> p (e n)"),
                                            ln[:, e, H2 + k:H2 + k + 1].rearrange("p e n -> p (e n)"),
                                            ALU.mult, ALU.add).then_inc(x_ok, 1)

            def bias(i, j):
                q, u = j % 2, i + j // 2
                e = expert(dve, i, j)
                for n in range(2):
                    dve.wait_ge(h_mm[q], START + 2 * u + n + 1)
                    if begun(i, j - 2):
                        dve.wait_ge(hT_mm, START + 2 * (2 * i + j) + n - 3)
                    nc.vector.tensor_tensor(h[q][:, n * 512:(n + 1) * 512], h_ps[:, 2 * q + n, :],
                                            b1[:, e, n * 512:(n + 1) * 512].rearrange("p e n -> p (e n)"),
                                            ALU.add).then_inc(biased[q], 1)

            def output(i, j):
                q = j % 2
                e = expert(dve, i, j)
                dve.wait_ge(y_mm, START + 2 * i + j + 1)
                dve.wait_ge(stored[q], START + 16 * (i + j // 2))
                nc.vector.tensor_tensor(y[q][:], y_ps[:, 0:D], b2[:, e, :].rearrange("p e n -> p (e n)"), ALU.add).then_inc(y_ok, 1)

            dve.wait_ge(w_ok, START + 16 * LOADS)
            steps(dve, ((gain, 1), (bias, 0), (output, -2)))


def stage_combine(nc, a, t):
    with ExitStack() as ctx:
        fetch = [sb(nc, ctx, f"c_fetch{c}", [TT, NTT], I32) for c in range(TOP)]
        w = [sb(nc, ctx, f"c_w{c}", [TT, NTT]) for c in range(TOP)]
        at = [sb(nc, ctx, f"c_at{q}", [TT, TOP, TILES], I32) for q in range(2)]
        got = [sb(nc, ctx, f"c_got{q}", [TT, TOP, TILES, D]) for q in range(2)]
        acc = [sb(nc, ctx, f"c_acc{q}", [TT, TILES, D]) for q in range(2)]
        token = sb(nc, ctx, "c_token", [P, 2])
        settled, loaded, token_ok = sems(nc, ctx, "c", "settled loaded token_ok")
        x_in, at_ok, got_in, half_ok, sum_ok, stored = (sems(nc, ctx, "c", f"{n}0 {n}1") for n in "x_in at_ok got_in half_ok sum_ok stored".split())
        pairs = NCH // 2
        block = ctx.enter_context(nc.Block())

        @block.sync
        def _(sp):
            for dst, source in ((fetch[0], "fetch0"), (fetch[1], "fetch1"), (w[0], "w1"), (w[1], "w2")):
                sp.dma_start(dst[:], t[source]).then_inc(loaded, 16)
            with sp.Fori(0, pairs) as i:
                for q in range(2):
                    sp.wait_ge(stored[q], START + 16 * i)
                    sp.dma_start(acc[q][:], t["x2"][bass.ds((i * 2 + q) * CH, CH), :].rearrange("(j p) f -> p j f", p=TT)).then_inc(x_in[q], 16)
                for q in range(2):
                    sp.wait_ge(sum_ok[q], START + TILES * (i + 1))
                    sp.dma_start(t["out"][bass.ds((i * 2 + q) * CH, CH), :].rearrange("(j p) f -> p j f", p=TT), acc[q][:]).then_inc(stored[q], 16)
            for q in range(2):
                sp.wait_ge(stored[q], START + 16 * pairs)

        @block.gpsimd
        def _(pool):
            nc.gpsimd.memset(token[:], 0.0).then_inc(token_ok, 1)
            pool.wait_ge(token_ok, START + 1)
            with pool.Fori(0, pairs) as i:
                for q in range(2):
                    pool.wait_ge(at_ok[q], START + TOP * (i + 1))
                    pool.wait_ge(sum_ok[q], START + TILES * i)
                    settle(nc, pool, token, settled, 2 * i + q)
                    for c in range(TOP):
                        for j in range(TILES):
                            nc.gpsimd.indirect_dma_start(
                                out=got[q][:, c, j, :], out_offset=None, in_=t["yd"],
                                in_offset=bass.IndirectOffsetOnAxis(ap=at[q][:, c, j:j + 1], axis=0)).then_inc(got_in[q], 16)

        @block.vector
        def _(dve):
            dve.wait_ge(loaded, START + 64)

            def where(i, q):
                for c in range(TOP):
                    nc.vector.tensor_copy(at[q][:, c, :], fetch[c][:, bass.ds((i * 2 + q) * TILES, TILES)]).then_inc(at_ok[q], 1)

            with dve.Fori(0, pairs) as i:
                for q in range(2):
                    dve.wait_ge(sum_ok[q], START + TILES * i)
                    where(i, q)
                for q in range(2):
                    dve.wait_ge(x_in[q], START + 16 * (i + 1))
                    dve.wait_ge(got_in[q], 16 * TOP * TILES * (i + 1))
                    for j in range(TILES):
                        nc.vector.scalar_tensor_tensor(acc[q][:, j, :], got[q][:, 0, j, :], w[0][:, bass.ds((i * 2 + q) * TILES + j, 1)],
                                                       acc[q][:, j, :], ALU.mult, ALU.add).then_inc(half_ok[q], 1)
                    for j in range(TILES):
                        dve.wait_ge(half_ok[q], START + TILES * i + j + 1)
                        nc.vector.scalar_tensor_tensor(acc[q][:, j, :], got[q][:, 1, j, :], w[1][:, bass.ds((i * 2 + q) * TILES + j, 1)],
                                                       acc[q][:, j, :], ALU.mult, ALU.add).then_inc(sum_ok[q], 1)


SCRATCH = {
    "xd": (XSLOTS * P, D), "yd": (XSLOTS * P, D), "fetch0": ((TT, NTT), I32), "fetch1": ((TT, NTT), I32),
    "w1": (TT, NTT), "w2": (TT, NTT), "slot_e": ((1, XSLOTS), I32),
    "logit": (NP, EXPERTS), "x2": (NP, D), "xe": (NP, D),
    "agg": (NP, D),
    "y": (NP, D),
    "v": (NP,), "rank": ((NP,), I32), "xs": (NP, D),
    "xnT": (D, NP), "xn": (NP, D), "table": (NP, ROW), "kv": (P, H2, KROW),
}


def build(nc, a, out):
    t = {n: nc.dram_tensor(f"t_{n}", list(s if not isinstance(s[0], tuple) else s[0]),
                           F32 if not isinstance(s[0], tuple) else s[1], kind="Internal").ap()
         for n, s in SCRATCH.items()}
    t["out"] = out
    stages = [stage_project, stage_rank, stage_mamba, stage_attend, stage_mix, stage_route,
              stage_experts, stage_combine]
    for stage in stages:
        held = nc.snapshot_sems()
        stage(nc, a, t)
        nc.clear_and_free_semaphores(nc.allocated_since(held))
        nc.all_engine_barrier()


def kernel(**inputs):
    import numpy as np
    import concourse.bacc as bacc
    from concourse.bass_utils import run_bass_kernel_spmd

    g = {k[len("L0_gnn_"):]: np.asarray(v) for k, v in inputs.items() if k.startswith("L0_gnn_")}
    m = {k[len("L0_mix_"):]: np.asarray(v) for k, v in inputs.items() if k.startswith("L0_mix_")}
    f = {k[len("L0_ffn_"):]: np.asarray(v) for k, v in inputs.items() if k.startswith("L0_ffn_")}
    x = np.asarray(inputs["x"])
    feed = {}
    feed["xT"] = np.zeros((D, NP), np.float32)
    feed["xT"][:, :N] = x.T
    feed["gat_w"] = g["gat_w"]
    feed["gat_wT"] = g["gat_w"].T
    blk = np.zeros((D, 2 * HEADS), np.float32)
    for h in range(HEADS):
        blk[h * FO:(h + 1) * FO, h] = g["gat_a_src"][h]
        blk[h * FO:(h + 1) * FO, HEADS + h] = g["gat_a_tgt"][h]
    feed["a_blk"] = blk
    feed["Wk"], feed["Wv"] = m["Wk"], m["Wv"]
    feed["valid"] = (np.arange(NP) < N).astype(np.float32).reshape(NTT, TT).T
    feed["src"] = np.asarray(inputs["src"]).reshape(EP, EC)
    noise = np.full(NP, 3e38, np.float32)
    noise[:N] = np.asarray(inputs["node_vec"])
    feed["noise"] = noise.reshape(NT, P).T
    feed["in_projT"], feed["out_projT"] = g["in_proj_w"].T, g["out_proj_w"].T
    feed["x_projT"] = np.concatenate([g["x_proj_w"][STATES:]] * PARTS + [g["x_proj_w"][:STATES]]).T
    feed["dt_projT"] = np.zeros((DBC, D), np.float32)
    feed["dt_projT"][PARTS * BC:] = g["dt_proj_w"].T
    feed["pick"] = np.repeat(np.tile(np.eye(BC, dtype=np.float32), (PARTS, 1))[:, :, None], P, axis=2)
    feed["mamba_vecs"] = np.concatenate([g["conv_w"], g["conv_b"][:, None], g["dt_proj_b"][:, None], g["D_param"][:, None]], 1)
    feed["A_log"] = g["A_log"]
    feed["dst"] = np.asarray(inputs["dst"]).reshape(EP, EC)
    edges = np.zeros((E + P, 2), np.int32)
    edges[:, 1] = 1 << 20
    edges[:E, 0], edges[:E, 1] = np.asarray(inputs["src"]), np.asarray(inputs["dst"])
    feed["edges"] = edges
    feed["below"] = np.triu(np.ones((P, P), np.float32), 1)
    feed["wlT"], feed["wgT"], feed["ff1T"], feed["ff2T"] = g["wl"].T, g["wg"].T, g["ff1_w"].T, g["ff2_w"].T
    for n in ("Wq", "Wm", "W1", "W2"):
        feed[n] = m[n]
    feed["ff1_b"], feed["Wr"], feed["br"] = g["ff1_b"].reshape(4, P).T, f["Wr"], f["br"]
    feed["mix_vecs"] = np.stack([g["gat_b"], g["ff2_b"], g["ln_local_g"], g["ln_local_b"], g["ln_global_g"], g["ln_global_b"],
                                 m["g1"], m["b1"], g["ln2_g"], g["ln2_b"], m["g2"], m["b2"]], 1)
    feed["same"] = np.kron(np.eye(4, dtype=np.float32), np.ones((32, 32), np.float32))
    feed["ffn_ln"] = np.concatenate([f["ln_g"].reshape(EXPERTS, H2, P), f["ln_b"].reshape(EXPERTS, H2, P)], 1).transpose(2, 0, 1)
    for n in ("W1", "W2", "b1", "b2"):
        feed["ffn_" + n] = f[n]
    feed["ident"] = np.eye(P, dtype=np.float32)

    nc = bacc.Bacc("TRN2", target_bir_lowering=False, num_devices=1)
    arrays, args = {}, {}
    for name, arr in feed.items():
        arr = np.ascontiguousarray(arr)
        arrays[f"in_{name}"] = arr
        args[name] = nc.dram_tensor(f"in_{name}", arr.shape, mybir.dt.from_np(arr.dtype), kind="ExternalInput").ap()
    out = nc.dram_tensor("out_rows", (NP, D), F32, kind="ExternalOutput").ap()
    build(nc, args, out)
    r = run_bass_kernel_spmd(nc, [arrays], core_ids=[0])
    return r.results[0]["out_rows"][:N]
```

```python
from contextlib import ExitStack

import concourse.bass as bass
from concourse import mybir

F32 = mybir.dt.float32
BF16 = mybir.dt.bfloat16
I32 = mybir.dt.int32
U32 = mybir.dt.uint32
ALU = mybir.AluOpType
ACT = mybir.ActivationFunctionType
AX = mybir.AxisListType

P = 128
N = 6250
D = 256
H2 = D // P
NT = -(-N // P)
NP = NT * P
TT = 112
TILES = 4
CH = TT * TILES
NCH = NP // CH
NTT = NP // TT
E = 100000
EP, EC = 125, 800
HEADS = 4
FO = D // HEADS
ROW = D + 2 * HEADS
KROW = P + 1
LN_EPS = 1e-5
START = 1


FROM_ZERO = ("moved", "sent", "got_in", "y_in")


def sb(nc, ctx, name, shape, dt=F32):
    return ctx.enter_context(nc.sbuf_tensor(name, shape, dt))


def ps(nc, ctx, name, shape, dt=F32):
    return ctx.enter_context(nc.psum_tensor(name, shape, dt))


def sems(nc, ctx, stage, names):
    made = [nc.alloc_semaphore(name=f"{stage}_{n}") for n in names.split()]
    for sem, n in zip(made, names.split()):
        if n.rstrip("0123456789") not in FROM_ZERO:
            nc.sync.sem_inc(sem, START)
    return made


def settle(nc, pool, token, settled, times):
    pool.wait_ge(settled, START + times)
    nc.gpsimd.tensor_tensor(token[:, 1:2], token[:, 0:1], token[:, 0:1], ALU.add).then_inc(settled, 1)


def halves(ap):
    return ap.rearrange("(h p) n -> p h n", p=P)


def over_halves(ap):
    return ap.unsqueeze(1).to_broadcast([P, H2, ap.shape[1]])


def stage_project(nc, a, t):
    with ExitStack() as ctx:
        inv_d = sb(nc, ctx, "p_inv_d", [P, P])
        ident = sb(nc, ctx, "p_ident", [P, P])
        w_gat = sb(nc, ctx, "p_w_gat", [P, H2, ROW])
        w_gat_o = sb(nc, ctx, "p_w_gat_o", [P, H2, D])
        a_blk = sb(nc, ctx, "p_a_blk", [P, H2, 2 * HEADS])
        w_kv = sb(nc, ctx, "p_w_kv", [P, H2, 2 * D])
        valid = sb(nc, ctx, "p_valid", [TT, NTT])
        x_c = [sb(nc, ctx, f"p_x{c}", [P, H2, CH]) for c in range(2)]
        cent = [sb(nc, ctx, f"p_cent{c}", [P, H2, CH]) for c in range(2)]
        sq = sb(nc, ctx, "p_sq", [P, H2, CH])
        std = sb(nc, ctx, "p_std", [P, CH])
        rstd = sb(nc, ctx, "p_rstd", [P, CH])
        xn = [sb(nc, ctx, f"p_xn{c}", [P, H2, CH]) for c in range(2)]
        rows = sb(nc, ctx, "p_rows", [TT, TILES, D])
        tab = sb(nc, ctx, "p_tab", [TT, TILES, ROW])
        kneg = sb(nc, ctx, "p_kneg", [TT, TILES, D])
        kexp = sb(nc, ctx, "p_kexp", [TT, TILES, D])
        k_t = sb(nc, ctx, "p_k", [TT, TILES, D])
        v_t = sb(nc, ctx, "p_v", [TT, TILES, D])
        kv_acc = sb(nc, ctx, "p_kv_acc", [P, H2, KROW])
        eps = sb(nc, ctx, "p_eps", [P, 1])

        mean_ps = ps(nc, ctx, "p_mean_ps", [P, 512])
        var_ps = ps(nc, ctx, "p_var_ps", [P, 512])
        tab_ps = ps(nc, ctx, "p_tab_ps", [P, 2, 512])
        k_ps = ps(nc, ctx, "p_k_ps", [P, 512])
        v_ps = ps(nc, ctx, "p_v_ps", [P, 512])
        rows_ps = ps(nc, ctx, "p_rows_ps", [P, 512])
        kv_ps = ps(nc, ctx, "p_kv_ps", [P, 512])

        (consts, w_in, w_scores, w_scored, mean_ok, centred, squared, var_ok, std_ok, rstd_ok, xn_ok,
         xn_out, rows_mm, rows_ok, rows_out, tab_out, kexp_ok, k_ok, kneg_ok, kv_mm, kv_ok, kv_out) = sems(
            nc, ctx, "p", "consts w_in w_scores w_scored mean_ok centred squared var_ok std_ok rstd_ok xn_ok "
            "xn_out rows_mm rows_ok rows_out tab_out kexp_ok k_ok kneg_ok kv_mm kv_ok kv_out")
        x_in = sems(nc, ctx, "p", "x_in0 x_in1")
        tab_mm = sems(nc, ctx, "p", "tab_mm0 tab_mm1")
        tab_ok = sems(nc, ctx, "p", "tab_ok0 tab_ok1")
        k_mm, v_mm, v_ok = sems(nc, ctx, "p", "k_mm v_mm v_ok")
        block = ctx.enter_context(nc.Block())

        def chunks(eng, chunk):
            with eng.Fori(0, NCH // 2 - 1) as i:
                for c in range(2):
                    chunk(i, c, False)
            for c in range(2):
                chunk(NCH // 2 - 1, c, c == 1)

        @block.gpsimd
        def _(pool):
            nc.gpsimd.memset(inv_d[:], 1.0 / D).then_inc(consts, 1)
            nc.gpsimd.memset(eps[:], LN_EPS).then_inc(consts, 1)
            nc.gpsimd.memset(kv_acc[:], 0.0).then_inc(consts, 1)

        @block.sync
        def _(sp):
            sp.dma_start(x_c[0][:], halves(a["xT"])[:, :, 0:CH]).then_inc(x_in[0], 16)
            sp.dma_start(w_gat_o[:], halves(a["gat_w"])).then_inc(w_in, 16)
            sp.dma_start(w_gat[:, :, 0:D], halves(a["gat_wT"])).then_inc(w_in, 16)
            sp.dma_start(a_blk[:], halves(a["a_blk"])).then_inc(w_in, 16)
            sp.dma_start(w_kv[:, :, 0:D], halves(a["Wk"])).then_inc(w_in, 16)
            sp.dma_start(w_kv[:, :, D:], halves(a["Wv"])).then_inc(w_in, 16)
            sp.dma_start(valid[:], a["valid"]).then_inc(w_in, 16)
            sp.dma_start(ident[:], a["ident"]).then_inc(w_in, 16)

            def chunk(i, c, final):
                g = i * 2 + c
                if not final:
                    sp.wait_ge(centred, START + g)
                    sp.dma_start(x_c[1 - c][:], halves(a["xT"])[:, :, bass.ds((g + 1) * CH, CH)]).then_inc(x_in[1 - c], 16)
                sp.wait_ge(xn_ok, START + g + 1)
                sp.dma_start(halves(t["xnT"])[:, :, bass.ds(g * CH, CH)], xn[c][:]).then_inc(xn_out, 16)
                sp.wait_ge(rows_ok, START + 4 * g + 4)
                sp.dma_start(t["xn"][bass.ds(g * CH, CH), :].rearrange("(j p) f -> p j f", p=TT), rows[:]).then_inc(rows_out, 16)
                for s in range(2):
                    sp.wait_ge(tab_ok[s], START + 2 * g + 2)
                sp.dma_start(t["table"][bass.ds(g * CH, CH), :].rearrange("(j p) f -> p j f", p=TT), tab[:]).then_inc(tab_out, 16)

            chunks(sp, chunk)
            sp.wait_ge(kv_ok, START + NCH)
            sp.dma_start(t["kv"], kv_acc[:]).then_inc(kv_out, 16)
            sp.wait_ge(xn_out, START + 16 * NCH)
            sp.wait_ge(rows_out, START + 16 * NCH)
            sp.wait_ge(tab_out, START + 16 * NCH)
            sp.wait_ge(kv_out, START + 16)

        @block.tensor
        def _(pe):
            def mean(i, c):
                g = i * 2 + c
                pe.wait_ge(x_in[c], START + 16 * (i + 1))
                pe.wait_ge(centred, START + g)
                for k in range(H2):
                    last = nc.tensor.matmul(mean_ps[:, 0:CH], inv_d[:], x_c[c][:, k, :], start=(k == 0), stop=(k == 1))
                last.then_inc(mean_ok, 1)

            def var(g):
                pe.wait_ge(squared, START + g + 1)
                pe.wait_ge(std_ok, START + g)
                for k in range(H2):
                    last = nc.tensor.matmul(var_ps[:, 0:CH], inv_d[:], sq[:, k, :], start=(k == 0), stop=(k == 1))
                last.then_inc(var_ok, 1)

            def chunk(i, c, final):
                g = i * 2 + c
                pe.wait_ge(xn_ok, START + g + 1)
                for j in range(TILES):
                    s, u = j % 2, j // 2
                    tok = slice(j * TT, (j + 1) * TT)
                    pe.wait_ge(tab_ok[s], START + 2 * g + u)
                    for k in range(H2):
                        last = nc.tensor.matmul(tab_ps[0:TT, s, 0:ROW], xn[c][:, k, tok], w_gat[:, k, :],
                                                start=(k == 0), stop=(k == 1))
                    last.then_inc(tab_mm[s], 1)
                    for bank, w, done, read in ((k_ps, 0, k_mm, k_ok), (v_ps, D, v_mm, v_ok)):
                        pe.wait_ge(read, START + 4 * g + j)
                        for k in range(H2):
                            last = nc.tensor.matmul(bank[0:TT, 0:D], xn[c][:, k, tok], w_kv[:, k, w:w + D],
                                                    start=(k == 0), stop=(k == 1))
                        last.then_inc(done, 1)
                    pe.wait_ge(rows_ok, START + 4 * g + j)
                    for k in range(H2):
                        last = nc.tensor.transpose(rows_ps[0:TT, k * P:(k + 1) * P], xn[c][:, k, tok], ident[:])
                    last.then_inc(rows_mm, 1)
                    if j == 0 and not final:
                        mean(i + c, 1 - c)
                    if j == 2 and not final:
                        var(g + 1)
                pe.wait_ge(k_ok, START + 4 * g + 4)
                pe.wait_ge(v_ok, START + 4 * g + 4)
                pe.wait_ge(kv_ok, START + g)
                for b in range(H2):
                    for j in range(TILES):
                        nc.tensor.matmul(kv_ps[:, b * KROW:b * KROW + P], k_t[:, j, b * P:(b + 1) * P],
                                         v_t[:, j, b * P:(b + 1) * P], start=(j == 0), stop=(j == TILES - 1))
                    for j in range(TILES):
                        last = nc.tensor.matmul(kv_ps[:, b * KROW + P:(b + 1) * KROW], k_t[:, j, b * P:(b + 1) * P],
                                                valid[:, bass.ds(g * TILES + j, 1)], start=(j == 0), stop=(j == TILES - 1))
                last.then_inc(kv_mm, 1)

            pe.wait_ge(consts, START + 3)
            mean(0, 0)
            pe.wait_ge(w_in, START + 16 * 7)
            for m in range(H2):
                for k in range(H2):
                    last = nc.tensor.matmul(tab_ps[:, 0, 8 * m:8 * m + 8], w_gat_o[:, k, m * P:(m + 1) * P], a_blk[:, k, :],
                                            start=(k == 0), stop=(k == H2 - 1))
            last.then_inc(w_scores, 1)
            pe.wait_ge(w_scored, START + 1)
            var(0)
            chunks(pe, chunk)

        @block.scalar
        def _(act):
            def square(g, c):
                act.wait_ge(centred, START + g + 1)
                act.wait_ge(var_ok, START + g)
                nc.scalar.activation(sq[:], cent[c][:], ACT.Square).then_inc(squared, 1)

            def root(g):
                act.wait_ge(var_ok, START + g + 1)
                act.wait_ge(rstd_ok, START + g)
                nc.scalar.activation(std[:], var_ps[:, 0:CH], ACT.Ln, bias=eps[:]).then_inc(std_ok, 1)
                act.wait_ge(std_ok, START + g + 1)
                act.wait_ge(xn_ok, START + g)
                nc.scalar.activation(rstd[:], std[:], ACT.Exp, scale=-0.5).then_inc(rstd_ok, 1)

            def chunk(i, c, final):
                g = i * 2 + c
                act.wait_ge(kv_mm, START + g)
                act.wait_ge(tab_out, START + 16 * g)
                for j in range(TILES):
                    s, u = j % 2, j // 2
                    act.wait_ge(tab_mm[s], START + 2 * g + u + 1)
                    nc.scalar.activation(tab[:, j, :], tab_ps[0:TT, s, 0:ROW], ACT.Copy).then_inc(tab_ok[s], 1)
                    act.wait_ge(kneg_ok, START + 4 * g + j + 1)
                    act.wait_ge(k_ok, START + 4 * g)
                    nc.scalar.activation(kexp[:, j, :], kneg[:, j, :], ACT.Exp).then_inc(kexp_ok, 1)
                    act.wait_ge(v_mm, START + 4 * g + j + 1)
                    nc.scalar.activation(v_t[:, j, :], v_ps[0:TT, 0:D], ACT.Copy).then_inc(v_ok, 1)
                    if j == 1 and not final:
                        square(g + 1, 1 - c)
                if not final:
                    root(g + 1)

            square(0, 0)
            root(0)
            chunks(act, chunk)

        @block.vector
        def _(dve):
            def centre(g, c):
                dve.wait_ge(mean_ok, START + g + 1)
                dve.wait_ge(squared, START + g)
                dve.wait_ge(xn_ok, START + g)
                nc.vector.tensor_tensor(cent[c][:], x_c[c][:], over_halves(mean_ps[:, 0:CH]), ALU.subtract).then_inc(centred, 1)

            def norm(g, c, ahead=True):
                dve.wait_ge(rstd_ok, START + g + 1)
                dve.wait_ge(centred, START + g + 1)
                if ahead:
                    dve.wait_ge(rows_mm, START + 4 * (g - 1))
                    dve.wait_ge(xn_out, START + 16 * (g - 1))
                nc.vector.tensor_tensor(xn[c][:], cent[c][:], over_halves(rstd[:]), ALU.mult).then_inc(xn_ok, 1)

            def chunk(i, c, final):
                g = i * 2 + c
                dve.wait_ge(rows_out, START + 16 * g)
                dve.wait_ge(kv_mm, START + g)
                for j in range(TILES):
                    dve.wait_ge(k_mm, START + 4 * g + j + 1)
                    dve.wait_ge(kexp_ok, START + 4 * g)
                    nc.vector.tensor_scalar(kneg[:, j, :], k_ps[0:TT, 0:D], 0.0, None, ALU.min).then_inc(kneg_ok, 1)
                    dve.wait_ge(kexp_ok, START + 4 * g + j + 1)
                    nc.vector.scalar_tensor_tensor(k_t[:, j, :], k_ps[0:TT, 0:D], 0.0, kexp[:, j, :],
                                                   ALU.max, ALU.add).then_inc(k_ok, 1)
                    dve.wait_ge(rows_mm, START + 4 * g + j + 1)
                    nc.vector.tensor_copy(rows[:, j, :], rows_ps[0:TT, 0:D]).then_inc(rows_ok, 1)
                    if j == 0 and not final:
                        centre(g + 1, 1 - c)
                if not final:
                    norm(g + 1, 1 - c)
                dve.wait_ge(kv_mm, START + g + 1)
                dve.wait_ge(kv_ok, START + g)
                nc.vector.tensor_tensor(kv_acc[:], kv_acc[:], kv_ps[:, 0:H2 * KROW].rearrange("p (h c) -> p h c", h=H2),
                                        ALU.add).then_inc(kv_ok, 1)

            centre(0, 0)
            dve.wait_ge(w_scores, START + 1)
            nc.vector.tensor_copy(w_gat[:, :, D:ROW], tab_ps[:, 0, 0:16].rearrange("p (h c) -> p h c", h=H2)).then_inc(w_scored, 1)
            norm(0, 0, False)
            chunks(dve, chunk)


GRP = 20
TINY = 1e-37


def stage_rank(nc, a, t):
    with ExitStack() as ctx:
        src_i = sb(nc, ctx, "r_src_i", [EP, EC], I32)
        part_i = sb(nc, ctx, "r_part_i", [EP, EC], I32)
        lo = sb(nc, ctx, "r_lo", [EP, EC], BF16)
        hi = sb(nc, ctx, "r_hi", [EP, EC], BF16)
        count = sb(nc, ctx, "r_count", [P, P], BF16)
        hot_lo = sb(nc, ctx, "r_hot_lo", [EP, 2, GRP, P], BF16)
        hot_hi = sb(nc, ctx, "r_hot_hi", [EP, 2, GRP, NT], BF16)
        zero = sb(nc, ctx, "r_zero", [P, P], BF16)
        zeros = sb(nc, ctx, "r_zeros", [P, D])
        ident = sb(nc, ctx, "r_ident", [P, P])
        noise = sb(nc, ctx, "r_noise", [P, NT])
        v_col = sb(nc, ctx, "r_v_col", [P, NT])
        v_row = sb(nc, ctx, "r_v_row", [NT, P])
        v_all = sb(nc, ctx, "r_v_all", [P, NP])
        before = sb(nc, ctx, "r_before", [P, 2 * NP], BF16)
        hits = sb(nc, ctx, "r_hits", [P, NP], BF16)
        rank_f = sb(nc, ctx, "r_rank_f", [P, NT])
        rank_i = sb(nc, ctx, "r_rank_i", [P, NT], I32)
        rank_row = sb(nc, ctx, "r_rank_row", [NT, P], I32)
        xrows = sb(nc, ctx, "r_xrows", [P, NT, D])
        deg_ps = ps(nc, ctx, "r_deg_ps", [P, 512])
        row_ps = ps(nc, ctx, "r_row_ps", [P, 512])
        (src_in, other_in, xrows_in, consts, before_ok, part_ok, lo_ok, hi_ok, deg_ok, vcol_ok, vrow_mm, vrow_ok,
         vrow_out, vall_in, rankf_ok, ranki_ok, rank_mm, rankrow_ok, rank_out, zeros_ok, emptied, moved) = sems(
            nc, ctx, "r", "src_in other_in xrows_in consts before_ok part_ok lo_ok hi_ok deg_ok vcol_ok vrow_mm "
            "vrow_ok vrow_out vall_in rankf_ok ranki_ok rank_mm rankrow_ok rank_out zeros_ok emptied moved")
        hotlo_ok = sems(nc, ctx, "r", "hotlo0 hotlo1")
        hothi_ok = sems(nc, ctx, "r", "hothi0 hothi1")
        hot_used = sems(nc, ctx, "r", "hot_used0 hot_used1")
        steps = EC // GRP // 2
        block = ctx.enter_context(nc.Block())

        @block.sync
        def _(sp):
            sp.dma_start(src_i[:], a["src"]).then_inc(src_in, 16)
            sp.dma_start(ident[:], a["ident"]).then_inc(other_in, 16)
            sp.dma_start(noise[:], a["noise"]).then_inc(other_in, 16)
            sp.dma_start(xrows[:], t["xn"].rearrange("(i p) f -> p i f", p=P)).then_inc(xrows_in, 16)
            sp.wait_ge(zeros_ok, START + 1)
            sp.dma_start(t["xd"].rearrange("(s p) f -> p s f", p=P), zeros[:].unsqueeze(1).to_broadcast([P, XSLOTS, D])).then_inc(emptied, 16)
            sp.wait_ge(vrow_ok, START + 1)
            sp.dma_start(t["v"].rearrange("(i p) -> i p", p=P), v_row[:]).then_inc(vrow_out, 16)
            sp.wait_ge(vrow_out, START + 16)
            sp.dma_start(v_all[:], t["v"].unsqueeze(0).to_broadcast([P, NP])).then_inc(vall_in, 16)
            sp.wait_ge(rankrow_ok, START + 1)
            sp.dma_start(t["rank"].rearrange("(i p) -> i p", p=P), rank_row[:]).then_inc(rank_out, 16)
            sp.wait_ge(rank_out, START + 16)
            sp.wait_ge(moved, 16 * NT)
            sp.wait_ge(emptied, START + 16)

        @block.gpsimd
        def _(pool):
            nc.gpsimd.iota(count[:], [[1, P]], base=0, channel_multiplier=0,
                           allow_small_or_imprecise_dtypes=True).then_inc(consts, 1)
            nc.gpsimd.memset(zero[:], 0.0).then_inc(consts, 1)
            nc.gpsimd.memset(zeros[:], 0.0).then_inc(zeros_ok, 1)
            nc.gpsimd.memset(before[:], TINY).then_inc(before_ok, 1)
            pool.wait_ge(before_ok, START + 1)
            nc.gpsimd.affine_select(out=before[:], in_=before[:], compare_op=ALU.is_gt, fill=0.0, base=NP,
                                    pattern=[[-1, 2 * NP]], channel_multiplier=1).then_inc(before_ok, 1)
            pool.wait_ge(xrows_in, START + 16)
            pool.wait_ge(ranki_ok, START + 1)
            for i in range(NT):
                nc.gpsimd.indirect_dma_start(
                    out=t["xs"], out_offset=bass.IndirectOffsetOnAxis(ap=rank_i[:, i:i + 1], axis=0),
                    in_=xrows[:, i, :], in_offset=None).then_inc(moved, 16)

        @block.vector
        def _(dve):
            dve.wait_ge(src_in, START + 16)
            nc.vector.tensor_single_scalar(part_i[:], src_i[:], P - 1, op=ALU.bitwise_and).then_inc(part_ok, 1)
            dve.wait_ge(part_ok, START + 1)
            nc.vector.tensor_copy(lo[:], part_i[:]).then_inc(lo_ok, 1)
            dve.wait_ge(lo_ok, START + 1)
            nc.vector.tensor_single_scalar(part_i[:], src_i[:], 7, op=ALU.logical_shift_right).then_inc(part_ok, 1)
            dve.wait_ge(part_ok, START + 2)
            nc.vector.tensor_copy(hi[:], part_i[:]).then_inc(hi_ok, 1)
            dve.wait_ge(consts, START + 2)
            dve.wait_ge(hi_ok, START + 1)
            with dve.Fori(0, steps) as i:
                for s in range(2):
                    cols = bass.ds((i * 2 + s) * GRP, GRP)
                    dve.wait_ge(hot_used[s], START + i)
                    for hot, val, n, done in ((hot_lo, lo, P, hotlo_ok), (hot_hi, hi, NT, hothi_ok)):
                        nc.vector.tensor_tensor(hot[:, s], count[0:EP, 0:n].unsqueeze(1).to_broadcast([EP, GRP, n]),
                                                val[:, cols].unsqueeze(2).to_broadcast([EP, GRP, n]),
                                                ALU.is_equal).then_inc(done[s], 1)
            dve.wait_ge(deg_ok, START + 1)
            dve.wait_ge(other_in, START + 32)
            nc.vector.tensor_tensor(v_col[:], deg_ps[:, 0:NT], noise[:], ALU.add).then_inc(vcol_ok, 1)
            dve.wait_ge(vrow_mm, START + 1)
            nc.vector.tensor_copy(v_row[:], row_ps[0:NT, 0:P]).then_inc(vrow_ok, 1)
            dve.wait_ge(vall_in, START + 16)
            dve.wait_ge(before_ok, START + 2)
            dve.wait_ge(vcol_ok, START + 1)
            with dve.Fori(0, NT) as i:
                dve.wait_ge(rankf_ok, START + i)
                nc.vector.scalar_tensor_tensor(hits[:], v_all[:], v_col[:, bass.ds(i, 1)], before[:, bass.ds(i * (-P) + NP, NP)],
                                               ALU.subtract, ALU.is_lt, accum_out=rank_f[:, bass.ds(i, 1)]).then_inc(rankf_ok, 1)
            dve.wait_ge(rankf_ok, START + NT)
            nc.vector.tensor_copy(rank_i[:], rank_f[:]).then_inc(ranki_ok, 1)
            dve.wait_ge(rank_mm, START + 1)
            nc.vector.tensor_copy(rank_row[:], row_ps[0:NT, 0:P]).then_inc(rankrow_ok, 1)

        @block.tensor
        def _(pe):
            pe.wait_ge(consts, START + 2)
            nc.tensor.matmul(deg_ps[:, 0:NT], zero[:], zero[:, 0:NT], start=True, stop=False, skip_group_check=True)
            with pe.Fori(0, steps) as i:
                for s in range(2):
                    pe.wait_ge(hotlo_ok[s], START + i + 1)
                    pe.wait_ge(hothi_ok[s], START + i + 1)
                    for g in range(GRP):
                        last = nc.tensor.matmul(deg_ps[:, 0:NT], hot_lo[:, s, g, :], hot_hi[:, s, g, :],
                                                start=False, stop=False, skip_group_check=True)
                    last.then_inc(hot_used[s], 1)
            nc.tensor.matmul(deg_ps[:, 0:NT], zero[:], zero[:, 0:NT], start=False, stop=True,
                             skip_group_check=True).then_inc(deg_ok, 1)
            pe.wait_ge(other_in, START + 32)
            pe.wait_ge(vcol_ok, START + 1)
            nc.tensor.transpose(row_ps[0:NT, 0:P], v_col[:], ident[:]).then_inc(vrow_mm, 1)
            pe.wait_ge(rankf_ok, START + NT)
            pe.wait_ge(vrow_ok, START + 1)
            nc.tensor.transpose(row_ps[0:NT, 0:P], rank_f[:], ident[:]).then_inc(rank_mm, 1)


STATES = 16
TAPS = 4
BC = 2 * STATES
PARTS = 3
DBC = PARTS * BC + STATES


def stage_mamba(nc, a, t):
    with ExitStack() as ctx:
        def two(name, shape, dt=F32):
            return [sb(nc, ctx, f"m_{name}{c}", shape, dt) for c in range(2)]

        ident = sb(nc, ctx, "m_ident", [P, P])
        w_in = sb(nc, ctx, "m_w_in", [P, H2, 2 * D])
        w_dbc = sb(nc, ctx, "m_w_dbc", [P, H2, DBC])
        w_dt = sb(nc, ctx, "m_w_dt", [DBC, D])
        w_out = sb(nc, ctx, "m_w_out", [P, H2, D])
        pick_f = sb(nc, ctx, "m_pick_f", [PARTS * BC, BC, P])
        pick = sb(nc, ctx, "m_pick", [PARTS * BC, BC, P], BF16)
        vecs = sb(nc, ctx, "m_vecs", [P, H2, TAPS + 3])
        a_log = sb(nc, ctx, "m_a_log", [P, H2, STATES])
        a_exp = sb(nc, ctx, "m_a_exp", [P, H2, STATES])
        a_neg = sb(nc, ctx, "m_a_neg", [P, H2, STATES])
        rows = sb(nc, ctx, "m_rows", [TT, TILES, D])
        xsT = sb(nc, ctx, "m_xsT", [P, H2, CH])
        tail = TAPS - 1
        xpad = sb(nc, ctx, "m_xpad", [P, H2, tail + CH])
        keep = sb(nc, ctx, "m_keep", [P, H2, tail])
        conv = sb(nc, ctx, "m_conv", [P, H2, CH])
        dbc = sb(nc, ctx, "m_dbc", [DBC, CH])
        rest = sb(nc, ctx, "m_rest", [PARTS * BC, CH])
        pre = sb(nc, ctx, "m_pre", [P, H2, CH])
        nabs = sb(nc, ctx, "m_nabs", [P, H2, CH])
        ex = sb(nc, ctx, "m_ex", [P, H2, CH])
        ex1 = sb(nc, ctx, "m_ex1", [P, H2, CH])
        lg = sb(nc, ctx, "m_lg", [P, H2, CH])
        zs, xc, dt, u = two("zs", [P, H2, CH]), two("xc", [P, H2, CH]), two("dt", [P, H2, CH]), two("u", [P, H2, CH])
        parts = two("parts", [PARTS * BC, CH], BF16)
        decay, drive, h_t, hc = (two(n, [P, H2, CH]) for n in ("decay", "drive", "h", "hc"))
        state = sb(nc, ctx, "m_state", [P, H2, STATES])
        ysum = sb(nc, ctx, "m_ysum", [P, H2, CH])
        yg = sb(nc, ctx, "m_yg", [P, H2, CH])
        yrow = sb(nc, ctx, "m_yrow", [TT, TILES, D])
        row_ps = ps(nc, ctx, "m_row_ps", [P, 512])
        lin_ps = ps(nc, ctx, "m_lin_ps", [P, 512])
        b_ps = ps(nc, ctx, "m_b_ps", [P, 2, 512])
        c_ps = ps(nc, ctx, "m_c_ps", [P, 2, 512])
        y_ps = ps(nc, ctx, "m_y_ps", [P, 2, 512])
        (w_ok, pick_ok, aexp_ok, aneg_ok, state0, rows_in, xs_mm, xs_ok, xz_mm, xz_ok, kept, keep_ok, tap, z_ok, xc_ok, dbc_mm,
         dbc_ok, rest_ok, parts_ok, dt_mm, pre_ok, nabs_ok, ex_ok, ex1_ok, lg_ok, resid, sum_ok, dt_ok, u_ok, ysum_ok, yg_ok,
         yrow_mm, yrow_ok, y_out) = sems(
            nc, ctx, "m", "w_ok pick_ok aexp_ok aneg_ok state0 rows_in xs_mm xs_ok xz_mm xz_ok kept keep_ok tap z_ok xc_ok "
            "dbc_mm dbc_ok rest_ok parts_ok dt_mm pre_ok nabs_ok ex_ok ex1_ok lg_ok resid sum_ok dt_ok u_ok ysum_ok yg_ok "
            "yrow_mm yrow_ok y_out")
        b_mm, c_mm, decay_ok, drive_ok, scanned, hc_ok, hc_used, saved = (
            sems(nc, ctx, "m", f"{n}0 {n}1") for n in "b_mm c_mm decay_ok drive_ok scanned hc_ok hc_used saved".split())
        U = STATES // 2
        block = ctx.enter_context(nc.Block())

        def chunks(eng, chunk):
            chunk(0, 0, True, False)
            with eng.Fori(0, NCH // 2 - 1) as i:
                for c in (1, 0):
                    chunk(i * 2 + (1 if c else 2), c, False, False)
            chunk(NCH - 1, 1, False, True)

        @block.sync
        def _(sp):
            loads = [(ident[:], a["ident"]), (w_in[:], halves(a["in_projT"])), (w_dbc[:], halves(a["x_projT"])),
                     (w_dt[:], a["dt_projT"]), (w_out[:], halves(a["out_projT"])), (pick_f[:], a["pick"]),
                     (vecs[:], halves(a["mamba_vecs"])), (a_log[:], halves(a["A_log"]))]
            sp.dma_start(rows[:], t["xs"][0:CH, :].rearrange("(j p) f -> p j f", p=TT)).then_inc(rows_in, 16)
            for dst, source in loads:
                sp.dma_start(dst, source).then_inc(w_ok, 16)
            with sp.Fori(1, NCH) as g:
                sp.wait_ge(xs_mm, START + 2 * g)
                sp.dma_start(rows[:], t["xs"][bass.ds(g * CH, CH), :].rearrange("(j p) f -> p j f", p=TT)).then_inc(rows_in, 16)
                sp.wait_ge(yrow_ok, START + 2 * g)
                sp.dma_start(t["y"][bass.ds((g - 1) * CH, CH), :].rearrange("(j p) f -> p j f", p=TT), yrow[:]).then_inc(y_out, 16)
            sp.wait_ge(yrow_ok, START + 2 * NCH)
            sp.dma_start(t["y"][(NCH - 1) * CH:, :].rearrange("(j p) f -> p j f", p=TT), yrow[:]).then_inc(y_out, 16)
            sp.wait_ge(y_out, START + 16 * NCH)

        @block.tensor
        def _(pe):
            def turn(g, p, outs=True):
                pe.wait_ge(rows_in, START + 16 * (g + 1))
                pe.wait_ge(xs_ok, START + 2 * g + p)
                if outs:
                    pe.wait_ge(yrow_ok, START + 2 * (g - 1))
                for k in range(H2):
                    for j in range(2):
                        last = nc.tensor.transpose(row_ps[:, (2 * k + j) * TT:(2 * k + j + 1) * TT],
                                                   rows[:, 2 * p + j, k * P:(k + 1) * P], ident[0:TT, 0:TT])
                last.then_inc(xs_mm, 1)

            def in_proj(g, m):
                pe.wait_ge(xs_ok, START + 2 * g + 2)
                pe.wait_ge(pre_ok, START + 2 * g) if m == 0 else pe.wait_ge(xz_ok, START + 2 * g + m) if m <= 2 else pe.wait_ge(z_ok, START + 2 * g + 1)
                for k in range(H2):
                    last = nc.tensor.matmul(lin_ps[:, 0:CH], w_in[:, k, m * P:(m + 1) * P], xsT[:, k, :],
                                            start=(k == 0), stop=(k == 1))
                last.then_inc(xz_mm, 1)

            def x_proj(g, c):
                pe.wait_ge(z_ok, START + 2 * g + 2)
                pe.wait_ge(xc_ok, START + 2 * g + 2)
                for k in range(H2):
                    last = nc.tensor.matmul(lin_ps[0:DBC, 0:CH], w_dbc[:, k, :], xc[c][:, k, :], start=(k == 0), stop=(k == 1))
                last.then_inc(dbc_mm, 1)

            def dt_proj(g, k):
                pe.wait_ge(dbc_ok, START + 2 * g + 2)
                pe.wait_ge(pre_ok, START + 2 * g + k)
                nc.tensor.matmul(lin_ps[:, 0:CH], w_dt[:, k * P:(k + 1) * P], dbc[:], start=True, stop=True).then_inc(dt_mm, 1)

            def spread_b(g, c, s):
                q, n = s % 2, s // 2
                pe.wait_ge(parts_ok, START + 2 * g + 2)
                pe.wait_ge(drive_ok[q], START + U * g + n)
                nc.tensor.matmul(b_ps[:, q, 0:CH], pick[:, s, :], parts[c][:], start=True, stop=True).then_inc(b_mm[q], 1)

            def spread_c(g, c, s):
                q, n = s % 2, s // 2
                pe.wait_ge(hc_ok[q], START + U * g + n)
                nc.tensor.matmul(c_ps[:, q, 0:CH], pick[:, STATES + s, :], parts[c][:], start=True, stop=True).then_inc(c_mm[q], 1)

            def add(g, s):
                q, n = s % 2, s // 2
                if s == 0:
                    pe.wait_ge(ysum_ok, START + 2 * g)
                pe.wait_ge(hc_ok[q], START + U * g + n + 1)
                for k in range(H2):
                    last = nc.tensor.matmul(y_ps[:, k, 0:CH], ident[:], hc[q][:, k, :], start=(s == 0), stop=(s == STATES - 1))
                last.then_inc(hc_used[q], 1)

            def out_rows(g, p, end=False):
                pe.wait_ge(yg_ok, START + g + 1)
                pe.wait_ge(yrow_ok, START + 2 * g + p)
                if not end:
                    pe.wait_ge(xs_ok, START + 2 * (g + 2))
                for j in range(2):
                    for k in range(H2):
                        last = nc.tensor.matmul(row_ps[0:TT, j * D:(j + 1) * D], yg[:, k, (2 * p + j) * TT:(2 * p + j + 1) * TT],
                                                w_out[:, k, :], start=(k == 0), stop=(k == 1))
                last.then_inc(yrow_mm, 1)

            def chunk(g, c, first, final):
                for s in range(STATES):
                    if s + 1 < STATES:
                        spread_c(g, c, s + 1)
                    elif not final:
                        spread_c(g + 1, 1 - c, 0)
                    if s + 2 < STATES:
                        spread_b(g, c, s + 2)
                    elif not final:
                        spread_b(g + 1, 1 - c, s + 2 - STATES)
                    if s > 0:
                        add(g, s - 1)
                    elif not first:
                        add(g - 1, STATES - 1)
                    if s in (1, 2) and not first:
                        out_rows(g - 1, s - 1)
                    if s in (3, 4) and not final:
                        turn(g + 1, s - 3, not first)
                    if not final:
                        if 5 <= s <= 8:
                            in_proj(g + 1, s - 5)
                        if s == 9:
                            x_proj(g + 1, 1 - c)
                        if s in (10, 11):
                            dt_proj(g + 1, s - 10)

            pe.wait_ge(w_ok, START + 16 * 8)
            pe.wait_ge(pick_ok, START + 1)
            for p in range(2):
                turn(0, p, False)
            for m in range(4):
                in_proj(0, m)
            x_proj(0, 0)
            for k in range(H2):
                dt_proj(0, k)
            spread_b(0, 0, 0)
            spread_b(0, 0, 1)
            spread_c(0, 0, 0)
            chunks(pe, chunk)
            add(NCH - 1, STATES - 1)
            for p in range(2):
                out_rows(NCH - 1, p, True)

        @block.scalar
        def _(act):
            def turned(g, p):
                act.wait_ge(xs_mm, START + 2 * g + p + 1)
                act.wait_ge(xz_mm, START + 4 * g)
                nc.scalar.activation(xsT[:, :, 2 * p * TT:2 * (p + 1) * TT],
                                     row_ps[:, 0:2 * H2 * TT].rearrange("p (k n) -> p k n", k=H2), ACT.Copy).then_inc(xs_ok, 1)

            def carry(g):
                act.wait_ge(tap, START + 8 * g)
                act.wait_ge(kept, START + g)
                nc.scalar.activation(xpad[:, :, 0:tail], keep[:], ACT.Copy).then_inc(keep_ok, 1)

            def conv_in(g, m):
                act.wait_ge(xz_mm, START + 4 * g + m + 1)
                act.wait_ge(keep_ok, START + g + 1)
                nc.scalar.activation(xpad[:, m, tail:], lin_ps[:, 0:CH], ACT.Copy).then_inc(xz_ok, 1)
                if m == 1:
                    act.wait_ge(xz_ok, START + 2 * g + 2)
                    nc.scalar.activation(keep[:], xpad[:, :, CH:], ACT.Copy).then_inc(kept, 1)

            def gate(g, c, m, ahead=True):
                act.wait_ge(xz_mm, START + 4 * g + m + 3)
                if ahead:
                    act.wait_ge(yg_ok, START + g - 1)
                nc.scalar.activation(zs[c][:, m, :], lin_ps[:, 0:CH], ACT.Silu).then_inc(z_ok, 1)

            def conv_out(g, c, k, ahead=True):
                act.wait_ge(tap, START + 8 * g + 4 * k + 4)
                if ahead:
                    act.wait_ge(ysum_ok, START + 2 * (g - 1))
                nc.scalar.activation(xc[c][:, k, :], conv[:, k, :], ACT.Silu, bias=vecs[:, k, TAPS:TAPS + 1]).then_inc(xc_ok, 1)

            def split_high(g, c, ahead=True):
                act.wait_ge(dbc_mm, START + g + 1)
                act.wait_ge(dt_mm, START + 2 * g)
                act.wait_ge(parts_ok, START + 2 * g)
                nc.scalar.activation(dbc[:], lin_ps[0:DBC, 0:CH], ACT.Copy).then_inc(dbc_ok, 1)
                if ahead:
                    act.wait_ge(c_mm[1], START + U * (g - 1))
                nc.scalar.activation(parts[c][:], lin_ps[0:PARTS * BC, 0:CH], ACT.Copy).then_inc(dbc_ok, 1)

            def exp_dt(g):
                act.wait_ge(nabs_ok, START + g + 1)
                nc.scalar.activation(ex[:], nabs[:], ACT.Exp).then_inc(ex_ok, 1)

            def log_dt(g):
                act.wait_ge(ex1_ok, START + g + 1)
                nc.scalar.activation(lg[:], ex1[:], ACT.Ln).then_inc(lg_ok, 1)

            def decays(g, c, s):
                q, n = s % 2, s // 2
                if s == 0:
                    act.wait_ge(dt_ok, START + g + 1)
                act.wait_ge(scanned[q], START + 2 * (U * g + n))
                for k in range(H2):
                    nc.scalar.activation(decay[q][:, k, :], dt[c][:, k, :], ACT.Exp, scale=a_neg[:, k, s:s + 1]).then_inc(decay_ok[q], 1)

            def save(g, s):
                q, n = s % 2, s // 2
                act.wait_ge(scanned[q], START + 2 * (U * g + n) + 2)
                nc.scalar.activation(state[:, :, s:s + 1], h_t[q][:, :, CH - 1:CH], ACT.Copy).then_inc(saved[q], 1)

            def out_row(g, p):
                act.wait_ge(yrow_mm, START + 2 * g + p + 1)
                act.wait_ge(y_out, START + 16 * g)
                nc.scalar.activation(yrow[:, 2 * p:2 * p + 2, :].rearrange("p j f -> p (j f)"), row_ps[0:TT, 0:2 * D],
                                     ACT.Copy).then_inc(yrow_ok, 1)

            def chunk(g, c, first, final):
                for s in range(STATES):
                    if s + 1 < STATES:
                        decays(g, c, s + 1)
                    elif not final:
                        decays(g + 1, 1 - c, 0)
                    if s > 0:
                        save(g, s - 1)
                    elif not first:
                        save(g - 1, STATES - 1)
                    if s in (1, 2) and not first:
                        out_row(g - 1, s - 1)
                    if not final:
                        if s in (3, 4):
                            turned(g + 1, s - 3)
                        if s == 5:
                            carry(g + 1)
                        if s in (5, 6):
                            conv_in(g + 1, s - 5)
                        if s in (7, 8):
                            gate(g + 1, 1 - c, s - 7, not first)
                            conv_out(g + 1, 1 - c, s - 7, not first)
                        if s == 9:
                            split_high(g + 1, 1 - c, not first)
                        if s == 12:
                            exp_dt(g + 1)
                        if s == 13:
                            log_dt(g + 1)

            act.wait_ge(w_ok, START + 16 * 8)
            nc.scalar.activation(pick[:], pick_f[:], ACT.Copy).then_inc(pick_ok, 1)
            nc.scalar.activation(a_exp[:], a_log[:], ACT.Exp).then_inc(aexp_ok, 1)
            act.wait_ge(aneg_ok, START + 1)
            act.wait_ge(state0, START + 2)
            for p in range(2):
                turned(0, p)
            carry(0)
            for m in range(2):
                conv_in(0, m)
            for m in range(2):
                gate(0, 0, m, False)
                conv_out(0, 0, m, False)
            split_high(0, 0, False)
            exp_dt(0)
            log_dt(0)
            decays(0, 0, 0)
            chunks(act, chunk)
            for p in range(2):
                out_row(NCH - 1, p)

        @block.gpsimd
        def _(pool):
            nc.gpsimd.memset(state[:], 0.0).then_inc(state0, 1)
            nc.gpsimd.memset(keep[:], 0.0).then_inc(state0, 1)

        @block.vector
        def _(dve):
            def convolve(g, k):
                dve.wait_ge(keep_ok, START + g + 1)
                dve.wait_ge(xc_ok, START + 2 * g)
                dve.wait_ge(xz_ok, START + 2 * g + k + 1)
                nc.vector.tensor_scalar(conv[:, k, :], xpad[:, k, 0:CH], vecs[:, k, 0:1], None, ALU.mult).then_inc(tap, 1)
                for c in range(1, TAPS):
                    dve.wait_ge(tap, START + 8 * g + 4 * k + c)
                    nc.vector.scalar_tensor_tensor(conv[:, k, :], xpad[:, k, c:c + CH], vecs[:, k, c:c + 1], conv[:, k, :],
                                                   ALU.mult, ALU.add).then_inc(tap, 1)

            def split_low(g, c):
                mid, low = slice(BC, 2 * BC), slice(2 * BC, 3 * BC)
                dve.wait_ge(dbc_ok, START + 2 * g + 2)
                nc.vector.tensor_tensor(rest[low], dbc[low], parts[c][low], ALU.subtract).then_inc(rest_ok, 1)
                nc.vector.tensor_tensor(parts[c][mid], dbc[mid], parts[c][mid], ALU.subtract).then_inc(parts_ok, 1)
                dve.wait_ge(rest_ok, START + 2 * g + 1)
                nc.vector.tensor_copy(parts[c][low], rest[low]).then_inc(rest_ok, 1)
                dve.wait_ge(rest_ok, START + 2 * g + 2)
                nc.vector.tensor_tensor(parts[c][low], rest[low], parts[c][low], ALU.subtract).then_inc(parts_ok, 1)

            def dt_in(g, k):
                dve.wait_ge(dt_mm, START + 2 * g + k + 1)
                nc.vector.tensor_scalar(pre[:, k, :], lin_ps[:, 0:CH], vecs[:, k, TAPS + 1:TAPS + 2], None, ALU.add).then_inc(pre_ok, 1)

            def dt_abs(g):
                dve.wait_ge(pre_ok, START + 2 * g + 2)
                dve.wait_ge(ex_ok, START + g)
                nc.vector.scalar_tensor_tensor(nabs[:], pre[:], -1.0, pre[:], ALU.mult, ALU.min).then_inc(nabs_ok, 1)

            def dt_one(g):
                dve.wait_ge(ex_ok, START + g + 1)
                nc.vector.tensor_scalar(ex1[:], ex[:], 1.0, None, ALU.add).then_inc(ex1_ok, 1)

            def dt_out(g, c, ahead=True):
                dve.wait_ge(ex1_ok, START + g + 1)
                dve.wait_ge(lg_ok, START + g + 1)
                nc.vector.scalar_tensor_tensor(nabs[:], ex1[:], -1.0, ex[:], ALU.add, ALU.subtract).then_inc(resid, 1)
                dve.wait_ge(resid, START + g + 1)
                nc.vector.tensor_tensor(nabs[:], lg[:], nabs[:], ALU.subtract).then_inc(sum_ok, 1)
                dve.wait_ge(sum_ok, START + g + 1)
                if ahead:
                    dve.wait_ge(decay_ok[1], START + 2 * U * (g - 1))
                nc.vector.scalar_tensor_tensor(dt[c][:], pre[:], 0.0, nabs[:], ALU.max, ALU.add).then_inc(dt_ok, 1)

            def dt_x(g, c):
                dve.wait_ge(dt_ok, START + g + 1)
                dve.wait_ge(xc_ok, START + 2 * g + 2)
                nc.vector.tensor_tensor(u[c][:], dt[c][:], xc[c][:], ALU.mult).then_inc(u_ok, 1)

            def drives(g, c, s):
                q, n = s % 2, s // 2
                if s == 0:
                    dve.wait_ge(u_ok, START + g + 1)
                dve.wait_ge(b_mm[q], START + U * g + n + 1)
                dve.wait_ge(scanned[q], START + 2 * (U * g + n))
                nc.vector.tensor_tensor(drive[q][:], u[c][:], over_halves(b_ps[:, q, 0:CH]), ALU.mult).then_inc(drive_ok[q], 1)

            def scan(g, s):
                q, n = s % 2, s // 2
                dve.wait_ge(drive_ok[q], START + U * g + n + 1)
                dve.wait_ge(saved[q], START + U * g + n)
                dve.wait_ge(hc_ok[q], START + U * g + n)
                for k in range(H2):
                    dve.wait_ge(decay_ok[q], START + 2 * (U * g + n) + k + 1)
                    nc.vector.tensor_tensor_scan(h_t[q][:, k, :], decay[q][:, k, :], drive[q][:, k, :],
                                                 state[:, k, s:s + 1], ALU.mult, ALU.add).then_inc(scanned[q], 1)

            def read_out(g, s):
                q, n = s % 2, s // 2
                dve.wait_ge(c_mm[q], START + U * g + n + 1)
                dve.wait_ge(scanned[q], START + 2 * (U * g + n) + 2)
                dve.wait_ge(hc_used[q], START + U * g + n)
                nc.vector.tensor_tensor(hc[q][:], h_t[q][:], over_halves(c_ps[:, q, 0:CH]), ALU.mult).then_inc(hc_ok[q], 1)

            def gated(g, c):
                dve.wait_ge(hc_used[1], START + U * g + U)
                dve.wait_ge(yg_ok, START + g)
                for k in range(H2):
                    nc.vector.scalar_tensor_tensor(ysum[:, k, :], xc[c][:, k, :], vecs[:, k, TAPS + 2:TAPS + 3], y_ps[:, k, 0:CH],
                                                   ALU.mult, ALU.add).then_inc(ysum_ok, 1)
                dve.wait_ge(ysum_ok, START + 2 * g + 2)
                dve.wait_ge(z_ok, START + 2 * g + 2)
                dve.wait_ge(yrow_mm, START + 2 * g)
                nc.vector.tensor_tensor(yg[:], ysum[:], zs[c][:], ALU.mult).then_inc(yg_ok, 1)

            def chunk(g, c, first, final):
                for s in range(STATES):
                    if s + 1 < STATES:
                        drives(g, c, s + 1)
                    elif not final:
                        drives(g + 1, 1 - c, 0)
                    scan(g, s)
                    read_out(g, s)
                    if s == 0 and not first:
                        gated(g - 1, 1 - c)
                    if not final:
                        if s in (6, 7):
                            convolve(g + 1, s - 6)
                        if s == 10:
                            split_low(g + 1, 1 - c)
                        if s in (10, 11):
                            dt_in(g + 1, s - 10)
                        if s == 11:
                            dt_abs(g + 1)
                        if s == 12:
                            dt_one(g + 1)
                        if s == 13:
                            dt_out(g + 1, 1 - c, not first)
                        if s == 14:
                            dt_x(g + 1, 1 - c)

            dve.wait_ge(aexp_ok, START + 1)
            nc.vector.tensor_scalar(a_neg[:], a_exp[:], -1.0, None, ALU.mult).then_inc(aneg_ok, 1)
            dve.wait_ge(state0, START + 2)
            for k in range(H2):
                convolve(0, k)
            split_low(0, 0)
            for k in range(H2):
                dt_in(0, k)
            dt_abs(0)
            dt_one(0)
            dt_out(0, 0, False)
            dt_x(0, 0)
            drives(0, 0, 0)
            chunks(dve, chunk)
            gated(NCH - 1, 1)


QUAD = 4
RING = 6
PAIR = 2
PAIRS = QUAD // PAIR
PAIRS_ALL = -(-(-(-E // (P * PAIR)) + NT) // (RING * PAIRS)) * RING * PAIRS
PAIR_SHIFT = 8
CODE = HEADS + 1
BIG = 1e30


def stage_attend(nc, a, t):
    with ExitStack() as ctx:
        ident = sb(nc, ctx, "g_ident", [P, P])
        token = sb(nc, ctx, "g_token", [P, 2])
        count = sb(nc, ctx, "g_count", [P, P])
        ones = sb(nc, ctx, "g_ones", [P, P])
        below = sb(nc, ctx, "g_below", [P, P])
        dst_i = sb(nc, ctx, "g_dst_i", [EP, EC], I32)
        dst_f = sb(nc, ctx, "g_dst_f", [EP, EC])
        ones_e = sb(nc, ctx, "g_ones_e", [EP, EC])
        less = sb(nc, ctx, "g_less", [EP, EC])
        bound = sb(nc, ctx, "g_bound", [P, NT + 1])
        part = sb(nc, ctx, "g_part", [EP, NT + 1])
        first = sb(nc, ctx, "g_first", [NT, 4])
        slots_i = sb(nc, ctx, "g_slots_i", [NT, 1], I32)
        tile_no = sb(nc, ctx, "g_tile_no", [NT, P])
        kk = sb(nc, ctx, "g_kk", [NT, PAIRS_ALL])
        hot = sb(nc, ctx, "g_hot", [NT, PAIRS_ALL])
        hot2 = sb(nc, ctx, "g_hot2", [NT, PAIRS_ALL])
        at = sb(nc, ctx, "g_at", [NT, PAIRS_ALL])
        slot_at = sb(nc, ctx, "g_slot_at", [1, PAIRS_ALL], I32)
        slot_tile = sb(nc, ctx, "g_slot_tile", [1, PAIRS_ALL], I32)
        slot_base = sb(nc, ctx, "g_slot_base", [P, PAIRS_ALL])
        score = sb(nc, ctx, "g_score", [P, NT, 2 * HEADS])
        code = sb(nc, ctx, "g_code", [P, NT, CODE])
        top = sb(nc, ctx, "g_top", [P, 8])
        top8 = sb(nc, ctx, "g_top8", [8, 1])
        lift = sb(nc, ctx, "g_lift", [1, 8])
        shift = sb(nc, ctx, "g_shift", [P, 1])
        guard = sb(nc, ctx, "g_guard", [P, 1])
        emax = sb(nc, ctx, "g_emax", [P, QUAD * HEADS])
        agg = sb(nc, ctx, "g_agg", [P, NT, D + HEADS])
        den = sb(nc, ctx, "g_den", [P, NT, HEADS])
        idx = sb(nc, ctx, "g_idx", [P, RING, QUAD, 2], I32)
        rel = sb(nc, ctx, "g_rel", [P, RING, QUAD])
        got = sb(nc, ctx, "g_got", [P, RING, QUAD, ROW])
        sel = sb(nc, ctx, "g_sel", [P, RING, QUAD, P])
        selT = sb(nc, ctx, "g_selT", [P, RING, QUAD, P])
        z = sb(nc, ctx, "g_z", [P, RING, QUAD, HEADS])
        pen = sb(nc, ctx, "g_pen", [P, RING, QUAD])
        lr = sb(nc, ctx, "g_lr", [P, RING, QUAD, HEADS])
        logit = sb(nc, ctx, "g_logit", [P, RING, QUAD, HEADS])
        wrow = sb(nc, ctx, "g_wrow", [P, RING, QUAD, D + HEADS])
        selT_ps = ps(nc, ctx, "g_selT_ps", [P, 2, 512])
        st_ps = ps(nc, ctx, "g_st_ps", [P, 2, 512])
        acc_ps = ps(nc, ctx, "g_acc_ps", [P, QUAD, 512])
        set_ps = acc_ps[:, 0:2, :]
        (settled, w_ok, score_in, consts, zeroed, dve_set, pe_set, act_set, emax_ok, fin, stored) = sems(
            nc, ctx, "g", "settled w_ok score_in consts zeroed dve_set pe_set act_set emax_ok fin stored")
        (idx_in, rel_ok, got_in, sel_ok, selT_mm, selT_ok, st_mm, z_ok, pen_ok, lr_ok, logit_ok, exp_ok, w_row_ok) = (
            sems(nc, ctx, "g", " ".join(f"{n}{q}" for q in range(RING))) for n in
            "idx_in rel_ok got_in sel_ok selT_mm selT_ok st_mm z_ok pen_ok lr_ok logit_ok exp_ok w_row_ok".split())
        acc_mm, acc_ok = (sems(nc, ctx, "g", " ".join(f"{n}{m}" for m in range(QUAD))) for n in ("acc_mm", "acc_ok"))
        HS = PAIRS_ALL // 2
        quads = PAIRS_ALL // PAIRS
        block = ctx.enter_context(nc.Block())

        def there(i, j):
            return not isinstance(i, int) or 0 <= RING * i + j < quads

        def done(eng, sem, i, j, each=1):
            if there(i, j):
                eng.wait_ge(sem[j % RING], START + each * (i + j // RING + 1))

        def uses(i, j):
            return i * (RING // 2) + j // 2

        def summed(eng, i, j):
            if there(i, j):
                eng.wait_ge(acc_mm[PAIRS * (j % 2) + PAIRS - 1], START + uses(i, j) + 1)

        def steps(eng, step, ahead):
            for k in range(-ahead, RING):
                step(k // RING, k % RING)
            with eng.Fori(1, quads // RING - 1) as i:
                for j in range(RING):
                    step(i, j)
            for k in range(quads - RING, quads + 1):
                step(k // RING, k % RING)

        @block.sync
        def _(sp):
            for dst, source in ((ident[:], a["ident"]), (below[:], a["below"]), (dst_i[:], a["dst"])):
                sp.dma_start(dst, source).then_inc(w_ok, 16)
            sp.dma_start(score[:], t["table"].rearrange("(i p) f -> p i f", p=P)[:, :, D:ROW]).then_inc(score_in, 16)
            sp.wait_ge(dve_set, START + 13)

            def step(i, j):
                if not there(i, j):
                    return
                q = j % RING
                done(sp, rel_ok, i, j - RING)
                if there(i, j - RING):
                    sp.wait_ge(got_in[q], 16 * QUAD * (i - 1) + 16 * QUAD)
                for b in range(PAIRS):
                    e0 = sp.value_load(slot_at[0:1, bass.ds((i * RING + j) * PAIRS + b, 1)], min_val=0, max_val=E)
                    sp.dma_start(idx[:, q, b * PAIR:(b + 1) * PAIR, :],
                                 a["edges"][bass.ds(e0, P * PAIR), :].rearrange("(m p) c -> p m c", p=P)).then_inc(idx_in[q], 16)

            steps(sp, step, 0)
            sp.wait_ge(fin, START + 3)
            sp.dma_start(t["agg"].rearrange("(i p) f -> p i f", p=P), agg[:, :, 0:D]).then_inc(stored, 16)
            sp.wait_ge(stored, START + 16)

        @block.gpsimd
        def _(pool):
            nc.gpsimd.iota(count[:], [[1, P]], base=0, channel_multiplier=0, allow_small_or_imprecise_dtypes=True).then_inc(consts, 1)
            nc.gpsimd.iota(bound[:], [[P, NT + 1]], base=0, channel_multiplier=0, allow_small_or_imprecise_dtypes=True).then_inc(consts, 1)
            nc.gpsimd.iota(tile_no[:], [[0, P]], base=0, channel_multiplier=1, allow_small_or_imprecise_dtypes=True).then_inc(consts, 1)
            nc.gpsimd.iota(kk[:], [[1, PAIRS_ALL]], base=0, channel_multiplier=0, allow_small_or_imprecise_dtypes=True).then_inc(consts, 1)
            nc.gpsimd.memset(ones[:], 1.0).then_inc(consts, 1)
            nc.gpsimd.memset(ones_e[:], 1.0).then_inc(consts, 1)
            nc.gpsimd.memset(code[:], 1.0).then_inc(consts, 1)
            nc.gpsimd.memset(emax[:], -BIG).then_inc(zeroed, 1)
            nc.gpsimd.memset(agg[:], 0.0).then_inc(zeroed, 1)
            nc.gpsimd.memset(token[:], 0.0).then_inc(zeroed, 1)
            pool.wait_ge(zeroed, START + 3)

            def step(i, j):
                if not there(i, j):
                    return
                q = j % RING
                done(pool, w_row_ok, i, j - RING)
                done(pool, idx_in, i, j, 16 * PAIRS)
                settle(nc, pool, token, settled, i * RING + j)
                for m in range(QUAD):
                    nc.gpsimd.indirect_dma_start(
                        out=got[:, q, m, :], out_offset=None, in_=t["table"],
                        in_offset=bass.IndirectOffsetOnAxis(ap=idx[:, q, m, 0:1], axis=0)).then_inc(got_in[q], 16)

            steps(pool, step, 0)

        @block.tensor
        def _(pe):
            pe.wait_ge(w_ok, START + 48)
            pe.wait_ge(consts, START + 7)
            pe.wait_ge(dve_set, START + 2)
            nc.tensor.matmul(set_ps[0:NT, 0, 0:1], part[:, 0:NT], ones[0:EP, 0:1], start=True, stop=True)
            nc.tensor.matmul(set_ps[0:NT, 0, 1:2], part[:, 1:NT + 1], ones[0:EP, 0:1], start=True, stop=True).then_inc(pe_set, 1)
            pe.wait_ge(dve_set, START + 7)
            nc.tensor.matmul(set_ps[0:NT, 0, 2:3], below[0:NT, 0:NT], first[:, 2:3], start=True, stop=True).then_inc(pe_set, 1)
            pe.wait_ge(dve_set, START + 12)
            for c in range(2):
                cols = slice(c * HS, (c + 1) * HS)
                pe.wait_ge(dve_set, START + (12 if c == 0 else 13))
                nc.tensor.matmul(set_ps[0:1, 0, 0:HS], ones[0:NT, 0:1], at[:, cols], start=True, stop=True).then_inc(pe_set, 1)
                nc.tensor.matmul(set_ps[:, 1, 0:HS], tile_no[:], hot2[:, cols], start=True, stop=True).then_inc(pe_set, 1)
                pe.wait_ge(dve_set, START + 13 + 3 * c + 2)
            pe.wait_ge(dve_set, START + 20)
            nc.tensor.transpose(set_ps[0:8, 0, 0:P], top[:], ident[:]).then_inc(pe_set, 1)
            pe.wait_ge(dve_set, START + 21)
            nc.tensor.matmul(set_ps[0:1, 1, 0:8], top8[:], ident[0:8, 0:8], start=True, stop=True).then_inc(pe_set, 1)
            pe.wait_ge(dve_set, START + 26)
            nc.tensor.matmul(set_ps[:, 0, 0:1], ones[0:1, :], lift[:, 7:8], start=True, stop=True).then_inc(pe_set, 1)

            def turn(i, j):
                q, b = j % RING, j % 2
                done(pe, sel_ok, i, j)
                done(pe, selT_ok, i, j - 2)
                for m in range(QUAD):
                    last = nc.tensor.transpose(selT_ps[:, b, m * P:(m + 1) * P], sel[:, q, m, :], ident[:])
                last.then_inc(selT_mm[q], 1)

            def target_scores(i, j):
                q, b = j % RING, j % 2
                tiles = [pe.value_load(slot_tile[0:1, bass.ds((i * RING + j) * PAIRS + b, 1)], min_val=0, max_val=NT - 1)
                         for b in range(PAIRS)]
                done(pe, selT_ok, i, j)
                done(pe, pen_ok, i, j - 2)
                for m in range(QUAD):
                    last = nc.tensor.matmul(st_ps[:, b, m * CODE:(m + 1) * CODE], selT[:, q, m, :],
                                            code[:, bass.ds(tiles[m // PAIR], 1), :], start=True, stop=True)
                last.then_inc(st_mm[q], 1)

            def sum_rows(i, j):
                q = j % RING
                done(pe, w_row_ok, i, j)
                for b in range(PAIRS):
                    bank = PAIRS * (j % 2) + b
                    pe.wait_ge(acc_ok[bank], START + uses(i, j))
                    for m in range(PAIR):
                        last = nc.tensor.matmul(acc_ps[:, bank, 0:D + HEADS], sel[:, q, b * PAIR + m, :], wrow[:, q, b * PAIR + m, :],
                                                start=(m == 0), stop=(m == PAIR - 1))
                    last.then_inc(acc_mm[bank], 1)

            def step(i, j):
                for run, ahead in ((target_scores, 1), (turn, 2), (sum_rows, -1)):
                    if there(i, j + ahead):
                        run(i, j + ahead)

            steps(pe, step, 2)
            pe.wait_ge(fin, START + 1)
            nc.tensor.transpose(set_ps[0:1, 0, 0:P], top[:, 0:1], ident[:]).then_inc(pe_set, 1)
            pe.wait_ge(act_set, START + 1)
            nc.tensor.matmul(set_ps[:, 1, 0:1], ones[0:1, :], lift[:, 6:7], start=True, stop=True).then_inc(pe_set, 1)

        @block.scalar
        def _(act):
            act.wait_ge(dve_set, START + 27)

            def copy_turned(i, j):
                q, b = j % RING, j % 2
                done(act, selT_mm, i, j)
                done(act, st_mm, i, j - RING)
                nc.scalar.activation(selT[:, q].rearrange("p j n -> p (j n)"), selT_ps[:, b, :], ACT.Copy).then_inc(selT_ok[q], 1)

            def exponential(i, j):
                q = j % RING
                done(act, logit_ok, i, j)
                summed(act, i, j - RING)
                nc.scalar.activation(wrow[:, q, :, D:], logit[:, q], ACT.Exp, bias=shift[:]).then_inc(exp_ok[q], 1)

            def step(i, j):
                for run, ahead in ((exponential, 1), (copy_turned, 2)):
                    if there(i, j + ahead):
                        run(i, j + ahead)

            steps(act, step, 2)
            act.wait_ge(fin, START + 2)
            nc.scalar.activation(lift[:, 6:7], lift[:, 5:6], ACT.Exp, bias=shift[0:1, :]).then_inc(act_set, 1)

        @block.vector
        def _(dve):
            step = [0]

            def set_up(ins):
                step[0] += 1
                ins.then_inc(dve_set, 1)
                dve.wait_ge(dve_set, START + step[0])

            dve.wait_ge(w_ok, START + 48)
            dve.wait_ge(consts, START + 7)
            set_up(nc.vector.tensor_copy(dst_f[:], dst_i[:]))
            for b in range(NT + 1):
                last = nc.vector.scalar_tensor_tensor(less[:], dst_f[:], bound[0:EP, b:b + 1], ones_e[:], ALU.is_lt, ALU.mult,
                                                      accum_out=part[:, b:b + 1])
                if b < NT:
                    last.then_inc(emax_ok, 1)
                    dve.wait_ge(emax_ok, START + b + 1)
            set_up(last)
            dve.wait_ge(pe_set, START + 1)
            set_up(nc.vector.tensor_copy(first[:, 0:2], set_ps[0:NT, 0, 0:2]))
            set_up(nc.vector.scalar_tensor_tensor(first[:, 1:2], first[:, 0:1], -1.0, first[:, 1:2], ALU.mult, ALU.add))
            set_up(nc.vector.tensor_scalar(slots_i[:], first[:, 1:2], float(P * PAIR - 1), None, ALU.add))
            set_up(nc.vector.tensor_single_scalar(slots_i[:], slots_i[:], PAIR_SHIFT, op=ALU.logical_shift_right))
            set_up(nc.vector.tensor_copy(first[:, 2:3], slots_i[:]))
            dve.wait_ge(pe_set, START + 2)
            set_up(nc.vector.tensor_copy(first[:, 3:4], set_ps[0:NT, 0, 2:3]))
            set_up(nc.vector.tensor_scalar(hot[:], kk[:], first[:, 3:4], None, ALU.is_ge))
            set_up(nc.vector.tensor_scalar(at[:], kk[:], first[:, 3:4], first[:, 2:3], ALU.subtract, ALU.subtract))
            set_up(nc.vector.scalar_tensor_tensor(hot2[:], at[:], 0.0, hot[:], ALU.is_lt, ALU.mult))
            nc.vector.tensor_scalar(hot[:], kk[:], first[:, 3:4], float(P * PAIR), ALU.subtract, ALU.mult).then_inc(emax_ok, 1)
            dve.wait_ge(emax_ok, START + NT + 1)
            nc.vector.tensor_scalar(at[:], hot[:], first[:, 0:1], float(-E), ALU.add, ALU.add).then_inc(emax_ok, 1)
            dve.wait_ge(emax_ok, START + NT + 2)
            set_up(nc.vector.tensor_tensor(at[:], at[:], hot2[:], ALU.mult))
            for c in range(2):
                cols = slice(c * HS, (c + 1) * HS)
                dve.wait_ge(pe_set, START + 4 + 2 * c)
                set_up(nc.vector.tensor_scalar(slot_at[:, cols], set_ps[0:1, 0, 0:HS], float(E), None, ALU.add))
                set_up(nc.vector.tensor_scalar(slot_base[:, cols], set_ps[:, 1, 0:HS], float(P), None, ALU.mult))
                set_up(nc.vector.tensor_copy(slot_tile[:, cols], set_ps[0:1, 1, 0:HS]))
            dve.wait_ge(score_in, START + 16)
            set_up(nc.vector.tensor_copy(code[:, :, 0:HEADS], score[:, :, HEADS:]))
            set_up(nc.vector.tensor_reduce(top[:], score[:].rearrange("p i h -> p h i"), AX.X, ALU.max))
            dve.wait_ge(pe_set, START + 7)
            set_up(nc.vector.tensor_reduce(top8[:], set_ps[0:8, 0, 0:P], AX.X, ALU.max))
            dve.wait_ge(pe_set, START + 8)
            set_up(nc.vector.tensor_copy(lift[:], set_ps[0:1, 1, 0:8]))
            set_up(nc.vector.tensor_tensor(lift[:, 0:4], lift[:, 0:4], lift[:, 4:8], ALU.add))
            set_up(nc.vector.scalar_tensor_tensor(lift[:, 0:4], lift[:, 0:4], 0.2, lift[:, 0:4], ALU.mult, ALU.max))
            set_up(nc.vector.tensor_reduce(lift[:, 4:5], lift[:, 0:4], AX.X, ALU.max))
            set_up(nc.vector.tensor_scalar(lift[:, 7:8], lift[:, 4:5], -1.0, None, ALU.mult))
            dve.wait_ge(pe_set, START + 9)
            set_up(nc.vector.tensor_copy(shift[:], set_ps[:, 0, 0:1]))
            dve.wait_ge(zeroed, START + 2)

            def select(i, j):
                q = j % RING
                done(dve, idx_in, i, j, 16 * PAIRS)
                nc.vector.tensor_tensor(rel[:, q].rearrange("p (b m) -> p b m", b=PAIRS), idx[:, q, :, 1].rearrange("p (b m) -> p b m", b=PAIRS),
                                        slot_base[:, bass.ds((i * RING + j) * PAIRS, PAIRS)].unsqueeze(2).to_broadcast([P, PAIRS, PAIR]),
                                        ALU.subtract).then_inc(rel_ok[q], 1)
                done(dve, rel_ok, i, j)
                summed(dve, i, j - RING)
                nc.vector.tensor_tensor(sel[:, q], count[:].unsqueeze(1).to_broadcast([P, QUAD, P]),
                                        rel[:, q].unsqueeze(2).to_broadcast([P, QUAD, P]), ALU.is_equal).then_inc(sel_ok[q], 1)

            def logits(i, j):
                q, b = j % RING, j % 2
                done(dve, st_mm, i, j)
                dve.wait_ge(got_in[q], 16 * QUAD * (i + j // RING + 1))
                st = st_ps[:, b, 0:QUAD * CODE].rearrange("p (j c) -> p j c", c=CODE)
                nc.vector.tensor_tensor(z[:, q], got[:, q, :, D:D + HEADS], st[:, :, 0:HEADS], ALU.add).then_inc(z_ok[q], 1)
                nc.vector.tensor_scalar(pen[:, q], st[:, :, HEADS], BIG, -BIG, ALU.mult, ALU.add).then_inc(pen_ok[q], 1)
                done(dve, z_ok, i, j)
                nc.vector.scalar_tensor_tensor(lr[:, q], z[:, q], 0.2, z[:, q], ALU.mult, ALU.max).then_inc(lr_ok[q], 1)
                done(dve, lr_ok, i, j)
                done(dve, pen_ok, i, j)
                done(dve, exp_ok, i, j - RING)
                nc.vector.tensor_tensor(logit[:, q], lr[:, q], pen[:, q].unsqueeze(2).to_broadcast([P, QUAD, HEADS]),
                                        ALU.add).then_inc(logit_ok[q], 1)
                done(dve, logit_ok, i, j)
                dve.wait_ge(emax_ok, START + i * RING + j + NT + 2)
                nc.vector.tensor_tensor(emax[:], emax[:], logit[:, q].rearrange("p j h -> p (j h)"), ALU.max).then_inc(emax_ok, 1)

            def weigh(i, j, m):
                q = j % RING
                done(dve, exp_ok, i, j)
                last = nc.vector.tensor_tensor(wrow[:, q, m, 0:D].rearrange("p (h f) -> p h f", h=HEADS),
                                               got[:, q, m, 0:D].rearrange("p (h f) -> p h f", h=HEADS),
                                               wrow[:, q, m, D:].unsqueeze(2).to_broadcast([P, HEADS, FO]), ALU.mult)
                if m == QUAD - 1:
                    last.then_inc(w_row_ok[q], 1)

            def add(i, j, b):
                bank = PAIRS * (j % 2) + b
                tile = dve.value_load(slot_tile[0:1, bass.ds((i * RING + j) * PAIRS + b, 1)], min_val=0, max_val=NT - 1)
                dve.wait_ge(acc_mm[bank], START + uses(i, j) + 1)
                dve.wait_ge(acc_ok[bank - 1], START + uses(i, j) + (1 if bank else 0))
                here = agg[:, bass.ds(tile, 1), :].rearrange("p i f -> p (i f)")
                nc.vector.tensor_tensor(here, here, acc_ps[:, bank, 0:D + HEADS], ALU.add).then_inc(acc_ok[bank], 1)

            def step(i, j):
                for run, ahead in ((logits, 1), (select, 3)):
                    if there(i, j + ahead):
                        run(i, j + ahead)
                for m in range(QUAD):
                    if m % PAIR == 1 and there(i, j - 1):
                        add(i, j - 1, m // PAIR)
                    if there(i, j):
                        weigh(i, j, m)

            steps(dve, step, 3)
            dve.wait_ge(emax_ok, START + quads + NT + 2)
            nc.vector.tensor_reduce(top[:, 0:1], emax[:], AX.X, ALU.max).then_inc(fin, 1)
            dve.wait_ge(pe_set, START + 10)
            nc.vector.tensor_reduce(lift[:, 5:6], set_ps[0:1, 0, 0:P], AX.X, ALU.max).then_inc(fin, 1)
            dve.wait_ge(pe_set, START + 11)
            nc.vector.tensor_scalar(guard[:], set_ps[:, 1, 0:1], 1e-16, None, ALU.mult).then_inc(dve_set, 1)
            dve.wait_ge(dve_set, START + 28)
            for m in range(QUAD):
                dve.wait_ge(acc_ok[m], START + quads // 2)
            nc.vector.tensor_scalar(den[:], agg[:, :, D:], guard[:], None, ALU.add).then_inc(dve_set, 1)
            dve.wait_ge(dve_set, START + 29)
            nc.vector.reciprocal(den[:], den[:]).then_inc(dve_set, 1)
            dve.wait_ge(dve_set, START + 30)
            for i in range(NT):
                mean = agg[:, i, 0:D].rearrange("p (h f) -> p h f", h=HEADS)
                last = nc.vector.tensor_tensor(mean, mean, den[:, i, :].unsqueeze(2).to_broadcast([P, HEADS, FO]), ALU.mult)
            last.then_inc(fin, 1)


EXPERTS = 8
ATT_EPS = 1e-6
LNS = 7
(LN_LOCAL, LN_GLOBAL, LN_MSG, LN_GNN, LN_MIX, LN_ROUTER, LN_EXPERT) = range(LNS)
LIN_USES = 22


def stage_mix(nc, a, t):
    with ExitStack() as ctx:
        ident = sb(nc, ctx, "x_ident", [P, P])
        inv_d = sb(nc, ctx, "x_inv_d", [P, P])
        w2 = {n: sb(nc, ctx, f"x_{n}", [P, H2, D]) for n in ("wlT", "wgT", "Wq", "Wm")}
        w_ff1 = sb(nc, ctx, "x_ff1", [P, H2, 2 * D])
        w_ff2 = sb(nc, ctx, "x_ff2", [P, 4, D])
        w_m1 = sb(nc, ctx, "x_m1", [P, 4, 2 * D])
        w_m2 = sb(nc, ctx, "x_m2", [P, 4, D])
        w_r = sb(nc, ctx, "x_wr", [P, H2, EXPERTS])
        b_r = sb(nc, ctx, "x_br", [TT, EXPERTS])
        vecs = sb(nc, ctx, "x_vecs", [P, H2, 12])
        b_ff1 = sb(nc, ctx, "x_bff1", [P, 4])
        eps = sb(nc, ctx, "x_eps", [P, 1])
        att_eps = sb(nc, ctx, "x_att_eps", [P, 1])
        same = sb(nc, ctx, "x_same", [P, P])
        kv = sb(nc, ctx, "x_kv", [P, H2, KROW])
        kv_blk = sb(nc, ctx, "x_kv_blk", [P, H2, P])
        ks_blk = sb(nc, ctx, "x_ks_blk", [P, H2, P])
        rank = sb(nc, ctx, "x_rank", [TT, NTT], I32)

        def two(name, shape):
            return [sb(nc, ctx, f"x_{name}{q}", shape) for q in range(2)]

        x, xn, low, up, hl, ha, cent, sq, qp, msg, gate, h, res, mix = (
            two(n, [P, H2, CH]) for n in "x xn low up hl ha cent sq qp msg gate h res mix".split())
        std, den = two("std", [P, CH]), two("den", [P, H2, CH])
        y_at = [sb(nc, ctx, f"x_y_at{q}", [TT, TILES], I32) for q in range(2)]
        arow, yrow, x2row, xerow = (two(n, [TT, TILES, D]) for n in ("arow", "yrow", "x2row", "xerow"))
        wide = two("wide", [P, 4, CH])
        logit = two("logit", [TT, TILES, EXPERTS])
        mean_ps = [ps(nc, ctx, f"x_mean_ps{q}", [P, 512]) for q in range(2)]
        var_ps = [ps(nc, ctx, f"x_var_ps{q}", [P, 512]) for q in range(2)]
        lin_ps = [[ps(nc, ctx, f"x_lin_ps{q}{b}", [P, 512]) for b in range(2)] for q in range(2)]
        token = sb(nc, ctx, "x_token", [P, 2])
        settled, passed, w_ok, consts, token_ok, blk_ok = sems(nc, ctx, "x", "settled passed w_ok consts token_ok blk_ok")
        (arow_in, xn_in, x_in, y_at_ok, y_in, low_ok, up_ok, exp_ok, elu_ok, qlow_ok, qexp_ok, den_ok, diff_ok, gated_ok, h_ok,
         sum1_ok, sum2_ok, x2_ok, sq_ok, log_ok, norm_ok, gain_ok, stored) = (
            sems(nc, ctx, "x", f"{n}0 {n}1") for n in
            "arow_in xn_in x_in y_at_ok y_in low_ok up_ok exp_ok elu_ok qlow_ok qexp_ok den_ok diff_ok gated_ok h_ok "
            "sum1_ok sum2_ok x2_ok sq_ok log_ok norm_ok gain_ok stored".split())
        mean_full, mean_read, var_full, var_read = (
            sems(nc, ctx, "x", f"{n}0 {n}1") for n in "mean_full mean_read var_full var_read".split())
        lin_full = [sems(nc, ctx, "x", f"lin_full{q}0 lin_full{q}1") for q in range(2)]
        lin_read = [sems(nc, ctx, "x", f"lin_read{q}0 lin_read{q}1") for q in range(2)]
        MEAN_USES = 1 + LNS + 1
        VAR_USES = 1 + LNS
        BANK_USES = 1 + LIN_USES // 2 + TILES
        pairs = NCH // 2
        Q_, Y_ROWS, DEN, NUM, GATE, WM, FF1, FF2, M1, M2 = -2, 0, 2, 4, 6, 8, 10, 14, 16, 20
        block = ctx.enter_context(nc.Block())

        def v(n, k):
            return vecs[:, k, n:n + 1]

        def chunk(i, q):
            return bass.ds((i * 2 + q) * CH, CH)

        @block.sync
        def _(sp):
            loads = [(ident[:], a["ident"]), (w_ff1[:], halves(a["ff1T"])), (w_ff2[:], a["ff2T"].rearrange("(h p) n -> p h n", p=P)),
                     (w_m1[:], a["W1"].rearrange("(h p) n -> p h n", p=P)), (w_m2[:], a["W2"].rearrange("(h p) n -> p h n", p=P)),
                     (w_r[:], halves(a["Wr"])), (b_r[:], a["br"].unsqueeze(0).to_broadcast([TT, EXPERTS])),
                     (vecs[:], halves(a["mix_vecs"])), (b_ff1[:], a["ff1_b"]),
                     (same[:], a["same"]), (kv[:], t["kv"])]
            loads += [(w2[n][:], halves(a[n])) for n in w2]
            assert len(loads) == 15
            for dst, source in loads:
                sp.dma_start(dst, source).then_inc(w_ok, 16)
            with nc.allow_non_contiguous_dma(reason="one rank per partition and token tile"):
                sp.dma_start(rank[:], t["rank"].rearrange("(i p) -> p i", p=TT)).then_inc(w_ok, 16)

            def load(i, q, buf, source, done):
                sp.dma_start(buf[q][:], source).then_inc(done[q], 16)

            def load_agg(i, q):
                load(i, q, arow, t["agg"][chunk(i, q), :].rearrange("(j p) f -> p j f", p=TT), arow_in)

            def load_xn(i, q):
                load(i, q, xn, halves(t["xnT"])[:, :, chunk(i, q)], xn_in)

            def load_x(i, q):
                load(i, q, x, halves(a["xT"])[:, :, chunk(i, q)], x_in)

            def store(i):
                for q in range(2):
                    sp.wait_ge(mean_read[q], START + MEAN_USES * (i + 1))
                    sp.dma_start(t["logit"][chunk(i, q), :].rearrange("(j p) f -> p j f", p=TT), logit[q][:]).then_inc(stored[q], 16)
                    sp.wait_ge(lin_read[q][0], START + BANK_USES * (i + 1))
                    sp.dma_start(t["x2"][chunk(i, q), :].rearrange("(j p) f -> p j f", p=TT), x2row[q][:]).then_inc(stored[q], 16)
                    sp.wait_ge(lin_read[q][1], START + BANK_USES * (i + 1))
                    sp.dma_start(t["xe"][chunk(i, q), :].rearrange("(j p) f -> p j f", p=TT), xerow[q][:]).then_inc(stored[q], 16)

            for q in range(2):
                load_agg(0, q)
                load_xn(0, q)
                load_x(0, q)
            with sp.Fori(0, pairs - 1) as i:
                for q in range(2):
                    sp.wait_ge(var_full[q], START + VAR_USES * i + 1)
                    sp.sem_inc(passed, 1)
                    load_agg(i + 1, q)
                for q in range(2):
                    sp.wait_ge(norm_ok[q], START + LNS * i + LN_MIX + 1)
                    sp.sem_inc(passed, 1)
                    load_xn(i + 1, q)
                for q in range(2):
                    sp.wait_ge(lin_full[q][0], START + BANK_USES * (i + 1))
                    sp.sem_inc(passed, 1)
                    load_x(i + 1, q)
                store(i)
            store(pairs - 1)
            for q in range(2):
                sp.wait_ge(stored[q], START + 48 * pairs)

        @block.gpsimd
        def _(pool):
            nc.gpsimd.memset(inv_d[:], 1.0 / D).then_inc(consts, 1)
            nc.gpsimd.memset(eps[:], LN_EPS).then_inc(consts, 1)
            nc.gpsimd.memset(att_eps[:], ATT_EPS).then_inc(consts, 1)
            nc.gpsimd.memset(token[:], 0.0).then_inc(token_ok, 1)
            pool.wait_ge(token_ok, START + 1)
            with pool.Fori(0, pairs) as i:
                for q in range(2):
                    pool.wait_ge(y_at_ok[q], START + i + 1)
                    settle(nc, pool, token, settled, 2 * i + q)
                    for j in range(TILES):
                        nc.gpsimd.indirect_dma_start(
                            out=yrow[q][:, j, :], out_offset=None, in_=t["y"],
                            in_offset=bass.IndirectOffsetOnAxis(ap=y_at[q][:, j:j + 1], axis=0)).then_inc(y_in[q], 16)

        @block.tensor
        def _(pe):
            pe.wait_ge(w_ok, START + 256)
            pe.wait_ge(consts, START + 3)
            pe.wait_ge(blk_ok, START + 4)
            with pe.Fori(0, pairs) as i:
                def lin(q, u, products):
                    b, n = u % 2, u // 2 + 1
                    pe.wait_ge(lin_read[q][b], START + BANK_USES * i + n)
                    for m, (w, r) in enumerate(products):
                        last = nc.tensor.matmul(lin_ps[q][b][:, 0:CH], w, r, start=(m == 0), stop=(m == len(products) - 1))
                    last.then_inc(lin_full[q][b], 1)

                def dense(q, u, weights, inputs, outs):
                    for m in range(outs):
                        lin(q, u + m, [(w[:, k, m * P:(m + 1) * P], r) for (w, k), r in zip(weights, inputs)])

                def written(q, u):
                    pe.wait_ge(lin_read[q][u % 2], START + BANK_USES * i + u // 2 + 2)

                def mean_of(q, n, src):
                    pe.wait_ge(mean_read[q], START + MEAN_USES * i + 1 + n)
                    for k in range(H2):
                        last = nc.tensor.matmul(mean_ps[q][:, 0:CH], inv_d[:], src[q][:, k, :], start=(k == 0), stop=(k == 1))
                    last.then_inc(mean_full[q], 1)

                def var_of(n):
                    for q in TWO:
                        pe.wait_ge(sq_ok[q], START + LNS * i + n + 1)
                        pe.wait_ge(var_read[q], START + VAR_USES * i + 1 + n)
                        for k in range(H2):
                            last = nc.tensor.matmul(var_ps[q][:, 0:CH], inv_d[:], sq[q][:, k, :], start=(k == 0), stop=(k == 1))
                        last.then_inc(var_full[q], 1)

                def xh(buf, q):
                    return [buf[q][:, k, :] for k in range(buf[q].shape[1])]

                TWO = range(2)
                for q in TWO:
                    pe.wait_ge(arow_in[q], START + 16 * (i + 1))
                    for k, (bank, read, uses, full) in enumerate(((mean_ps, mean_read, MEAN_USES, mean_full),
                                                                  (var_ps, var_read, VAR_USES, var_full))):
                        pe.wait_ge(read[q], START + uses * i)
                        for j in range(TILES):
                            last = nc.tensor.transpose(bank[q][:, j * TT:(j + 1) * TT], arow[q][:, j, k * P:(k + 1) * P], ident[0:TT, 0:TT])
                        last.then_inc(full[q], 1)
                for q in TWO:
                    pe.wait_ge(xn_in[q], START + 16 * (i + 1))
                    dense(q, Q_, [(w2["Wq"], 0), (w2["Wq"], 1)], xh(xn, q), 2)
                for q in TWO:
                    pe.wait_ge(elu_ok[q], START + i + 1)
                    mean_of(q, LN_LOCAL, hl)
                var_of(LN_LOCAL)
                for q in TWO:
                    pe.wait_ge(y_in[q], 64 * (i + 1))
                    for k in range(H2):
                        pe.wait_ge(lin_read[q][k], START + BANK_USES * i + Y_ROWS // 2 + 1)
                        for j in range(TILES):
                            last = nc.tensor.transpose(lin_ps[q][k][:, j * TT:(j + 1) * TT], yrow[q][:, j, k * P:(k + 1) * P], ident[0:TT, 0:TT])
                        last.then_inc(lin_full[q][k], 1)
                for q in TWO:
                    for k in range(H2):
                        written(q, Y_ROWS + k)
                    mean_of(q, LN_GLOBAL, ha)
                for q in TWO:
                    for k in range(H2):
                        lin(q, DEN + k, [(ks_blk[:, k, :], qp[q][:, k, :])])
                for q in TWO:
                    for k in range(H2):
                        lin(q, NUM + k, [(kv_blk[:, k, :], qp[q][:, k, :])])
                var_of(LN_GLOBAL)
                for q in TWO:
                    pe.wait_ge(gain_ok[q], START + 5 * i + 2)
                    dense(q, GATE, [(w2["wlT"], 0), (w2["wlT"], 1), (w2["wgT"], 0), (w2["wgT"], 1)], xh(hl, q) + xh(ha, q), 2)
                for q in TWO:
                    for k in range(H2):
                        written(q, NUM + k)
                    dense(q, WM, [(w2["Wm"], 0), (w2["Wm"], 1)], xh(msg, q), 2)
                for q in TWO:
                    pe.wait_ge(h_ok[q], START + i + 1)
                    dense(q, FF1, [(w_ff1, 0), (w_ff1, 1)], xh(h, q), 4)
                for q in TWO:
                    written(q, WM)
                    written(q, WM + 1)
                    mean_of(q, LN_MSG, qp)
                for q in TWO:
                    for u in (FF1 + 2, FF1 + 3):
                        written(q, u)
                    dense(q, FF2, [(w_ff2, k) for k in range(4)], xh(wide, q), 2)
                var_of(LN_MSG)
                for q in TWO:
                    for u in (FF2, FF2 + 1):
                        written(q, u)
                    mean_of(q, LN_GNN, res)
                for q in TWO:
                    pe.wait_ge(gain_ok[q], START + 5 * i + 3)
                    dense(q, M1, [(w_m1, k) for k in range(4)], xh(xn, q) + xh(msg, q), 4)
                var_of(LN_GNN)
                for q in TWO:
                    for u in (M1 + 2, M1 + 3):
                        written(q, u)
                    dense(q, M2, [(w_m2, k) for k in range(4)], xh(wide, q), 2)
                for q in TWO:
                    for u in (M2, M2 + 1):
                        written(q, u)
                    mean_of(q, LN_MIX, mix)
                var_of(LN_MIX)
                for q in TWO:
                    pe.wait_ge(x2_ok[q], START + i + 1)
                    mean_of(q, LN_ROUTER, x)
                var_of(LN_ROUTER)
                for q in TWO:
                    pe.wait_ge(norm_ok[q], START + LNS * i + LN_ROUTER + 1)
                    mean_of(q, LN_EXPERT, ha)
                var_of(LN_EXPERT)
                for q in TWO:
                    pe.wait_ge(mean_read[q], START + MEAN_USES * i + 1 + LNS)
                    for j in range(TILES):
                        for k in range(H2):
                            last = nc.tensor.matmul(mean_ps[q][0:TT, j * EXPERTS:(j + 1) * EXPERTS], ha[q][:, k, j * TT:(j + 1) * TT],
                                                    w_r[:, k, :], start=(k == 0), stop=(k == 1))
                    last.then_inc(mean_full[q], 1)
                for q in TWO:
                    pe.wait_ge(norm_ok[q], START + LNS * i + LNS)
                    for j in range(TILES):
                        for n, src in enumerate((x, hl)):
                            pe.wait_ge(lin_read[q][n], START + BANK_USES * i + 1 + LIN_USES // 2 + j)
                            for k in range(H2):
                                last = nc.tensor.transpose(lin_ps[q][n][0:TT, k * P:(k + 1) * P], src[q][:, k, j * TT:(j + 1) * TT], ident[:])
                            last.then_inc(lin_full[q][n], 1)

        def full(eng, q, u, i):
            eng.wait_ge(lin_full[q][u % 2], START + BANK_USES * i + u // 2 + 2)

        @block.scalar
        def _(act):
            act.wait_ge(consts, START + 3)
            act.wait_ge(w_ok, START + 256)
            with act.Fori(0, pairs) as i:
                TWO = range(2)

                def square(n):
                    for q in TWO:
                        act.wait_ge(mean_read[q], START + MEAN_USES * i + n + 2)
                        act.wait_ge(var_full[q], START + VAR_USES * i + 1 + n)
                        nc.scalar.activation(sq[q][:], cent[q][:], ACT.Square).then_inc(sq_ok[q], 1)

                def root(n):
                    for q in TWO:
                        act.wait_ge(var_full[q], START + VAR_USES * i + n + 2)
                        act.wait_ge(norm_ok[q], START + LNS * i + n)
                        nc.scalar.activation(std[q][:], var_ps[q][:, 0:CH], ACT.Ln, bias=eps[:]).then_inc(log_ok[q], 1)
                    for q in TWO:
                        act.wait_ge(log_ok[q], START + LNS * i + n + 1)
                        nc.scalar.activation(std[q][:], std[q][:], ACT.Exp, scale=-0.5).then_inc(var_read[q], 1)

                def affine(n, buf, gained):
                    for q in TWO:
                        act.wait_ge(norm_ok[q], START + LNS * i + n + 1)
                        for k in range(H2):
                            last = nc.scalar.activation(buf[q][:, k, :], buf[q][:, k, :], ACT.Identity,
                                                        scale=v(2 + 2 * gained, k), bias=v(3 + 2 * gained, k))
                        last.then_inc(gain_ok[q], 1)

                def drain(u, outs, dst, func, bias=None):
                    for q in TWO:
                        for m in range(outs):
                            full(act, q, u + m, i)
                            kw = {} if bias is None else {"bias": bias[:, m:m + 1]}
                            nc.scalar.activation(dst[q][:, m, :], lin_ps[q][(u + m) % 2][:, 0:CH], func, **kw).then_inc(
                                lin_read[q][(u + m) % 2], 1)

                for q in TWO:
                    act.wait_ge(low_ok[q], START + i + 1)
                    nc.scalar.activation(low[q][:], low[q][:], ACT.Exp).then_inc(exp_ok[q], 1)
                for q in TWO:
                    act.wait_ge(qlow_ok[q], START + 2 * i + 2)
                    nc.scalar.activation(msg[q][:], msg[q][:], ACT.Exp).then_inc(qexp_ok[q], 1)
                square(LN_LOCAL)
                root(LN_LOCAL)
                affine(LN_LOCAL, hl, 0)
                square(LN_GLOBAL)
                for q in TWO:
                    for k in range(H2):
                        full(act, q, DEN + k, i)
                        nc.scalar.activation(den[q][:, k, :], lin_ps[q][k][:, 0:CH], ACT.Ln, bias=att_eps[:]).then_inc(lin_read[q][k], 1)
                for q in TWO:
                    for k in range(H2):
                        act.wait_ge(lin_read[q][k], START + BANK_USES * i + DEN // 2 + 2)
                    nc.scalar.activation(den[q][:], den[q][:], ACT.Exp, scale=-1.0).then_inc(den_ok[q], 1)
                root(LN_GLOBAL)
                affine(LN_GLOBAL, ha, 1)
                drain(GATE, 2, gate, ACT.Sigmoid)
                drain(WM, 2, qp, ACT.Copy)
                drain(FF1, 4, wide, ACT.Relu, b_ff1)
                square(LN_MSG)
                root(LN_MSG)
                affine(LN_MSG, msg, 2)
                square(LN_GNN)
                for q in TWO:
                    full(act, q, FF2 + 1, i)
                drain(M1, 4, wide, ACT.Relu)
                root(LN_GNN)
                affine(LN_GNN, res, 3)
                drain(M2, 2, mix, ACT.Copy)
                square(LN_MIX)
                root(LN_MIX)
                affine(LN_MIX, mix, 4)
                square(LN_ROUTER)
                root(LN_ROUTER)
                square(LN_EXPERT)
                root(LN_EXPERT)
                for q in TWO:
                    for j in range(TILES):
                        act.wait_ge(lin_full[q][1], START + BANK_USES * i + 1 + LIN_USES // 2 + j + 1)
                        act.wait_ge(stored[q], START + 48 * i)
                        nc.scalar.activation(xerow[q][:, j, :], lin_ps[q][1][0:TT, 0:D], ACT.Copy).then_inc(lin_read[q][1], 1)

        @block.vector
        def _(dve):
            dve.wait_ge(w_ok, START + 256)
            for k in range(H2):
                nc.vector.tensor_tensor(kv_blk[:, k, :], kv[:, k, 0:P], same[:], ALU.mult).then_inc(blk_ok, 1)
                nc.vector.tensor_scalar(ks_blk[:, k, :], same[:], kv[:, k, P:KROW], None, ALU.mult).then_inc(blk_ok, 1)
            with dve.Fori(0, pairs) as i:
                TWO = range(2)

                def centre(n, src):
                    for q in TWO:
                        dve.wait_ge(mean_full[q], START + MEAN_USES * i + n + 2)
                        dve.wait_ge(norm_ok[q], START + LNS * i + n)
                        nc.vector.tensor_tensor(cent[q][:], src[q][:], over_halves(mean_ps[q][:, 0:CH]), ALU.subtract).then_inc(mean_read[q], 1)

                def norm(n, dst):
                    for q in TWO:
                        dve.wait_ge(var_read[q], START + VAR_USES * i + n + 2)
                        nc.vector.tensor_tensor(dst[q][:], cent[q][:], over_halves(std[q][:]), ALU.mult).then_inc(norm_ok[q], 1)

                for q in TWO:
                    nc.vector.tensor_copy(y_at[q][:], rank[:, bass.ds((i * 2 + q) * TILES, TILES)]).then_inc(y_at_ok[q], 1)
                for q in TWO:
                    dve.wait_ge(xn_in[q], START + 16 * (i + 1))
                    for k, (bank, ready, uses, read) in enumerate(((mean_ps, mean_full, MEAN_USES, mean_read),
                                                                   (var_ps, var_full, VAR_USES, var_read))):
                        dve.wait_ge(ready[q], START + uses * i + 1)
                        nc.vector.scalar_tensor_tensor(up[q][:, k, :], bank[q][:, 0:CH], v(0, k), xn[q][:, k, :],
                                                       ALU.add, ALU.add).then_inc(read[q], 1)
                for q in TWO:
                    dve.wait_ge(mean_read[q], START + MEAN_USES * i + 1)
                    dve.wait_ge(var_read[q], START + VAR_USES * i + 1)
                    nc.vector.tensor_scalar(low[q][:], up[q][:], 0.0, None, ALU.min).then_inc(low_ok[q], 1)
                    dve.wait_ge(low_ok[q], START + i + 1)
                    nc.vector.tensor_scalar(up[q][:], up[q][:], 0.0, -1.0, ALU.max, ALU.add).then_inc(up_ok[q], 1)
                for q in TWO:
                    for k in range(H2):
                        full(dve, q, Q_ + k, i)
                        nc.vector.tensor_scalar(msg[q][:, k, :], lin_ps[q][k][:, 0:CH], 0.0, None, ALU.min).then_inc(qlow_ok[q], 1)
                for q in TWO:
                    dve.wait_ge(up_ok[q], START + i + 1)
                    dve.wait_ge(exp_ok[q], START + i + 1)
                    nc.vector.tensor_tensor(hl[q][:], up[q][:], low[q][:], ALU.add).then_inc(elu_ok[q], 1)
                for q in TWO:
                    dve.wait_ge(qexp_ok[q], START + i + 1)
                    for k in range(H2):
                        nc.vector.scalar_tensor_tensor(qp[q][:, k, :], lin_ps[q][k][:, 0:CH], 0.0, msg[q][:, k, :],
                                                       ALU.max, ALU.add).then_inc(lin_read[q][k], 1)
                centre(LN_LOCAL, hl)
                for q in TWO:
                    for k in range(H2):
                        full(dve, q, Y_ROWS + k, i)
                        nc.vector.tensor_tensor(ha[q][:, k, :], lin_ps[q][k][:, 0:CH], xn[q][:, k, :], ALU.add).then_inc(lin_read[q][k], 1)
                norm(LN_LOCAL, hl)
                centre(LN_GLOBAL, ha)
                for q in TWO:
                    for k in range(H2):
                        dve.wait_ge(den_ok[q], START + i + 1)
                        full(dve, q, NUM + k, i)
                        nc.vector.tensor_tensor(msg[q][:, k, :], lin_ps[q][k][:, 0:CH], den[q][:, k, :], ALU.mult).then_inc(lin_read[q][k], 1)
                norm(LN_GLOBAL, ha)
                for q in TWO:
                    dve.wait_ge(gain_ok[q], START + 5 * i + 2)
                    nc.vector.tensor_tensor(low[q][:], hl[q][:], ha[q][:], ALU.subtract).then_inc(diff_ok[q], 1)
                    for k in range(H2):
                        dve.wait_ge(lin_read[q][k], START + BANK_USES * i + GATE // 2 + 2)
                    dve.wait_ge(diff_ok[q], START + i + 1)
                    nc.vector.tensor_tensor(gate[q][:], gate[q][:], low[q][:], ALU.mult).then_inc(gated_ok[q], 1)
                    dve.wait_ge(gated_ok[q], START + i + 1)
                    nc.vector.tensor_tensor(h[q][:], gate[q][:], ha[q][:], ALU.add).then_inc(h_ok[q], 1)
                centre(LN_MSG, qp)
                for q in TWO:
                    for k in range(H2):
                        full(dve, q, FF2 + k, i)
                        nc.vector.scalar_tensor_tensor(res[q][:, k, :], lin_ps[q][k][:, 0:CH], v(1, k), h[q][:, k, :],
                                                       ALU.add, ALU.add).then_inc(lin_read[q][k], 1)
                norm(LN_MSG, msg)
                centre(LN_GNN, res)
                norm(LN_GNN, res)
                for q in TWO:
                    dve.wait_ge(x_in[q], START + 16 * (i + 1))
                    nc.vector.tensor_tensor(x[q][:], x[q][:], xn[q][:], ALU.add).then_inc(sum1_ok[q], 1)
                    dve.wait_ge(gain_ok[q], START + 5 * i + 4)
                    dve.wait_ge(sum1_ok[q], START + i + 1)
                    nc.vector.tensor_tensor(x[q][:], x[q][:], res[q][:], ALU.add).then_inc(sum2_ok[q], 1)
                centre(LN_MIX, mix)
                norm(LN_MIX, mix)
                for q in TWO:
                    dve.wait_ge(gain_ok[q], START + 5 * i + 5)
                    dve.wait_ge(sum2_ok[q], START + i + 1)
                    nc.vector.tensor_tensor(x[q][:], x[q][:], mix[q][:], ALU.add).then_inc(x2_ok[q], 1)
                centre(LN_ROUTER, x)
                norm(LN_ROUTER, ha)
                centre(LN_EXPERT, ha)
                norm(LN_EXPERT, hl)
                for q in TWO:
                    dve.wait_ge(mean_full[q], START + MEAN_USES * (i + 1))
                    dve.wait_ge(stored[q], START + 48 * i)
                    nc.vector.tensor_tensor(logit[q][:], mean_ps[q][0:TT, 0:TILES * EXPERTS].rearrange("p (j e) -> p j e", j=TILES),
                                            b_r[:].unsqueeze(1).to_broadcast([TT, TILES, EXPERTS]), ALU.add).then_inc(mean_read[q], 1)
                for q in TWO:
                    for j in range(TILES):
                        dve.wait_ge(lin_full[q][0], START + BANK_USES * i + 1 + LIN_USES // 2 + j + 1)
                        nc.vector.tensor_copy(x2row[q][:, j, :], lin_ps[q][0][0:TT, 0:D]).then_inc(lin_read[q][0], 1)


TOP = 2
XSLOTS = -(-((N * TOP + EXPERTS * (P - 1)) // P) // 2) * 2
FAR = 1e6


def stage_route(nc, a, t):
    with ExitStack() as ctx:
        shape = [TT, NTT, EXPERTS]
        logit, rest, mark, hot1, hot2, both, inner, upto, pos = (
            sb(nc, ctx, f"o_{n}", shape) for n in "logit rest mark hot1 hot2 both inner upto pos".split())
        valid, first, second, m1, m2, diff, w1, w2, invalid, p1, p2 = (
            sb(nc, ctx, f"o_{n}", [TT, NTT]) for n in "valid first second m1 m2 diff w1 w2 invalid p1 p2".split())
        below = sb(nc, ctx, "o_below", [P, P])
        ones = sb(nc, ctx, "o_ones", [TT, NTT * EXPERTS])
        order = sb(nc, ctx, "o_order", [TT, EXPERTS])
        tiles_i = sb(nc, ctx, "o_tiles_i", [TT, EXPERTS], I32)
        tiles, ends, base = (sb(nc, ctx, f"o_{n}", [TT, EXPERTS]) for n in ("tiles", "ends", "base"))
        slot = sb(nc, ctx, "o_slot", [1, XSLOTS])
        slot_e = sb(nc, ctx, "o_slot_e", [1, XSLOTS])
        slot_i = sb(nc, ctx, "o_slot_i", [1, XSLOTS], I32)
        send = [sb(nc, ctx, f"o_send{c}", [TT, NTT], I32) for c in range(TOP)]
        fetch = [sb(nc, ctx, f"o_fetch{c}", [TT, NTT], I32) for c in range(TOP)]
        to = [sb(nc, ctx, f"o_to{q}", [TT, TOP, TILES], I32) for q in range(2)]
        rows = [sb(nc, ctx, f"o_rows{q}", [TT, TILES, D]) for q in range(2)]
        inner_ps = ps(nc, ctx, "o_inner_ps", [P, 512])
        total_ps = ps(nc, ctx, "o_total_ps", [P, 512])
        token = sb(nc, ctx, "o_token", [P, 2])
        weights_in, settled, loaded, consts, token_ok, step_ok, counted, exp_ok, saved = sems(
            nc, ctx, "o", "weights_in settled loaded consts token_ok step_ok counted exp_ok saved")
        rows_in, to_ok, sent = (sems(nc, ctx, "o", f"{n}0 {n}1") for n in "rows_in to_ok sent".split())
        pairs = NCH // 2
        XSTEPS = 14
        block = ctx.enter_context(nc.Block())

        def each(ap):
            return ap.unsqueeze(2).to_broadcast(shape)

        @block.sync
        def _(sp):
            for dst, source in ((logit[:], t["logit"].rearrange("(i p) e -> p i e", p=TT)), (valid[:], a["valid"]), (below[:], a["below"])):
                sp.dma_start(dst, source).then_inc(loaded, 16)
            for q in range(2):
                sp.dma_start(rows[q][:], t["xe"][q * CH:(q + 1) * CH, :].rearrange("(j p) f -> p j f", p=TT)).then_inc(rows_in[q], 16)
            with sp.Fori(1, pairs) as i:
                for q in range(2):
                    sp.wait_ge(sent[q], 16 * TOP * TILES * i)
                    sp.dma_start(rows[q][:], t["xe"][bass.ds((i * 2 + q) * CH, CH), :].rearrange("(j p) f -> p j f", p=TT)).then_inc(rows_in[q], 16)
            sp.wait_ge(counted, START + 2)
            for dst, source in ((t["fetch0"], fetch[0]), (t["fetch1"], fetch[1]), (t["w1"], w1), (t["w2"], w2), (t["slot_e"], slot_i)):
                sp.dma_start(dst, source[:]).then_inc(saved, 16)
            sp.wait_ge(saved, START + 80)
            for q in range(2):
                sp.wait_ge(sent[q], 16 * TOP * TILES * pairs)

        @block.gpsimd
        def _(pool):
            nc.gpsimd.iota(order[:], [[-1, EXPERTS]], base=EXPERTS, channel_multiplier=0, allow_small_or_imprecise_dtypes=True).then_inc(consts, 1)
            nc.gpsimd.iota(slot[:], [[1, XSLOTS]], base=0, channel_multiplier=0, allow_small_or_imprecise_dtypes=True).then_inc(consts, 1)
            nc.gpsimd.memset(ones[:], 1.0).then_inc(consts, 1)
            nc.gpsimd.memset(token[:], 0.0).then_inc(token_ok, 1)
            pool.wait_ge(token_ok, START + 1)
            with pool.Fori(0, pairs) as i:
                for q in range(2):
                    pool.wait_ge(rows_in[q], START + 16 * (i + 1))
                    pool.wait_ge(to_ok[q], START + TOP * (i + 1))
                    settle(nc, pool, token, settled, 2 * i + q)
                    for c in range(TOP):
                        for j in range(TILES):
                            nc.gpsimd.indirect_dma_start(
                                out=t["xd"], out_offset=bass.IndirectOffsetOnAxis(ap=to[q][:, c, j:j + 1], axis=0),
                                in_=rows[q][:, j, :], in_offset=None, bounds_check=XSLOTS * P - 1, oob_is_err=False).then_inc(sent[q], 16)

        @block.tensor
        def _(pe):
            pe.wait_ge(loaded, START + 48)
            pe.wait_ge(counted, START + 1)
            flat = both[:].rearrange("p i e -> p (i e)")
            nc.tensor.matmul(inner_ps[0:TT, 0:NTT * EXPERTS], below[0:TT, 0:TT], flat, start=True, stop=True)
            nc.tensor.matmul(total_ps[0:TT, 0:NTT * EXPERTS], ones[:, 0:TT], flat, start=True, stop=True).then_inc(exp_ok, 1)

        @block.scalar
        def _(act):
            act.wait_ge(loaded, START + 48)
            for e in range(EXPERTS):
                act.dma_start(t["expert_w1"][:, e, :].rearrange("p (k n) -> p k n", k=H2), a["ffn_W1"][e].rearrange("(k p) n -> p k n", p=P)).then_inc(weights_in, 16)
                act.dma_start(t["expert_w2"][:, e, :].rearrange("p (k n) -> p k n", k=HC), a["ffn_W2"][e].rearrange("(k p) n -> p k n", p=P)).then_inc(weights_in, 16)
                act.dma_start(t["expert_b1"][:, e, :], a["ffn_b1"][e].unsqueeze(0).to_broadcast([P, HID])).then_inc(weights_in, 16)
            act.wait_ge(step_ok, START + XSTEPS)
            nc.scalar.activation(w2[:], diff[:], ACT.Exp).then_inc(exp_ok, 1)
            act.wait_ge(weights_in, START + 48 * EXPERTS)

        @block.vector
        def _(dve):
            n = [0]

            def go(ins):
                n[0] += 1
                ins.then_inc(step_ok, 1)
                dve.wait_ge(step_ok, START + n[0])

            V = nc.vector
            dve.wait_ge(loaded, START + 48)
            dve.wait_ge(consts, START + 3)
            rank_of = order[:].unsqueeze(1).to_broadcast(shape)
            for l, m, f, hot in ((logit, m1, first, hot1), (rest, m2, second, hot2)):
                go(V.tensor_reduce(m[:], l[:], AX.X, ALU.max))
                go(V.tensor_tensor(mark[:], l[:], each(m[:]), ALU.is_equal))
                go(V.tensor_tensor(mark[:], mark[:], rank_of, ALU.mult))
                go(V.tensor_reduce(f[:], mark[:], AX.X, ALU.max))
                go(V.tensor_tensor(hot[:], each(f[:]), rank_of, ALU.is_equal))
                if hot is hot1:
                    go(V.scalar_tensor_tensor(rest[:].rearrange("p i e -> p (i e)"), hot1[:].rearrange("p i e -> p (i e)"), -BIG,
                                              logit[:].rearrange("p i e -> p (i e)"), ALU.mult, ALU.add))
            go(V.tensor_tensor(both[:], hot1[:], hot2[:], ALU.add))
            both_done = V.tensor_tensor(both[:], both[:], each(valid[:]), ALU.mult)
            both_done.then_inc(counted, 1)
            go(V.tensor_tensor(diff[:], m2[:], m1[:], ALU.subtract))
            go(V.tensor_scalar(invalid[:], valid[:], -FAR, FAR, ALU.mult, ALU.add))
            dve.wait_ge(exp_ok, START + 2)
            go(V.tensor_scalar(diff[:], w2[:], 1.0, None, ALU.add))
            go(V.reciprocal(w1[:], diff[:]))
            go(V.tensor_tensor(w2[:], w2[:], w1[:], ALU.mult))
            flat = "p i e -> p (i e)"
            go(V.tensor_copy(inner[:].rearrange(flat), inner_ps[0:TT, 0:NTT * EXPERTS]))
            go(V.tensor_copy(mark[:].rearrange(flat), total_ps[0:TT, 0:NTT * EXPERTS]))
            for e in range(EXPERTS):
                go(V.tensor_tensor_scan(upto[:, :, e], ones[:, 0:NTT], mark[:, :, e], 0.0, ALU.mult, ALU.add))
            go(V.tensor_scalar(tiles_i[:], upto[:, NTT - 1, :], float(P - 1), None, ALU.add))
            go(V.tensor_single_scalar(tiles_i[:], tiles_i[:], 7, op=ALU.logical_shift_right))
            go(V.tensor_copy(tiles[:], tiles_i[:]))
            go(V.tensor_tensor_scan(ends[:], ones[:, 0:EXPERTS], tiles[:], 0.0, ALU.mult, ALU.add))
            go(V.tensor_tensor(base[:], ends[:], tiles[:], ALU.subtract))
            go(V.tensor_scalar(base[:], base[:], float(P), None, ALU.mult))
            go(V.tensor_tensor(pos[:], upto[:], mark[:], ALU.subtract))
            go(V.tensor_tensor(pos[:], pos[:], inner[:], ALU.add))
            go(V.tensor_tensor(pos[:], pos[:], base[:].unsqueeze(1).to_broadcast(shape), ALU.add))
            for hot, pp, c in ((hot1, p1, 0), (hot2, p2, 1)):
                go(V.tensor_tensor(mark[:], hot[:], pos[:], ALU.mult))
                go(V.tensor_reduce(pp[:], mark[:], AX.X, ALU.add))
                go(V.tensor_tensor(send[c][:], pp[:], invalid[:], ALU.add))
                go(V.tensor_tensor(fetch[c][:], pp[:], valid[:], ALU.mult))
            go(V.tensor_scalar(slot_e[:], slot[:], ends[0:1, 0:1], None, ALU.is_ge))
            for e in range(1, EXPERTS):
                go(V.scalar_tensor_tensor(slot_e[:], slot[:], ends[0:1, e:e + 1], slot_e[:], ALU.is_ge, ALU.add))
            V.tensor_scalar(slot_i[:], slot_e[:], float(EXPERTS - 1), None, ALU.min).then_inc(counted, 1)
            for q in range(2):
                for c in range(TOP):
                    nc.vector.tensor_copy(to[q][:, c, :], send[c][:, q * TILES:(q + 1) * TILES]).then_inc(to_ok[q], 1)
            with dve.Fori(1, pairs) as i:
                for q in range(2):
                    dve.wait_ge(sent[q], 16 * TOP * TILES * i)
                    for c in range(TOP):
                        nc.vector.tensor_copy(to[q][:, c, :], send[c][:, bass.ds((i * 2 + q) * TILES, TILES)]).then_inc(to_ok[q], 1)


HID = 1024
HC = HID // P


def stage_experts(nc, a, t):
    with ExitStack() as ctx:
        ident = sb(nc, ctx, "e_ident", [P, P])
        w1, w2, b1 = t["expert_w1"], t["expert_w2"], t["expert_b1"]
        b2 = sb(nc, ctx, "e_b2", [P, EXPERTS, D])
        ln = sb(nc, ctx, "e_ln", [P, EXPERTS, 2 * H2])
        slot_e = sb(nc, ctx, "e_slot_e", [1, XSLOTS], I32)
        rows = [sb(nc, ctx, f"e_rows{q}", [P, D]) for q in range(2)]
        xT = [sb(nc, ctx, f"e_xT{q}", [P, H2, P]) for q in range(2)]
        h = [sb(nc, ctx, f"e_h{q}", [P, HID]) for q in range(2)]
        hT = [sb(nc, ctx, f"e_hT{q}", [P, HC, P]) for q in range(2)]
        y = [sb(nc, ctx, f"e_y{q}", [P, D]) for q in range(2)]
        x_ps = ps(nc, ctx, "e_x_ps", [P, 512])
        h_ps = ps(nc, ctx, "e_h_ps", [P, 4, 512])
        hT_ps = ps(nc, ctx, "e_hT_ps", [P, 2, 512])
        y_ps = ps(nc, ctx, "e_y_ps", [P, 512])
        w_ok, x_mm, x_ok, hT_mm, hT_ok, y_mm, y_ok = sems(nc, ctx, "e", "w_ok x_mm x_ok hT_mm hT_ok y_mm y_ok")
        rows_in, h_mm, biased, gelu_ok, stored = (sems(nc, ctx, "e", f"{n}0 {n}1") for n in "rows_in h_mm biased gelu_ok stored".split())
        LOADS = 3 + EXPERTS
        block = ctx.enter_context(nc.Block())

        def steps(eng, runs):
            def step(i, j):
                for run, ahead in runs:
                    if not isinstance(i, int) or 0 <= 2 * i + j + ahead < XSLOTS:
                        run(i, j + ahead)

            for s in range(-2, 2):
                step(s // 2, s % 2)
            with eng.Fori(1, XSLOTS // 2 - 1) as i:
                for j in range(2):
                    step(i, j)
            for s in range(XSLOTS - 2, XSLOTS + 2):
                step(s // 2, s % 2)

        def begun(i, j):
            return not isinstance(i, int) or 2 * i + j >= 0

        def expert(eng, i, j):
            return bass.ds(eng.value_load(slot_e[0:1, bass.ds(i * 2 + j, 1)], min_val=0, max_val=EXPERTS - 1), 1)

        @block.sync
        def _(sp):
            for dst, source in ((slot_e[:], t["slot_e"]), (ident[:], a["ident"]), (ln[:], a["ffn_ln"])):
                sp.dma_start(dst, source).then_inc(w_ok, 16)
            for e in range(EXPERTS):
                sp.dma_start(b2[:, e, :], a["ffn_b2"][e].unsqueeze(0).to_broadcast([P, D])).then_inc(w_ok, 16)

            def load(i, j):
                if begun(i, j - 2):
                    sp.wait_ge(x_mm, START + 2 * i + j - 1)
                sp.dma_start(rows[j % 2][:], t["xd"][bass.ds((i * 2 + j) * P, P), :]).then_inc(rows_in[j % 2], 16)

            def store(i, j):
                sp.wait_ge(y_ok, START + 2 * i + j + 1)
                sp.dma_start(t["yd"][bass.ds((i * 2 + j) * P, P), :], y[j % 2][:]).then_inc(stored[j % 2], 16)

            steps(sp, ((load, 2), (store, -2)))
            for q in range(2):
                sp.wait_ge(stored[q], START + 16 * (XSLOTS // 2))

        @block.tensor
        def _(pe):
            def turn_rows(i, j):
                q = j % 2
                pe.wait_ge(rows_in[q], START + 16 * (i + j // 2 + 1))
                pe.wait_ge(x_ok, START + 2 * (2 * i + j))
                for k in range(H2):
                    last = nc.tensor.transpose(x_ps[:, k * P:(k + 1) * P], rows[q][:, k * P:(k + 1) * P], ident[:])
                last.then_inc(x_mm, 1)

            def hidden(n):
                def run(i, j):
                    q, u = j % 2, i + j // 2
                    e = expert(pe, i, j)
                    pe.wait_ge(x_ok, START + 2 * (2 * i + j) + 2)
                    if begun(i, j - 2):
                        pe.wait_ge(biased[q], START + 2 * u + n - 1)
                    for k in range(H2):
                        last = nc.tensor.matmul(h_ps[:, 2 * q + n, :], xT[q][:, k, :],
                                                w1[:, e, k * HID + n * 512:k * HID + (n + 1) * 512].rearrange("p e n -> p (e n)"),
                                                start=(k == 0), stop=(k == H2 - 1))
                    last.then_inc(h_mm[q], 1)
                return run

            def turn_hidden(n):
                def run(i, j):
                    q, u = j % 2, i + j // 2
                    pe.wait_ge(gelu_ok[q], START + 2 * u + n + 1)
                    if begun(i, j - 1):
                        pe.wait_ge(hT_ok, START + 2 * (2 * i + j) + n - 1)
                    for c in range(4):
                        cc = n * 4 + c
                        last = nc.tensor.transpose(hT_ps[:, n, c * P:(c + 1) * P], h[q][:, cc * P:(cc + 1) * P], ident[:])
                    last.then_inc(hT_mm, 1)
                return run

            def output(i, j):
                e = expert(pe, i, j)
                pe.wait_ge(hT_ok, START + 2 * (2 * i + j) + 2)
                pe.wait_ge(y_ok, START + 2 * i + j)
                for c in range(HC):
                    last = nc.tensor.matmul(y_ps[:, 0:D], hT[j % 2][:, c, :], w2[:, e, c * D:(c + 1) * D].rearrange("p e n -> p (e n)"),
                                            start=(c == 0), stop=(c == HC - 1))
                last.then_inc(y_mm, 1)

            pe.wait_ge(w_ok, START + 16 * LOADS)
            steps(pe, ((turn_rows, 1), (hidden(0), 0), (turn_hidden(0), -1), (hidden(1), 0), (turn_hidden(1), -1), (output, -2)))

        @block.scalar
        def _(act):
            def gelu(n):
                def run(i, j):
                    q = j % 2
                    act.wait_ge(biased[q], START + 2 * (i + j // 2) + n + 1)
                    half = h[q][:, n * 512:(n + 1) * 512]
                    nc.scalar.activation(half, half, ACT.Gelu).then_inc(gelu_ok[q], 1)
                return run

            def copy_turned(n):
                def run(i, j):
                    act.wait_ge(hT_mm, START + 2 * (2 * i + j) + n + 1)
                    if begun(i, j - 2):
                        act.wait_ge(y_mm, START + 2 * i + j - 1)
                    nc.scalar.activation(hT[j % 2][:, 4 * n:4 * n + 4, :].rearrange("p c n -> p (c n)"), hT_ps[:, n, :],
                                         ACT.Copy).then_inc(hT_ok, 1)
                return run

            act.wait_ge(w_ok, START + 16 * LOADS)
            steps(act, ((copy_turned(0), -1), (gelu(0), 0), (copy_turned(1), -1), (gelu(1), 0)))

        @block.vector
        def _(dve):
            def gain(i, j):
                q = j % 2
                e = expert(dve, i, j)
                dve.wait_ge(x_mm, START + 2 * i + j + 1)
                dve.wait_ge(h_mm[q], START + 2 * (i + j // 2))
                for k in range(H2):
                    nc.vector.tensor_scalar(xT[q][:, k, :], x_ps[:, k * P:(k + 1) * P],
                                            ln[:, e, k:k + 1].rearrange("p e n -> p (e n)"),
                                            ln[:, e, H2 + k:H2 + k + 1].rearrange("p e n -> p (e n)"),
                                            ALU.mult, ALU.add).then_inc(x_ok, 1)

            def bias(i, j):
                q, u = j % 2, i + j // 2
                e = expert(dve, i, j)
                for n in range(2):
                    dve.wait_ge(h_mm[q], START + 2 * u + n + 1)
                    if begun(i, j - 2):
                        dve.wait_ge(hT_mm, START + 2 * (2 * i + j) + n - 3)
                    nc.vector.tensor_tensor(h[q][:, n * 512:(n + 1) * 512], h_ps[:, 2 * q + n, :],
                                            b1[:, e, n * 512:(n + 1) * 512].rearrange("p e n -> p (e n)"),
                                            ALU.add).then_inc(biased[q], 1)

            def output(i, j):
                q = j % 2
                e = expert(dve, i, j)
                dve.wait_ge(y_mm, START + 2 * i + j + 1)
                dve.wait_ge(stored[q], START + 16 * (i + j // 2))
                nc.vector.tensor_tensor(y[q][:], y_ps[:, 0:D], b2[:, e, :].rearrange("p e n -> p (e n)"), ALU.add).then_inc(y_ok, 1)

            dve.wait_ge(w_ok, START + 16 * LOADS)
            steps(dve, ((gain, 1), (bias, 0), (output, -2)))


def stage_combine(nc, a, t):
    with ExitStack() as ctx:
        fetch = [sb(nc, ctx, f"c_fetch{c}", [TT, NTT], I32) for c in range(TOP)]
        w = [sb(nc, ctx, f"c_w{c}", [TT, NTT]) for c in range(TOP)]
        at = [sb(nc, ctx, f"c_at{q}", [TT, TOP, TILES], I32) for q in range(2)]
        got = [sb(nc, ctx, f"c_got{q}", [TT, TOP, TILES, D]) for q in range(2)]
        acc = [sb(nc, ctx, f"c_acc{q}", [TT, TILES, D]) for q in range(2)]
        token = sb(nc, ctx, "c_token", [P, 2])
        settled, loaded, token_ok = sems(nc, ctx, "c", "settled loaded token_ok")
        x_in, at_ok, got_in, half_ok, sum_ok, stored = (sems(nc, ctx, "c", f"{n}0 {n}1") for n in "x_in at_ok got_in half_ok sum_ok stored".split())
        pairs = NCH // 2
        block = ctx.enter_context(nc.Block())

        @block.sync
        def _(sp):
            for dst, source in ((fetch[0], "fetch0"), (fetch[1], "fetch1"), (w[0], "w1"), (w[1], "w2")):
                sp.dma_start(dst[:], t[source]).then_inc(loaded, 16)
            with sp.Fori(0, pairs) as i:
                for q in range(2):
                    sp.wait_ge(stored[q], START + 16 * i)
                    sp.dma_start(acc[q][:], t["x2"][bass.ds((i * 2 + q) * CH, CH), :].rearrange("(j p) f -> p j f", p=TT)).then_inc(x_in[q], 16)
                for q in range(2):
                    sp.wait_ge(sum_ok[q], START + TILES * (i + 1))
                    sp.dma_start(t["out"][bass.ds((i * 2 + q) * CH, CH), :].rearrange("(j p) f -> p j f", p=TT), acc[q][:]).then_inc(stored[q], 16)
            for q in range(2):
                sp.wait_ge(stored[q], START + 16 * pairs)

        @block.gpsimd
        def _(pool):
            nc.gpsimd.memset(token[:], 0.0).then_inc(token_ok, 1)
            pool.wait_ge(token_ok, START + 1)
            with pool.Fori(0, pairs) as i:
                for q in range(2):
                    pool.wait_ge(at_ok[q], START + TOP * (i + 1))
                    pool.wait_ge(sum_ok[q], START + TILES * i)
                    settle(nc, pool, token, settled, 2 * i + q)
                    for c in range(TOP):
                        for j in range(TILES):
                            nc.gpsimd.indirect_dma_start(
                                out=got[q][:, c, j, :], out_offset=None, in_=t["yd"],
                                in_offset=bass.IndirectOffsetOnAxis(ap=at[q][:, c, j:j + 1], axis=0)).then_inc(got_in[q], 16)

        @block.vector
        def _(dve):
            dve.wait_ge(loaded, START + 64)

            def where(i, q):
                for c in range(TOP):
                    nc.vector.tensor_copy(at[q][:, c, :], fetch[c][:, bass.ds((i * 2 + q) * TILES, TILES)]).then_inc(at_ok[q], 1)

            with dve.Fori(0, pairs) as i:
                for q in range(2):
                    dve.wait_ge(sum_ok[q], START + TILES * i)
                    where(i, q)
                for q in range(2):
                    dve.wait_ge(x_in[q], START + 16 * (i + 1))
                    dve.wait_ge(got_in[q], 16 * TOP * TILES * (i + 1))
                    for j in range(TILES):
                        nc.vector.scalar_tensor_tensor(acc[q][:, j, :], got[q][:, 0, j, :], w[0][:, bass.ds((i * 2 + q) * TILES + j, 1)],
                                                       acc[q][:, j, :], ALU.mult, ALU.add).then_inc(half_ok[q], 1)
                    for j in range(TILES):
                        dve.wait_ge(half_ok[q], START + TILES * i + j + 1)
                        nc.vector.scalar_tensor_tensor(acc[q][:, j, :], got[q][:, 1, j, :], w[1][:, bass.ds((i * 2 + q) * TILES + j, 1)],
                                                       acc[q][:, j, :], ALU.mult, ALU.add).then_inc(sum_ok[q], 1)


SCRATCH = {
    "xd": (XSLOTS * P, D), "yd": (XSLOTS * P, D), "fetch0": ((TT, NTT), I32), "fetch1": ((TT, NTT), I32),
    "w1": (TT, NTT), "w2": (TT, NTT), "slot_e": ((1, XSLOTS), I32),
    "logit": (NP, EXPERTS), "x2": (NP, D), "xe": (NP, D),
    "agg": (NP, D),
    "y": (NP, D),
    "v": (NP,), "rank": ((NP,), I32), "xs": (NP, D),
    "xnT": (D, NP), "xn": (NP, D), "table": (NP, ROW), "kv": (P, H2, KROW),
}


def build(nc, a, out):
    t = {n: nc.dram_tensor(f"t_{n}", list(s if not isinstance(s[0], tuple) else s[0]),
                           F32 if not isinstance(s[0], tuple) else s[1], kind="Internal").ap()
         for n, s in SCRATCH.items()}
    t["out"] = out
    stages = [stage_project, stage_rank, stage_mamba, stage_attend, stage_mix, stage_route,
              stage_experts, stage_combine]
    with ExitStack() as ctx:
        for stage in stages:
            if stage is stage_route:
                t["expert_w1"] = sb(nc, ctx, "expert_w1", [P, EXPERTS, H2 * HID])
                t["expert_w2"] = sb(nc, ctx, "expert_w2", [P, EXPERTS, HC * D])
                t["expert_b1"] = sb(nc, ctx, "expert_b1", [P, EXPERTS, HID])
            held = nc.snapshot_sems()
            stage(nc, a, t)
            nc.clear_and_free_semaphores(nc.allocated_since(held))
            nc.all_engine_barrier()


def kernel(**inputs):
    import numpy as np
    import concourse.bacc as bacc
    from concourse.bass_utils import run_bass_kernel_spmd

    g = {k[len("L0_gnn_"):]: np.asarray(v) for k, v in inputs.items() if k.startswith("L0_gnn_")}
    m = {k[len("L0_mix_"):]: np.asarray(v) for k, v in inputs.items() if k.startswith("L0_mix_")}
    f = {k[len("L0_ffn_"):]: np.asarray(v) for k, v in inputs.items() if k.startswith("L0_ffn_")}
    x = np.asarray(inputs["x"])
    feed = {}
    feed["xT"] = np.zeros((D, NP), np.float32)
    feed["xT"][:, :N] = x.T
    feed["gat_w"] = g["gat_w"]
    feed["gat_wT"] = g["gat_w"].T
    blk = np.zeros((D, 2 * HEADS), np.float32)
    for h in range(HEADS):
        blk[h * FO:(h + 1) * FO, h] = g["gat_a_src"][h]
        blk[h * FO:(h + 1) * FO, HEADS + h] = g["gat_a_tgt"][h]
    feed["a_blk"] = blk
    feed["Wk"], feed["Wv"] = m["Wk"], m["Wv"]
    feed["valid"] = (np.arange(NP) < N).astype(np.float32).reshape(NTT, TT).T
    feed["src"] = np.asarray(inputs["src"]).reshape(EP, EC)
    noise = np.full(NP, 3e38, np.float32)
    noise[:N] = np.asarray(inputs["node_vec"])
    feed["noise"] = noise.reshape(NT, P).T
    feed["in_projT"], feed["out_projT"] = g["in_proj_w"].T, g["out_proj_w"].T
    feed["x_projT"] = np.concatenate([g["x_proj_w"][STATES:]] * PARTS + [g["x_proj_w"][:STATES]]).T
    feed["dt_projT"] = np.zeros((DBC, D), np.float32)
    feed["dt_projT"][PARTS * BC:] = g["dt_proj_w"].T
    feed["pick"] = np.repeat(np.tile(np.eye(BC, dtype=np.float32), (PARTS, 1))[:, :, None], P, axis=2)
    feed["mamba_vecs"] = np.concatenate([g["conv_w"], g["conv_b"][:, None], g["dt_proj_b"][:, None], g["D_param"][:, None]], 1)
    feed["A_log"] = g["A_log"]
    feed["dst"] = np.asarray(inputs["dst"]).reshape(EP, EC)
    edges = np.zeros((E + P * PAIR, 2), np.int32)
    edges[:, 1] = 1 << 20
    edges[:E, 0], edges[:E, 1] = np.asarray(inputs["src"]), np.asarray(inputs["dst"])
    feed["edges"] = edges
    feed["below"] = np.triu(np.ones((P, P), np.float32), 1)
    feed["wlT"], feed["wgT"], feed["ff1T"], feed["ff2T"] = g["wl"].T, g["wg"].T, g["ff1_w"].T, g["ff2_w"].T
    for n in ("Wq", "Wm", "W1", "W2"):
        feed[n] = m[n]
    feed["ff1_b"], feed["Wr"], feed["br"] = g["ff1_b"].reshape(4, P).T, f["Wr"], f["br"]
    feed["mix_vecs"] = np.stack([g["gat_b"], g["ff2_b"], g["ln_local_g"], g["ln_local_b"], g["ln_global_g"], g["ln_global_b"],
                                 m["g1"], m["b1"], g["ln2_g"], g["ln2_b"], m["g2"], m["b2"]], 1)
    feed["same"] = np.kron(np.eye(4, dtype=np.float32), np.ones((32, 32), np.float32))
    feed["ffn_ln"] = np.concatenate([f["ln_g"].reshape(EXPERTS, H2, P), f["ln_b"].reshape(EXPERTS, H2, P)], 1).transpose(2, 0, 1)
    for n in ("W1", "W2", "b1", "b2"):
        feed["ffn_" + n] = f[n]
    feed["ident"] = np.eye(P, dtype=np.float32)

    nc = bacc.Bacc("TRN2", target_bir_lowering=False, num_devices=1)
    arrays, args = {}, {}
    for name, arr in feed.items():
        arr = np.ascontiguousarray(arr)
        arrays[f"in_{name}"] = arr
        args[name] = nc.dram_tensor(f"in_{name}", arr.shape, mybir.dt.from_np(arr.dtype), kind="ExternalInput").ap()
    out = nc.dram_tensor("out_rows", (NP, D), F32, kind="ExternalOutput").ap()
    build(nc, args, out)
    r = run_bass_kernel_spmd(nc, [arrays], core_ids=[0])
    return r.results[0]["out_rows"][:N]
```
